# Optimizing a Trainium2 kernel written in Bass

```python
import numpy as np
import jax
import jax.numpy as jnp

def _softmax(x, axis=-1):
    return jax.nn.softmax(x, axis=axis)

def _gelu(x):
    return jax.nn.gelu(x, approximate=True)

def _silu(x):
    return jax.nn.silu(x)

def _sigmoid(x):
    return jax.nn.sigmoid(x)

def _layernorm(x, axis=-1, eps=1e-05):
    m = jnp.mean(x, axis=axis, keepdims=True)
    v = jnp.var(x, axis=axis, keepdims=True)
    return (x - m) / jnp.sqrt(v + eps)

def _scatter_add(tgt, idx, src, axis=0):
    return tgt.at[idx].add(src)

def _segment_sum(src, seg, n):
    return jax.ops.segment_sum(src, seg, n)
kernel_name = 'mk_hybrid_d1_jaxref_r4_cd16bc'

def setup_inputs(seed: int=0):
    np.random.seed(seed)
    _w = jnp.asarray

    def _L0_attn_a_setup():
        import jax, jax.numpy as jnp
        import numpy as np
        NUM_HEADS = 16
        WINDOW = 64
        key = jax.random.key(seed)
        ks = jax.random.split(key, 6)
        b, l, d = (2, 512, 256)
        s = 1.0 / np.sqrt(d)
        return {'x': jax.random.normal(ks[0], (b, l, d), dtype=jnp.float32), 'Wq': jax.random.normal(ks[1], (d, d), dtype=jnp.float32) * s, 'Wk': jax.random.normal(ks[2], (d, d), dtype=jnp.float32) * s, 'Wv': jax.random.normal(ks[3], (d, d), dtype=jnp.float32) * s, 'Wo': jax.random.normal(ks[4], (d, d), dtype=jnp.float32) * s, 'bo': jax.random.normal(ks[5], (d,), dtype=jnp.float32) * 0.01}
    _L0_attn_a_in = _L0_attn_a_setup()

    def _L0_attn_b_setup():
        import jax, jax.numpy as jnp
        import numpy as np
        B, L, D, H = (4, 256, 256, 16)
        HD = D // H
        MAX_LEN = 256
        SCALE = HD ** 0.5

        def _rel_idx(seq_len):
            r = jnp.arange(seq_len)
            dist = r[None, :] - r[:, None]
            return jnp.clip(dist, -MAX_LEN, MAX_LEN) + MAX_LEN
        key = jax.random.key(seed)
        ks = jax.random.split(key, 7)
        sd = 1.0 / np.sqrt(D)
        x = jax.random.normal(ks[0], (B, L, D), dtype=jnp.float32)
        Wq = jax.random.normal(ks[1], (D, D), dtype=jnp.float32) * sd
        Wk = jax.random.normal(ks[2], (D, D), dtype=jnp.float32) * sd
        Wv = jax.random.normal(ks[3], (D, D), dtype=jnp.float32) * sd
        Wo = jax.random.normal(ks[4], (D, D), dtype=jnp.float32) * sd
        pek = jax.random.normal(ks[5], (2 * MAX_LEN + 1, HD), dtype=jnp.float32) / np.sqrt(HD)
        pev = jax.random.normal(ks[6], (2 * MAX_LEN + 1, HD), dtype=jnp.float32) / np.sqrt(HD)
        return {'x': x, 'Wq': Wq, 'Wk': Wk, 'Wv': Wv, 'Wo': Wo, 'pek': pek, 'pev': pev}
    _L0_attn_b_in = _L0_attn_b_setup()

    def _L0_ffn_setup():
        import jax, jax.numpy as jnp
        import numpy as np
        E = 8
        TOPK = 2
        PRIME = 11
        HASH_OFF = 7919
        N_SHARED = 1
        key = jax.random.key(seed)
        ks = jax.random.split(key, 8)
        B, T, C, Hs, Hr = (4, 2048, 256, 512, 256)
        sc = lambda k, shape, fan: jax.random.normal(k, shape, jnp.float32) * fan ** (-0.5)
        return {'x': jax.random.normal(ks[0], (B, T, C), jnp.float32), 't_emb': jax.random.normal(ks[1], (B, C), jnp.float32), 'sw1': sc(ks[2], (C, Hs), C), 'sb1': jnp.zeros((Hs,), jnp.float32), 'sw3': sc(ks[3], (C, Hs), C), 'sb3': jnp.zeros((Hs,), jnp.float32), 'sw2': sc(ks[4], (Hs, C), Hs), 'sb2': jnp.zeros((C,), jnp.float32), 'w1': sc(ks[5], (E, C, Hr), C), 'b1': jnp.zeros((E, Hr), jnp.float32), 'w2': sc(ks[6], (E, Hr, C), Hr), 'b2': jnp.zeros((E, C), jnp.float32)}
    _L0_ffn_in = _L0_ffn_setup()
    _d = {'L0_attn_a_x': _L0_attn_a_in['x'], 'L0_attn_a_Wq': _L0_attn_a_in['Wq'], 'L0_attn_a_Wk': _L0_attn_a_in['Wk'], 'L0_attn_a_Wv': _L0_attn_a_in['Wv'], 'L0_attn_a_Wo': _L0_attn_a_in['Wo'], 'L0_attn_a_bo': _L0_attn_a_in['bo'], 'L0_attn_b_Wq': _L0_attn_b_in['Wq'], 'L0_attn_b_Wk': _L0_attn_b_in['Wk'], 'L0_attn_b_Wv': _L0_attn_b_in['Wv'], 'L0_attn_b_Wo': _L0_attn_b_in['Wo'], 'L0_attn_b_pek': _L0_attn_b_in['pek'], 'L0_attn_b_pev': _L0_attn_b_in['pev'], 'L0_ffn_t_emb': _L0_ffn_in['t_emb'], 'L0_ffn_sw1': _L0_ffn_in['sw1'], 'L0_ffn_sb1': _L0_ffn_in['sb1'], 'L0_ffn_sw3': _L0_ffn_in['sw3'], 'L0_ffn_sb3': _L0_ffn_in['sb3'], 'L0_ffn_sw2': _L0_ffn_in['sw2'], 'L0_ffn_sb2': _L0_ffn_in['sb2'], 'L0_ffn_w1': _L0_ffn_in['w1'], 'L0_ffn_b1': _L0_ffn_in['b1'], 'L0_ffn_w2': _L0_ffn_in['w2'], 'L0_ffn_b2': _L0_ffn_in['b2']}
    _x0 = _d['L0_attn_a_x']
    _d['L0_attn_a_x'] = jax.random.normal(jax.random.fold_in(jax.random.key(seed), 1), (2, 2048, 256), dtype=_x0.dtype)
    del _x0
    return _d

def reference(L0_attn_a_x, L0_attn_a_Wq, L0_attn_a_Wk, L0_attn_a_Wv, L0_attn_a_Wo, L0_attn_a_bo, L0_attn_b_Wq, L0_attn_b_Wk, L0_attn_b_Wv, L0_attn_b_Wo, L0_attn_b_pek, L0_attn_b_pev, L0_ffn_t_emb, L0_ffn_sw1, L0_ffn_sb1, L0_ffn_sw3, L0_ffn_sb3, L0_ffn_sw2, L0_ffn_sb2, L0_ffn_w1, L0_ffn_b1, L0_ffn_w2, L0_ffn_b2):

    def _L0_attn_a_ref(x, Wq, Wk, Wv, Wo, bo):
        import jax, jax.numpy as jnp
        import numpy as np
        NUM_HEADS = 16
        WINDOW = 64
        b, l, d = x.shape
        h, w = (NUM_HEADS, WINDOW)
        dh = d // h
        p = w // 2
        q = (x @ Wq.T).reshape(b, l, h, dh)
        xp = jnp.pad(x, ((0, 0), (p, p), (0, 0)))
        k = (xp @ Wk.T).reshape(b, l + 2 * p, h, dh)
        v = (xp @ Wv.T).reshape(b, l + 2 * p, h, dh)
        win_idx = jnp.arange(l)[:, None] + jnp.arange(w)[None, :]
        kw = k[:, win_idx]
        vw = v[:, win_idx]
        scale = 1.0 / np.float32(np.sqrt(dh))
        scores = jnp.einsum('blhd,blwhd->blhw', q, kw) * scale
        attn = jax.nn.softmax(scores, axis=-1)
        out = jnp.einsum('blhw,blwhd->blhd', attn, vw).reshape(b, l, d)
        return out @ Wo.T + bo

    def _L0_attn_b_ref(x, Wq, Wk, Wv, Wo, pek, pev):
        import jax, jax.numpy as jnp
        import numpy as np
        B, L, D, H = (4, 256, 256, 16)
        HD = D // H
        MAX_LEN = 256
        SCALE = HD ** 0.5

        def _rel_idx(seq_len):
            r = jnp.arange(seq_len)
            dist = r[None, :] - r[:, None]
            return jnp.clip(dist, -MAX_LEN, MAX_LEN) + MAX_LEN
        b, s, _ = x.shape

        def proj(W):
            return (x @ W.T).reshape(b, s, H, HD).transpose(0, 2, 1, 3)
        Q, K, V = (proj(Wq), proj(Wk), proj(Wv))
        scores = jnp.einsum('bhqd,bhkd->bhqk', Q, K) / SCALE
        idx = _rel_idx(s)
        rel_k = pek[idx]
        scores = scores + jnp.einsum('bhqd,qkd->bhqk', Q, rel_k) / SCALE
        causal = jnp.tril(jnp.ones((s, s), dtype=bool))
        scores = jnp.where(causal[None, None], scores, -jnp.inf)
        attn = jax.nn.softmax(scores, axis=-1)
        out = jnp.einsum('bhqk,bhkd->bhqd', attn, V)
        rel_v = pev[idx]
        out = out + jnp.einsum('bhqk,qkd->bhqd', attn, rel_v)
        out = out.transpose(0, 2, 1, 3).reshape(b, s, D)
        return out @ Wo.T

    def _L0_ffn_ref(x, t_emb, sw1, sb1, sw3, sb3, sw2, sb2, w1, b1, w2, b2):
        import jax, jax.numpy as jnp
        import numpy as np
        E = 8
        TOPK = 2
        PRIME = 11
        HASH_OFF = 7919
        N_SHARED = 1
        B, T, C = x.shape
        N = B * T
        xf = x.reshape(N, C)
        shared = jax.nn.silu(xf @ sw1 + sb1) * (xf @ sw3 + sb3) @ sw2 + sb2
        tok = jnp.arange(N)
        out = jnp.zeros((N, C), x.dtype)
        for k in range(TOPK):
            exp_ids = (tok * PRIME + k * HASH_OFF) % E
            sort_idx = jnp.argsort(exp_ids)
            xs = xf[sort_idx].reshape(E, N // E, C)
            h = jax.nn.gelu(jnp.einsum('enc,ech->enh', xs, w1) + b1[:, None, :], approximate=False)
            y = jnp.einsum('enh,ehc->enc', h, w2) + b2[:, None, :]
            out = out.at[sort_idx].add(y.reshape(N, C))
        out = out / TOPK
        return ((shared + out) / (N_SHARED + 1)).reshape(B, T, C)
    x = L0_attn_a_x
    x = x + _L0_attn_a_ref(_layernorm(x, axis=-1), L0_attn_a_Wq, L0_attn_a_Wk, L0_attn_a_Wv, L0_attn_a_Wo, L0_attn_a_bo)
    x = x + _L0_ffn_ref(_layernorm(x, axis=-1), L0_ffn_t_emb, L0_ffn_sw1, L0_ffn_sb1, L0_ffn_sw3, L0_ffn_sb3, L0_ffn_sw2, L0_ffn_sb2, L0_ffn_w1, L0_ffn_b1, L0_ffn_w2, L0_ffn_b2)
    x = x + _L0_attn_b_ref(_layernorm(x, axis=-1), L0_attn_b_Wq, L0_attn_b_Wk, L0_attn_b_Wv, L0_attn_b_Wo, L0_attn_b_pek, L0_attn_b_pev)
    x = x + _L0_ffn_ref(_layernorm(x, axis=-1), L0_ffn_t_emb, L0_ffn_sw1, L0_ffn_sb1, L0_ffn_sw3, L0_ffn_sb3, L0_ffn_sw2, L0_ffn_sb2, L0_ffn_w1, L0_ffn_b1, L0_ffn_w2, L0_ffn_b2)
    return x

_drawn_inputs = setup_inputs


def setup_inputs(seed=0):
    import zlib

    import numpy as np

    out = dict(_drawn_inputs(seed))
    spreads = {'L0_ffn_sb1': (0.0, 0.1),
     'L0_ffn_sb3': (0.0, 0.1),
     'L0_ffn_sb2': (0.0, 0.1),
     'L0_ffn_b1': (0.0, 0.1),
     'L0_ffn_b2': (0.0, 0.1)}
    factors = {'L0_attn_a_bo': 4.156}
    for name, (base, spread) in spreads.items():
        noise = np.random.default_rng([zlib.crc32(name.encode()), seed]).standard_normal(out[name].shape)
        drawn = base * np.exp(spread * noise) if base else spread * noise
        out[name] = jnp.asarray(drawn.astype(out[name].dtype))
    for name, factor in factors.items():
        out[name] = (out[name] * factor).astype(out[name].dtype)
    return out
```

```python
from contextlib import ExitStack

import concourse.bass as bass
from concourse import mybir

ALU = mybir.AluOpType
ACT = mybir.ActivationFunctionType
AX = mybir.AxisListType
F32 = mybir.dt.float32
BF16 = mybir.dt.bfloat16

P = 128
B, L, D = 2, 2048, 256
NTOK = B * L
CK = D // P
H = 16
DH = D // H
WINDOW = 64
PAD = WINDOW // 2
GROUP = 512
TILES = GROUP // P
MAX_REL = 256
LN_EPS = 1e-5
SCORE_SCALE = float(DH) ** -0.5
MASKED = -1e30
LEFT = (0, 0, 0, 1, 1, 2)
RIGHT = (0, 1, 2, 0, 1, 0)
STACK = len(LEFT) * DH


class Stage:

    def __init__(self, nc, name):
        self.nc, self.name, self.ctx, self.semaphores = nc, name, ExitStack(), []

    def __enter__(self):
        self.ctx.__enter__()
        return self

    def __exit__(self, *e):
        self.ctx.__exit__(*e)
        self.nc.clear_and_free_semaphores(self.semaphores)
        self.nc.all_engine_barrier()

    def sb(self, name, shape, dt=F32):
        return self.ctx.enter_context(self.nc.sbuf_tensor(f"{self.name}_{name}", shape, dt))

    def ps(self, name, shape, dt=F32):
        return self.ctx.enter_context(self.nc.psum_tensor(f"{self.name}_{name}", shape, dt))

    def sem(self, name):
        self.semaphores.append(self.nc.alloc_semaphore(f"{self.name}_{name}"))
        return self.semaphores[-1]

    def sems(self, name, n):
        return [self.sem(f"{name}{i}") for i in range(n)]

    def block(self):
        return self.ctx.enter_context(self.nc.Block())


def for_turns(engine, turns, turn):
    turn(0)
    with engine.Fori(1, turns) as t:
        turn(t)


def make_identity(nc, pool, ident, zeroed, ready):
    nc.gpsimd.memset(ident[:, :], 0.0).then_inc(zeroed, 1)
    pool.wait_ge(zeroed, 1)
    nc.gpsimd.affine_select(out=ident[:, :], in_=ident[:, :], compare_op=ALU.not_equal, fill=1.0,
                            base=0, pattern=[[-1, P]], channel_multiplier=1).then_inc(ready, 1)


def project_stage(nc, name, x, wq_t, wk_t, wv_t, qk, v, pek0=None, pev0=None):
    rel = pek0 is not None
    off = 0 if rel else PAD
    turns = NTOK // GROUP // 2
    with Stage(nc, name) as s:
        ident, zeroed, ident_ready = s.sb("ident", [P, P]), s.sem("zeroed"), s.sem("ident_ready")
        w = s.sb("w", [P, 3, CK, D])
        w_loaded = s.sem("w_loaded")
        eps = s.sb("eps", [P, 1])
        kbias = s.sb("kbias", [P, 2])
        vbias = s.sb("vbias", [P, DH])
        const_set = s.sem("const_set")
        xg = s.sb("xg", [P, 2, TILES, D])
        stats = s.sb("stats", [P, 2, TILES, 6])
        mv = s.sb("mv", [P, 2, TILES, 2])
        spare = s.sb("spare", [P, 1])
        std = s.sb("std", [P, 2, TILES])
        rstd = s.sb("rstd", [P, 2, TILES])
        xn = s.sb("xn", [P, 2, TILES, D])
        xt = s.sb("xt", [P, 2, CK, GROUP])
        parts = s.sb("parts", [P, 2, 4, 3, GROUP], BF16)
        rest = s.sb("rest", [P, 4, GROUP])
        vout = s.sb("vout", [P, 2, H, TILES, DH]) if rel else s.sb("vout", [P, 2, TILES, D])
        ps_t = s.ps("ps_t", [P, CK, GROUP])
        ps_qk = s.ps("ps_qk", [P, 4, GROUP])
        ps_v = s.ps("ps_v", [P, TILES, D])

        x_loaded, stats_done, mv_done, std_done, rstd_done, normed = (
            s.sems(n, 2) for n in ("x_loaded", "stats_done", "mv_done", "std_done", "rstd_done", "normed"))
        turned, turned_out_a, turned_out_v = (s.sems(n, 2) for n in ("turned", "turned_out_a", "turned_out_v"))
        qk_done, high_done, rest_done, mid_done, low_done, parts_stored = (
            [s.sems(f"{n}{k}", 4) for k in range(2)]
            for n in ("qk_done", "high_done", "rest_done", "mid_done", "low_done", "parts_stored"))
        v_done, v_out, v_stored = (s.sems(n, 2) for n in ("v_done", "v_out", "v_stored"))
        edges_stored = s.sem("edges_stored")
        edge = s.sb("edge", [P, D])
        block = s.block()
        xv = x.rearrange("(u k i p) c -> u k p i c", p=P, i=TILES, k=2)

        @block.sync
        def _(sp):
            for n, src in enumerate((wq_t, wk_t, wv_t)):
                sp.dma_start(w[:, n, :, :], src.rearrange("(k p) f -> p k f", p=P)).then_inc(w_loaded, 16)
            if rel:
                for hh in range(P // DH):
                    sp.dma_start(kbias[hh * DH:(hh + 1) * DH, 1:2], pek0.rearrange("a d -> d a")).then_inc(w_loaded, 16)
                sp.dma_start(vbias[:, :], bass.AP(pev0.tensor, pev0.offset, [[0, P], [1, DH]])).then_inc(w_loaded, 16)
            for k in range(2):
                sp.dma_start(xg[:, k, :, :], xv[0, k, :, :, :]).then_inc(x_loaded[k], 16)
            def turn(t):
                done = sp.snap(t + 1)
                col = sp.snap((t % 2) * (2 * GROUP) + off)
                batch = sp.snap(t // 2)
                tile = sp.snap((t % 2) * (2 * TILES))
                ahead = sp.snap((t + 1) % turns)
                for k in range(2):
                    sp.wait_ge(normed[k], done)
                    sp.dma_start(xg[:, k, :, :], xv[ahead, k, :, :, :]).then_inc(x_loaded[k], 16)
                for k in range(2):
                    for q in range(4):
                        a, ck = q // 2, q % 2
                        sp.wait_ge(low_done[k][q], done)
                        dst = qk[a, :, ck * P:(ck + 1) * P, batch, bass.ds(col + k * GROUP, GROUP)]
                        sp.dma_start(dst.rearrange("a f c -> f a c"), parts[:, k, q, :, :])\
                            .then_inc(parts_stored[k][q], 16)
                    sp.wait_ge(v_out[k], done)
                    if rel:
                        dst = v[batch, :, :, bass.ds(tile + k * TILES, TILES), :]
                        sp.dma_start(dst.rearrange("h p i d -> p h i d"), vout[:, k, :, :, :]).then_inc(v_stored[k], 16)
                    else:
                        dst = v[batch, bass.ds(col + k * GROUP, GROUP), :]
                        sp.dma_start(dst.rearrange("(i p) c -> p i c", p=P), vout[:, k, :, :]).then_inc(v_stored[k], 16)

            for_turns(sp, turns, turn)
            for k in range(2):
                sp.wait_ge(x_loaded[k], 16 * (turns + 1))
                for q in range(4):
                    sp.wait_ge(parts_stored[k][q], 16 * turns)
                sp.wait_ge(v_stored[k], 16 * turns)

        n_consts = 16 * (3 + (P // DH + 1) * rel)

        @block.gpsimd
        def _(pool):
            make_identity(nc, pool, ident, zeroed, ident_ready)
            nc.gpsimd.memset(eps[:, :], LN_EPS).then_inc(const_set, 1)
            if not rel:
                nc.gpsimd.memset(kbias[:, :], 0.0).then_inc(const_set, 1)
                nc.gpsimd.memset(edge[:, :], 0.0).then_inc(const_set, 1)
                pool.wait_ge(const_set, 3)
                for bb in range(B):
                    for c0 in (0, PAD + L):
                        for a in range(2):
                            for part in range(3):
                                for ck in range(CK):
                                    pool.dma_start(qk[a, part, ck * P:(ck + 1) * P, bb, c0:c0 + PAD],
                                                   edge[:, 0:PAD // 2].bitcast(BF16)).then_inc(edges_stored, 16)
                        pool.dma_start(v[bb, c0:c0 + PAD, :], edge[0:PAD, :]).then_inc(edges_stored, 16)
            else:
                nc.gpsimd.memset(kbias[:, 0:1], 0.0).then_inc(const_set, 1)
            def turn(t):
                done = pool.snap(t + 1)
                for k in range(2):
                    for q in range(4):
                        pool.wait_ge(mid_done[k][q], done)
                        nc.gpsimd.tensor_tensor(parts[:, k, q, 2, :], rest[:, q, :], parts[:, k, q, 1, :],
                                                ALU.subtract).then_inc(low_done[k][q], 1)

            for_turns(pool, turns, turn)
            if not rel:
                pool.wait_ge(edges_stored, 16 * B * 2 * (2 * 3 * CK + 1))

        @block.vector
        def _(dve):
            dve.wait_ge(w_loaded, n_consts)
            dve.wait_ge(const_set, 2)
            def turn(t):
                done, loaded = dve.snap(t + 1), dve.snap(t * 16 + 16)
                before = dve.snap(t * 16)
                for k in range(2):
                    dve.wait_ge(x_loaded[k], loaded)
                    for i in range(TILES):
                        last = nc.vector.bn_stats(stats[:, k, i, :], xg[:, k, i, :])
                    last.then_inc(stats_done[k], 1)
                    dve.wait_ge(stats_done[k], done)
                    nc.vector.memset(spare[:, :], 0.0)
                    for i in range(TILES):
                        last = nc.vector.bn_aggr(mv[:, k, i, :], stats[:, k, i, :])
                    last.then_inc(mv_done[k], 1)
                    dve.wait_ge(std_done[k], done)
                    nc.vector.reciprocal(rstd[:, k, :], std[:, k, :]).then_inc(rstd_done[k], 1)
                    dve.wait_ge(rstd_done[k], done)
                    dve.wait_ge(turned[k], t)
                    for i in range(TILES):
                        last = nc.vector.tensor_scalar(xn[:, k, i, :], xg[:, k, i, :], mv[:, k, i, 0:1],
                                                       rstd[:, k, i:i + 1], ALU.subtract, ALU.mult)
                    last.then_inc(normed[k], 1)
                    dve.wait_ge(turned[k], done)
                    nc.vector.tensor_copy(xt[:, k, 1, :], ps_t[:, 1, :]).then_inc(turned_out_v[k], 1)
                    for q in range(4):
                        dve.wait_ge(high_done[k][q], done)
                        if k:
                            dve.wait_ge(low_done[0][q], done)
                        else:
                            dve.wait_ge(low_done[1][q], t)
                        scale_or_bias, op = (SCORE_SCALE, ALU.mult) if q < 2 else (kbias[:, 1:2], ALU.add)
                        nc.vector.scalar_tensor_tensor(rest[:, q, :], ps_qk[:, q, :], scale_or_bias,
                                                       parts[:, k, q, 0, :], op, ALU.subtract)\
                            .then_inc(rest_done[k][q], 1)
                    dve.wait_ge(v_done[k], done)
                    dve.wait_ge(v_stored[k], before)
                    for i in range(TILES):
                        if rel:
                            last = nc.vector.tensor_tensor(vout[:, k, :, i, :],
                                                           ps_v[:, i, :].rearrange("p (h d) -> p h d", d=DH),
                                                           vbias[:, None, :].to_broadcast([P, H, DH]), ALU.add)
                        else:
                            last = nc.vector.tensor_copy(vout[:, k, i, :], ps_v[:, i, :])
                    last.then_inc(v_out[k], 1)

            for_turns(dve, turns, turn)

        @block.scalar
        def _(act):
            act.wait_ge(w_loaded, n_consts)
            act.wait_ge(const_set, 2)
            def turn(t):
                done, before = act.snap(t + 1), act.snap(t * 16)
                for k in range(2):
                    act.wait_ge(mv_done[k], done)
                    nc.scalar.activation(std[:, k, :], mv[:, k, :, 1], ACT.Sqrt, bias=eps[:, 0:1]).then_inc(std_done[k], 1)
                    act.wait_ge(turned[k], done)
                    nc.scalar.activation(xt[:, k, 0, :], ps_t[:, 0, :], ACT.Copy).then_inc(turned_out_a[k], 1)
                    for q in range(4):
                        act.wait_ge(qk_done[k][q], done)
                        act.wait_ge(parts_stored[k][q], before)
                        nc.scalar.activation(parts[:, k, q, 0, :], ps_qk[:, q, :], ACT.Identity,
                                             bias=kbias[:, q // 2:q // 2 + 1], scale=SCORE_SCALE if q < 2 else 1.0)\
                            .then_inc(high_done[k][q], 1)
                    for q in range(4):
                        act.wait_ge(rest_done[k][q], done)
                        nc.scalar.activation(parts[:, k, q, 1, :], rest[:, q, :], ACT.Copy).then_inc(mid_done[k][q], 1)

            for_turns(act, turns, turn)

        @block.tensor
        def _(pe):
            pe.wait_ge(ident_ready, 1)
            pe.wait_ge(w_loaded, n_consts)
            def turn(t):
                done = pe.snap(t + 1)
                for k in range(2):
                    pe.wait_ge(normed[k], done)
                    for out in (turned_out_a, turned_out_v):
                        pe.wait_ge(out[1 - k], t if k == 0 else done)
                    for i in range(TILES):
                        for ck in range(CK):
                            last = nc.tensor.transpose(ps_t[:, ck, i * P:(i + 1) * P],
                                                       xn[:, k, i, ck * P:(ck + 1) * P], ident[:, :])
                    last.then_inc(turned[k], 1)
                    pe.wait_ge(turned_out_a[k], done)
                    pe.wait_ge(turned_out_v[k], done)
                    for q in range(4):
                        a, fc = q // 2, q % 2
                        pe.wait_ge(rest_done[1 - k][q], t if k == 0 else done)
                        for ck in range(CK):
                            last = nc.tensor.matmul(ps_qk[:, q, :], w[:, a, ck, fc * P:(fc + 1) * P],
                                                    xt[:, k, ck, :], start=ck == 0, stop=ck == CK - 1)
                        last.then_inc(qk_done[k][q], 1)
                    pe.wait_ge(v_out[1 - k], t if k == 0 else done)
                    for i in range(TILES):
                        for ck in range(CK):
                            last = nc.tensor.matmul(ps_v[:, i, :], xt[:, k, ck, i * P:(i + 1) * P],
                                                    w[:, 2, ck, :], start=ck == 0, stop=ck == CK - 1)
                    last.then_inc(v_done[k], 1)

            for_turns(pe, turns, turn)
EXPERTS = 8
HS = 512
HR = 256
RUN = GROUP // EXPERTS
HC, RC = HS // P, HR // P
RESIDUE = [3 * j % EXPERTS for j in range(EXPERTS)]


def ffn_stage(nc, name, x, out, sw1, sb1, sw3, sb3, sw2, sb2, w1, b1, w2, b2):
    turns = NTOK // GROUP // 2
    with Stage(nc, name) as s:
        ident, zeroed, ident_ready = s.sb("ident", [P, P]), s.sem("zeroed"), s.sem("ident_ready")
        w_loaded = s.sem("w_loaded")
        sw1_sb, sw3_sb = s.sb("sw1", [P, CK, HS]), s.sb("sw3", [P, CK, HS])
        sw2_in, sw2_sb = s.sb("sw2_in", [P, HC, D]), s.sb("sw2", [P, HC, D])
        w1_sb, w2_sb = s.sb("w1", [P, EXPERTS, CK, HR]), s.sb("w2", [P, EXPERTS, RC, D])
        sb1_sb, sb3_sb = s.sb("sb1", [P, HC]), s.sb("sb3", [P, HC])
        b1_sb = s.sb("b1", [P, EXPERTS, RC])
        b2_sb, sb2_sb = s.sb("b2", [P, CK, EXPERTS]), s.sb("sb2", [P, CK])
        bias, bias2, sb2x = s.sb("bias", [P, CK, EXPERTS]), s.sb("bias2", [P, CK, EXPERTS]), s.sb("sb2x", [P, CK])
        eps, spare = s.sb("eps", [P, 1]), s.sb("spare", [P, 1])
        const_set, bias_steps, doubled = s.sem("const_set"), s.sem("bias_steps"), s.sem("doubled")
        xg = s.sb("xg", [P, 2, TILES, D])
        xo = s.sb("xo", [P, 2, TILES, D])
        stats = s.sb("stats", [P, 2, TILES, 6])
        mv = s.sb("mv", [P, 2, TILES, 2])
        std, rstd = s.sb("std", [P, 2, TILES]), s.sb("rstd", [P, 2, TILES])
        xn = s.sb("xn", [P, 2, TILES, D])
        xt = s.sb("xt", [P, 2, CK, GROUP])
        sil = s.sb("sil", [P, 2, GROUP])
        gated = s.sb("gated", [P, HC, GROUP])
        hidden = s.sb("hidden", [P, EXPERTS, RC, 2 * RUN])
        yt = s.sb("yt", [P, CK, GROUP])
        ps_t = s.ps("ps_t", [P, CK, GROUP])
        ps_h = s.ps("ps_h", [P, 4, GROUP])
        ps_y = s.ps("ps_y", [P, CK, GROUP])

        x_loaded, stats_done, mv_done, std_done, rstd_done, normed = (
            s.sems(n, 2) for n in ("x_loaded", "stats_done", "mv_done", "std_done", "rstd_done", "normed"))
        turned, turned_out_a, turned_out_v = (s.sems(n, 2) for n in ("turned", "turned_out_a", "turned_out_v"))
        up_done, sil_done, gated_done = ([s.sems(f"{n}{k}", HC) for k in range(2)]
                                         for n in ("up_done", "sil_done", "gated_done"))
        eup_done, hidden_done = ([s.sems(f"{n}{k}", EXPERTS) for k in range(2)] for n in ("eup_done", "hidden_done"))
        down_done, y_out, back_done, res_done, stored = (
            s.sems(n, 2) for n in ("down_done", "y_out", "back_done", "res_done", "stored"))
        block = s.block()
        xv = x.rearrange("(u k n r) c -> u k r n c", k=2, n=RUN, r=EXPERTS)
        ov = out.rearrange("(u k n r) c -> u k r n c", k=2, n=RUN, r=EXPERTS)

        def pair(a, e):
            v = a.rearrange("p (j n) -> p j n", n=RUN)
            return v[:, e:e + 2, :] if e < EXPERTS - 1 else v[:, EXPERTS - 1::-(EXPERTS - 1), :]

        @block.sync
        def _(sp):
            def load(k, u):
                for j in range(EXPERTS):
                    sp.dma_start(xg[(j % 2) * RUN:(j % 2 + 1) * RUN, k, j // 2, :], xv[u, k, RESIDUE[j], :, :])\
                        .then_inc(x_loaded[k], 16)

            load(0, 0)
            sp.dma_start(sw1_sb[:, :, :], sw1.rearrange("(k p) f -> p k f", p=P)).then_inc(w_loaded, 16)
            sp.dma_start(sw3_sb[:, :, :], sw3.rearrange("(k p) f -> p k f", p=P)).then_inc(w_loaded, 16)
            sp.dma_start(w1_sb[:, :, :, :], w1.rearrange("e (k p) f -> p e k f", p=P)).then_inc(w_loaded, 16)
            sp.dma_start(sb1_sb[:, :], sb1.rearrange("(k p) -> p k", p=P),
                             allow_slow_non_contiguous=True).then_inc(w_loaded, 16)
            sp.dma_start(sb3_sb[:, :], sb3.rearrange("(k p) -> p k", p=P),
                             allow_slow_non_contiguous=True).then_inc(w_loaded, 16)
            sp.dma_start(sb2_sb[:, :], sb2.rearrange("(k p) -> p k", p=P),
                             allow_slow_non_contiguous=True).then_inc(w_loaded, 16)
            for c in range(RC):
                sp.dma_start(b1_sb[:, :, c], b1[:, c * P:(c + 1) * P].rearrange("e p -> p e"),
                             allow_slow_non_contiguous=True).then_inc(w_loaded, 16)
                sp.dma_start(b2_sb[:, c, :], b2[:, c * P:(c + 1) * P].rearrange("e p -> p e"),
                             allow_slow_non_contiguous=True).then_inc(w_loaded, 16)
            sp.dma_start(sw2_in[:, :, :], sw2.rearrange("(k p) f -> p k f", p=P)).then_inc(w_loaded, 16)
            sp.dma_start(w2_sb[:, :, :, :], w2.rearrange("e (k p) f -> p e k f", p=P)).then_inc(w_loaded, 16)
            load(1, 0)
            def turn(t):
                done = sp.snap(t + 1)
                ahead = sp.snap((t + 1) % turns)
                for k in range(2):
                    sp.wait_ge(res_done[k], done)
                    for j in range(EXPERTS):
                        sp.dma_start(ov[t, k, RESIDUE[j], :, :], xo[(j % 2) * RUN:(j % 2 + 1) * RUN, k, j // 2, :])\
                            .then_inc(stored[k], 16)
                    load(k, ahead)

            for_turns(sp, turns, turn)
            for k in range(2):
                sp.wait_ge(x_loaded[k], 16 * EXPERTS * (turns + 1))
                sp.wait_ge(stored[k], 16 * EXPERTS * turns)

        n_weights = 16 * (8 + 2 * RC)

        @block.gpsimd
        def _(pool):
            make_identity(nc, pool, ident, zeroed, ident_ready)
            nc.gpsimd.memset(eps[:, :], LN_EPS).then_inc(const_set, 1)
            pool.wait_ge(w_loaded, n_weights)
            nc.gpsimd.tensor_scalar(sw2_sb[:, :, :], sw2_in[:, :, :], 2.0, None, ALU.mult).then_inc(doubled, 1)

        @block.vector
        def _(dve):
            dve.wait_ge(w_loaded, n_weights)
            nc.vector.tensor_scalar(sb2x[:, :], sb2_sb[:, :], 2.0, None, ALU.mult).then_inc(bias_steps, 1)
            nc.vector.tensor_tensor(bias2[:, :, 1:EXPERTS], b2_sb[:, :, 1:EXPERTS], b2_sb[:, :, 0:EXPERTS - 1],
                                    ALU.add).then_inc(bias_steps, 1)
            nc.vector.tensor_tensor(bias2[:, :, 0:1], b2_sb[:, :, 0:1], b2_sb[:, :, EXPERTS - 1:EXPERTS],
                                    ALU.add).then_inc(bias_steps, 1)
            dve.wait_ge(bias_steps, 3)
            nc.vector.tensor_tensor(bias[:, :, :], bias2[:, :, :], sb2x[:, :, None].to_broadcast([P, CK, EXPERTS]),
                                    ALU.add).then_inc(bias_steps, 1)
            dve.wait_ge(bias_steps, 4)

            def normalise(t, done, loaded, k):
                dve.wait_ge(x_loaded[k], loaded)
                for i in range(TILES):
                    last = nc.vector.bn_stats(stats[:, k, i, :], xg[:, k, i, :])
                last.then_inc(stats_done[k], 1)
                dve.wait_ge(stats_done[k], done)
                nc.vector.memset(spare[:, :], 0.0)
                for i in range(TILES):
                    last = nc.vector.bn_aggr(mv[:, k, i, :], stats[:, k, i, :])
                last.then_inc(mv_done[k], 1)
                dve.wait_ge(std_done[k], done)
                nc.vector.reciprocal(rstd[:, k, :], std[:, k, :]).then_inc(rstd_done[k], 1)
                dve.wait_ge(rstd_done[k], done)
                dve.wait_ge(turned[k], t)
                for i in range(TILES):
                    last = nc.vector.tensor_scalar(xn[:, k, i, :], xg[:, k, i, :], mv[:, k, i, 0:1],
                                                   rstd[:, k, i:i + 1], ALU.subtract, ALU.mult)
                last.then_inc(normed[k], 1)

            def finish(t, done, before, k):
                dve.wait_ge(down_done[k], done)
                for fc in range(CK):
                    last = nc.vector.tensor_tensor(yt[:, fc, :].rearrange("p (j n) -> p j n", n=RUN),
                                                   ps_y[:, fc, :].rearrange("p (j n) -> p j n", n=RUN),
                                                   bias[:, fc, :, None].to_broadcast([P, EXPERTS, RUN]), ALU.add)
                last.then_inc(y_out[k], 1)

            def residual(t, done, before, k):
                dve.wait_ge(back_done[k], done)
                dve.wait_ge(stored[k], before)
                nc.vector.scalar_tensor_tensor(xo[:, k, :, :], ps_t[:, :, :].rearrange("p a (b c) -> p (a b) c", c=D),
                                               0.25, xg[:, k, :, :], ALU.mult, ALU.add).then_inc(res_done[k], 1)

            def turn(t):
                done, loaded = dve.snap(t + 1), dve.snap(t * (16 * EXPERTS) + 16 * EXPERTS)
                before = dve.snap(t * (16 * EXPERTS))
                for k in range(2):
                    normalise(t, done, loaded, k)
                    if k:
                        finish(t, done, before, 0)
                        residual(t, done, before, 0)
                    dve.wait_ge(turned[k], done)
                    nc.vector.tensor_copy(xt[:, k, 1, :], ps_t[:, 1, :]).then_inc(turned_out_v[k], 1)
                    for c in range(HC):
                        dve.wait_ge(sil_done[k][c], done)
                        if c == 0:
                            dve.wait_ge(down_done[1 - k], done if k else t)
                        nc.vector.scalar_tensor_tensor(gated[:, c, :], ps_h[:, 2 * (c % 2) + 1, :], sb3_sb[:, c:c + 1],
                                                       sil[:, c % 2, :], ALU.add, ALU.mult).then_inc(gated_done[k][c], 1)
                finish(t, done, before, 1)
                residual(t, done, before, 1)

            for_turns(dve, turns, turn)

        @block.scalar
        def _(act):
            act.wait_ge(w_loaded, n_weights)
            act.wait_ge(const_set, 1)
            def turn(t):
                done = act.snap(t + 1)
                for k in range(2):
                    act.wait_ge(mv_done[k], done)
                    nc.scalar.activation(std[:, k, :], mv[:, k, :, 1], ACT.Sqrt, bias=eps[:, 0:1]).then_inc(std_done[k], 1)
                    act.wait_ge(turned[k], done)
                    nc.scalar.activation(xt[:, k, 0, :], ps_t[:, 0, :], ACT.Copy).then_inc(turned_out_a[k], 1)
                    for c in range(HC):
                        act.wait_ge(up_done[k][c], done)
                        if c >= 2:
                            act.wait_ge(gated_done[k][c - 2], done)
                        else:
                            act.wait_ge(gated_done[1 - k][c + 2], done if k else t)
                        nc.scalar.activation(sil[:, c % 2, :], ps_h[:, 2 * (c % 2), :], ACT.Silu,
                                             bias=sb1_sb[:, c:c + 1]).then_inc(sil_done[k][c], 1)
                    act.wait_ge(down_done[1 - k], done if k else t)
                    for e in range(EXPERTS):
                        act.wait_ge(eup_done[k][e], done)
                        for c in range(RC):
                            last = nc.scalar.activation(hidden[:, e, c, :], ps_h[:, e % 4, c * 2 * RUN:(c + 1) * 2 * RUN],
                                                        ACT.Gelu, bias=b1_sb[:, e, c:c + 1])
                        last.then_inc(hidden_done[k][e], 1)

            for_turns(act, turns, turn)

        @block.tensor
        def _(pe):
            pe.wait_ge(ident_ready, 1)
            pe.wait_ge(w_loaded, n_weights)
            pe.wait_ge(doubled, 1)

            def turn_in(t, done, k):
                pe.wait_ge(normed[k], done)
                pe.wait_ge(res_done[1 - k], done if k else t)
                for i in range(TILES):
                    for ck in range(CK):
                        last = nc.tensor.transpose(ps_t[:, ck, i * P:(i + 1) * P], xn[:, k, i, ck * P:(ck + 1) * P],
                                                   ident[:, :])
                last.then_inc(turned[k], 1)

            def up(t, done, k):
                pe.wait_ge(turned_out_a[k], done)
                pe.wait_ge(turned_out_v[k], done)
                for c in range(HC):
                    if c < 2:
                        for e in (4 + 2 * c, 5 + 2 * c):
                            pe.wait_ge(hidden_done[1 - k][e], done if k else t)
                    else:
                        pe.wait_ge(gated_done[k][c - 2], done)
                    for n, w in enumerate((sw1_sb, sw3_sb)):
                        for ck in range(CK):
                            last = nc.tensor.matmul(ps_h[:, 2 * (c % 2) + n, :], w[:, ck, c * P:(c + 1) * P],
                                                    xt[:, k, ck, :], start=ck == 0, stop=ck == CK - 1)
                    last.then_inc(up_done[k][c], 1)
                for e in range(EXPERTS):
                    if e < 4:
                        pe.wait_ge(gated_done[k][2 + e // 2], done)
                    else:
                        pe.wait_ge(hidden_done[k][e - 4], done)
                    for c in range(RC):
                        for ck in range(CK):
                            last = nc.tensor.matmul(ps_h[:, e % 4, c * 2 * RUN:(c + 1) * 2 * RUN],
                                                    w1_sb[:, e, ck, c * P:(c + 1) * P], pair(xt[:, k, ck, :], e),
                                                    start=ck == 0, stop=ck == CK - 1)
                    last.then_inc(eup_done[k][e], 1)

            def down(t, done, k):
                pe.wait_ge(y_out[1 - k], done if k else t)
                pe.wait_ge(gated_done[k][HC - 1], done)
                for fc in range(CK):
                    for c in range(HC):
                        nc.tensor.matmul(ps_y[:, fc, :], sw2_sb[:, c, fc * P:(fc + 1) * P], gated[:, c, :],
                                         start=c == 0, stop=False, skip_group_check=True)
                for e in range(EXPERTS):
                    pe.wait_ge(hidden_done[k][e], done)
                    for fc in range(CK):
                        for c in range(RC):
                            last = nc.tensor.matmul(pair(ps_y[:, fc, :], e), w2_sb[:, e, c, fc * P:(fc + 1) * P],
                                                    hidden[:, e, c, :], start=False,
                                                    stop=e == EXPERTS - 1 and c == RC - 1, skip_group_check=True)
                last.then_inc(down_done[k], 1)

            def turn_back(t, done, k):
                pe.wait_ge(y_out[k], done)
                for i in range(TILES):
                    for fc in range(CK):
                        last = nc.tensor.transpose(ps_t[:, i // 2, (i % 2) * D + fc * P:(i % 2) * D + (fc + 1) * P],
                                                   yt[:, fc, i * P:(i + 1) * P], ident[:, :])
                last.then_inc(back_done[k], 1)

            def turn(t):
                done = pe.snap(t + 1)
                turn_in(t, done, 0)
                up(t, done, 0)
                down(t, done, 0)
                turn_back(t, done, 0)
                turn_in(t, done, 1)
                up(t, done, 1)
                down(t, done, 1)
                turn_back(t, done, 1)

            for_turns(pe, turns, turn)


def window_stage(nc, name, x, out, qk, v, wo_t, bo):
    turns = NTOK // GROUP // 2
    HG = 4
    PER_TILE = H // HG
    ITEMS = 2 * TILES * PER_TILE
    HALF = P // 2
    WIN = GROUP // HALF
    KEYS = GROUP + WINDOW
    VW = 32
    with Stage(nc, name) as s:
        ident, zeroed, ident_ready = s.sb("ident", [P, P]), s.sem("zeroed"), s.sem("ident_ready")
        identb, zeroedb = s.sb("identb", [P, P], BF16), s.sem("zeroedb")
        mask = s.sb("mask", [P, HG, P], BF16)
        mask_steps = s.sem("mask_steps")
        wo_sb, bo_sb = s.sb("wo", [P, CK, D]), s.sb("bo", [P, D])
        w_loaded = s.sem("w_loaded")
        qs = s.sb("qs", [STACK, 2, H, GROUP], BF16)
        ks = s.sb("ks", [STACK, 2, H, KEYS], BF16)
        vin = s.sb("vin", [P, 2, WIN, D])
        vp = s.sb("vp", [P, 2, WIN, H, VW])
        xg = s.sb("xg", [P, 2, TILES, D])
        xb = s.sb("xb", [P, 2, TILES, D])
        sc = s.sb("sc", [P, 2, HG, P])
        pr = s.sb("pr", [P, 2, HG, P])
        pt = s.sb("pt", [P, 2, HG, P])
        ot = s.sb("ot", [P, 2, P])
        top = s.sb("top", [P, 2, HG])
        rden = s.sb("rden", [P, 2, HG])
        att = s.sb("att", [P, 2, D])
        attt = s.sb("attt", [P, CK, P])
        xo = s.sb("xo", [P, 2, D])
        ps_s = s.ps("ps_s", [P, 2, HG, P])
        ps_p = s.ps("ps_p", [P, 2, HG, P])
        ps_o = s.ps("ps_o", [P, GROUP])
        ps_b = s.ps("ps_b", [P, GROUP])
        ps_w = s.ps("ps_w", [P, GROUP])
        ps_y = s.ps("ps_y", [P, GROUP])
        qk_loaded, v_loaded, x_loaded = (s.sems(n, 2) for n in ("qk_loaded", "v_loaded", "x_loaded"))
        v_ready, xb_ready = (s.sems(n, 2) for n in ("v_ready", "xb_ready"))
        vset = s.sem("vset")
        (scored, topped, less_top, expd, p_turned, p_out, pv_done, o_out, o_back, inverted, att_done) = (
            s.sem(n) for n in ("scored", "topped", "less_top", "expd", "p_turned", "p_out", "pv_done", "o_out",
                               "o_back", "inverted", "att_done"))
        w_turned, w_out, w_done, x_out = (s.sem(n) for n in ("w_turned", "w_out", "w_done", "x_out"))
        x_stored = s.sems("x_stored", 2)
        block = s.block()
        xv = x.rearrange("(u k i p) c -> u k p i c", p=P, i=TILES, k=2)
        ov = out.rearrange("(u k i p) c -> u k p i c", p=P, i=TILES, k=2)
        TT = 2 * TILES

        def u_batch(u):
            return u // 2

        def u_col(u):
            return (u % 2) * (2 * GROUP)

        @block.sync
        def _(sp):
            sp.dma_start(wo_sb[:, :, :], wo_t.rearrange("(k p) f -> p k f", p=P)).then_inc(w_loaded, 16)
            sp.dma_start(bo_sb[:, :], bass.AP(bo.tensor, bo.offset, [[0, P], [1, D]])).then_inc(w_loaded, 16)

            def load_q_k_x(k, u):
                batch, col = u_batch(u), u_col(u)
                for n in range(len(LEFT)):
                    sp.dma_start(qs[n * DH:(n + 1) * DH, k, :, :],
                                 qk[0, LEFT[n], :, batch, bass.ds(col + (PAD + k * GROUP), GROUP)]
                                 .rearrange("(h d) c -> d h c", d=DH)).then_inc(qk_loaded[k], 16)
                    sp.dma_start(ks[n * DH:(n + 1) * DH, k, :, :],
                                 qk[1, RIGHT[n], :, batch, bass.ds(col + k * GROUP, KEYS)]
                                 .rearrange("(h d) c -> d h c", d=DH)).then_inc(qk_loaded[k], 16)
                sp.dma_start(xg[:, k, :, :], xv[u, k, :, :, :]).then_inc(x_loaded[k], 16)

            def load_v(k, u):
                batch, col = u_batch(u), u_col(u)
                for odd in range(2):
                    sp.dma_start(vin[:, k, odd::2, :],
                                 v[batch, bass.ds(col + (k * GROUP + odd * HALF), GROUP), :]
                                 .rearrange("(w p) c -> p w c", p=P)).then_inc(v_loaded[k], 16)

            for k in range(2):
                load_q_k_x(k, 0)
                load_v(k, 0)

            def turn(t, last):
                tiles_out = [sp.snap(t * TT + i + 1) for i in range(TT)]
                done = sp.snap(t + 1)
                ahead = None if last else sp.snap(t + 1)
                for i in range(TT):
                    sp.wait_ge(x_out, tiles_out[i])
                    sp.dma_start(ov[t, i // TILES, :, i % TILES, :], xo[:, i % 2, :])\
                        .then_inc(x_stored[i % 2], 16)
                    if i % TILES == TILES - 1 and not last:
                        k = i // TILES
                        sp.wait_ge(v_ready[k], done)
                        load_q_k_x(k, ahead)
                        load_v(k, ahead)

            turn(0, False)
            with sp.Fori(1, turns - 1) as t:
                turn(t, False)
            turn(turns - 1, True)
            for slot in range(2):
                sp.wait_ge(x_stored[slot], 16 * turns * TILES)

        @block.gpsimd
        def _(pool):
            make_identity(nc, pool, ident, zeroed, ident_ready)
            make_identity(nc, pool, identb, zeroedb, ident_ready)
            nc.gpsimd.memset(mask[:, :, :], 0.0).then_inc(mask_steps, 1)
            nc.gpsimd.memset(vp[:, :, :, :, :], 0.0).then_inc(vset, 1)
            pool.wait_ge(vset, 1)
            step = 1
            for half in range(2):
                for base, sign in ((0, 1), (WINDOW - 1, -1)):
                    m = mask[half * HALF:(half + 1) * HALF, :, :]
                    pool.wait_ge(mask_steps, step)
                    nc.gpsimd.affine_select(out=m, in_=m, compare_op=ALU.is_ge, fill=MASKED, base=base,
                                            pattern=[[0, HG], [sign, P]], channel_multiplier=-sign)\
                        .then_inc(mask_steps, 1)
                    step += 1
            pool.wait_ge(mask_steps, step)
            nc.gpsimd.memset(vp[:, :, :, :, DH:DH + 1], 1.0).then_inc(vset, 1)
            pool.wait_ge(w_loaded, 32)
            def turn(t):
                tiles, done, loaded, loaded_v = (pool.snap(t * TT), pool.snap(t + 1), pool.snap(t * 16 + 16),
                                                 pool.snap(t * 32 + 32))
                for k in range(2):
                    pool.wait_ge(x_out, tiles)
                    pool.wait_ge(v_loaded[k], loaded_v)
                    pool.wait_ge(x_loaded[k], loaded)
                    nc.gpsimd.tensor_tensor(xb[:, k, :, :], xg[:, k, :, :],
                                            bo_sb[:, None, :].to_broadcast([P, TILES, D]), ALU.add)\
                        .then_inc(xb_ready[k], 1)
                    nc.gpsimd.tensor_copy(vp[:, k, :, :, 0:DH], vin[:, k, :, :].rearrange("p w (h d) -> p w h d", d=DH))\
                        .then_inc(v_ready[k], 1)

            for_turns(pool, turns, turn)

        def steps(lags, tile_lags):
            for n in range(ITEMS + 8):
                for what, lag in lags:
                    if 0 <= n - lag < ITEMS:
                        yield what, n - lag
                for what, lag in tile_lags:
                    m = n - lag
                    if 0 <= m < ITEMS and m % PER_TILE == PER_TILE - 1:
                        yield what, m // PER_TILE

        @block.vector
        def _(dve):
            def turn(t):
                base, tbase, done = dve.snap(t * ITEMS), dve.snap(t * TT), dve.snap(t + 1)
                sbase = dve.snap(t * (16 * TILES))

                def maximum(n):
                    dve.wait_ge(scored, base + n + 1)
                    nc.vector.tensor_reduce(top[:, n % 2, :], ps_s[:, n % 2, :, :], AX.X, ALU.max).then_inc(topped, 1)
                    dve.wait_ge(topped, base + n + 1)
                    if n >= 2:
                        dve.wait_ge(expd, base + n - 1)
                    nc.vector.tensor_tensor(sc[:, n % 2, :, :], ps_s[:, n % 2, :, :],
                                            top[:, n % 2, :, None].to_broadcast([P, HG, P]), ALU.subtract)\
                        .then_inc(less_top, 1)

                def weigh(n):
                    i, hg = n // PER_TILE, n % PER_TILE
                    view = ps_b[:, 0:P].rearrange("p (h d) -> p h d", d=VW)
                    dve.wait_ge(o_back, base + n + 1)
                    nc.vector.reciprocal(rden[:, n % 2, :], view[:, :, DH]).then_inc(inverted, 1)
                    dve.wait_ge(inverted, base + n + 1)
                    if hg == 0 and i >= 2:
                        dve.wait_ge(w_turned, tbase + i - 1)
                    nc.vector.tensor_tensor(att[:, i % 2, hg * HG * DH:(hg + 1) * HG * DH]
                                            .rearrange("p (h d) -> p h d", d=DH), view[:, :, 0:DH],
                                            rden[:, n % 2, :, None].to_broadcast([P, HG, DH]), ALU.mult)\
                        .then_inc(att_done, 1)

                def add_x(i):
                    dve.wait_ge(w_done, tbase + i + 1)
                    dve.wait_ge(xb_ready[i // TILES], done)
                    dve.wait_ge(x_stored[i % 2], sbase + 16 * (i // 2))
                    nc.vector.tensor_tensor(xo[:, i % 2, :], ps_y[:, 0:D], xb[:, i // TILES, i % TILES, :], ALU.add)\
                        .then_inc(x_out, 1)

                todo = {"max": maximum, "weigh": weigh, "add": add_x}
                for what, n in steps((("max", 0), ("weigh", 4)), (("add", 6),)):
                    todo[what](n)

            for_turns(dve, turns, turn)

        @block.scalar
        def _(act):
            def turn(t):
                base, tbase = act.snap(t * ITEMS), act.snap(t * TT)

                def exp(n):
                    act.wait_ge(less_top, base + n + 1)
                    if n >= 2:
                        act.wait_ge(p_turned, base + n - 1)
                    nc.scalar.activation(pr[:, n % 2, :, :], sc[:, n % 2, :, :], ACT.Exp)\
                        .then_inc(expd, 1)

                def copy_p(n):
                    act.wait_ge(p_turned, base + n + 1)
                    if n >= 2:
                        act.wait_ge(pv_done, base + n - 1)
                    nc.scalar.activation(pt[:, n % 2, :, :], ps_p[:, n % 2, :, :], ACT.Copy).then_inc(p_out, 1)

                def copy_o(n):
                    act.wait_ge(pv_done, base + n + 1)
                    if n >= 2:
                        act.wait_ge(o_back, base + n - 1)
                    nc.scalar.activation(ot[:, n % 2, :], ps_o[:, 0:P], ACT.Copy).then_inc(o_out, 1)

                def copy_att(i):
                    act.wait_ge(w_turned, tbase + i + 1)
                    act.wait_ge(w_done, tbase + i)
                    nc.scalar.activation(attt[:, :, :], ps_w[:, 0:D].rearrange("p (k q) -> p k q", k=CK), ACT.Copy)\
                        .then_inc(w_out, 1)

                todo = {"exp": exp, "copy_p": copy_p, "copy_o": copy_o, "copy_att": copy_att}
                for what, n in steps((("exp", 0), ("copy_p", 2), ("copy_o", 3)), (("copy_att", 5),)):
                    todo[what](n)

            for_turns(act, turns, turn)

        @block.tensor
        def _(pe):
            pe.wait_ge(ident_ready, 2)
            pe.wait_ge(mask_steps, 5)
            pe.wait_ge(vset, 2)
            pe.wait_ge(w_loaded, 32)
            def turn(t):
                base, tbase, done = pe.snap(t * ITEMS), pe.snap(t * TT), pe.snap(t + 1)
                n_qk = 16 * 2 * len(LEFT)
                qk_here = pe.snap(t * n_qk + n_qk)

                def score(n):
                    i, hg = n // PER_TILE, n % PER_TILE
                    k = i // TILES
                    if n % (TILES * PER_TILE) == 0:
                        pe.wait_ge(qk_loaded[k], qk_here)
                    if n >= 2:
                        pe.wait_ge(less_top, base + n - 1)
                    nc.tensor.matmul(ps_s[:, n % 2, :, :], identb[:, :], mask[:, :, :], start=True, stop=False,
                                     skip_group_check=True)
                    for h in range(HG):
                        for half in range(2):
                            q0 = (i % TILES) * P + half * HALF
                            last = nc.tensor.matmul(ps_s[half * HALF:(half + 1) * HALF, n % 2, h, :],
                                                    qs[:, k, hg * HG + h, q0:q0 + HALF],
                                                    ks[:, k, hg * HG + h, q0:q0 + P],
                                                    start=False, stop=h == HG - 1, skip_group_check=True)
                    last.then_inc(scored, 1)

                def turn_p(n):
                    pe.wait_ge(expd, base + n + 1)
                    if n >= 2:
                        pe.wait_ge(p_out, base + n - 1)
                    for h in range(HG):
                        last = nc.tensor.transpose(ps_p[:, n % 2, h, :], pr[:, n % 2, h, :], ident[:, :])
                    last.then_inc(p_turned, 1)

                def weigh_v(n):
                    i, hg = n // PER_TILE, n % PER_TILE
                    k = i // TILES
                    pe.wait_ge(p_out, base + n + 1)
                    if n % (TILES * PER_TILE) == 0:
                        pe.wait_ge(v_ready[k], done)
                    pe.wait_ge(o_out, base + n)
                    for half in range(2):
                        for h in range(HG):
                            last = nc.tensor.matmul(ps_o[h * VW:(h + 1) * VW, half * HALF:(half + 1) * HALF],
                                                    vp[:, k, 2 * (i % TILES) + half, hg * HG + h, :],
                                                    pt[:, n % 2, h, half * HALF:(half + 1) * HALF],
                                                    start=True, stop=True)
                    last.then_inc(pv_done, 1)

                def turn_o(n):
                    pe.wait_ge(o_out, base + n + 1)
                    pe.wait_ge(att_done, base + n)
                    nc.tensor.transpose(ps_b[:, 0:P], ot[:, n % 2, :], ident[:, :]).then_inc(o_back, 1)

                def turn_att(i):
                    pe.wait_ge(att_done, base + (i + 1) * PER_TILE)
                    pe.wait_ge(w_out, tbase + i)
                    for ck in range(CK):
                        last = nc.tensor.transpose(ps_w[:, ck * P:(ck + 1) * P], att[:, i % 2, ck * P:(ck + 1) * P],
                                                   ident[:, :])
                    last.then_inc(w_turned, 1)

                def project(i):
                    pe.wait_ge(w_out, tbase + i + 1)
                    pe.wait_ge(x_out, tbase + i)
                    for ck in range(CK):
                        last = nc.tensor.matmul(ps_y[:, 0:D], attt[:, ck, :], wo_sb[:, ck, :],
                                                start=ck == 0, stop=ck == CK - 1)
                    last.then_inc(w_done, 1)

                todo = {"score": score, "turn_p": turn_p, "weigh_v": weigh_v, "turn_o": turn_o,
                        "turn_att": turn_att, "project": project}
                for what, n in steps((("score", 0), ("turn_p", 2), ("weigh_v", 3), ("turn_o", 4)),
                                     (("turn_att", 5), ("project", 6))):
                    todo[what](n)

            for_turns(pe, turns, turn)


VECTOR_CHUNKS = ((0,), (1,), (1,), (1,))
LAGS = (-7, -6, 1, 2, 3, 4, 6, 7, 8, 9, 10)


def causal_stage(nc, name, att, qk, v, pek, pev, bias_rows, prob_rows):
    NEAR = 3 * P
    UNITS_HEAD = L // P
    HEADS = 2
    UNITS = HEADS * UNITS_HEAD
    turns = B * H // HEADS
    SLOTS = 8
    PSLOTS = 4
    RELATE, SHIFT, EXP, STORE, TURN, LOAD, TURN_W, WEIGH, COPY_O, TURN_O, COMBINE = LAGS
    LEAD, TAIL = -RELATE, COMBINE + 3
    GPH = UNITS_HEAD // 4
    CT = 32

    def far_chunks(i):
        keys = max(0, (i - 2) * P)
        return [(c, min(GROUP, keys - c)) for c in range(0, keys, GROUP)]

    def blocks_of(i):
        return [(c, min(4, i + 1 - c)) for c in range(0, i + 1, 4)]

    score_at, turned_at, uses, n_turned = {}, {}, [0, 0, 0], 0
    for m in range(UNITS):
        i = m % UNITS_HEAD
        for c in range(len(far_chunks(i)) + 1):
            bank = sum(uses) % 3
            score_at[m, c] = bank, uses[bank]
            uses[bank] += 1
        for c in range(len(blocks_of(i))):
            turned_at[m, c] = n_turned % 2, n_turned // 2
            n_turned += 1

    def use(t, m):
        return t * (UNITS // SLOTS) + (m // SLOTS + 1)

    def of_turn(t, m):
        return t + m // UNITS, m % UNITS

    def group_count(t, g):
        tt, g = of_turn(t, 4 * g)[0], g % (UNITS // 4)
        return tt * GPH + g % GPH + 1

    def bank_count(t, table, per_turn, m, c):
        tt, mm = of_turn(t, m)
        bank, n = table[mm, c]
        return bank, tt * per_turn[bank] + (n + 1)

    def emit(engine, steps):
        def turn(t, first, last):
            for n in range(-LEAD if first else 0, UNITS + (TAIL if last else 0)):
                steps(t, n, lambda m: (m >= 0 or not first) and (m < UNITS or not last), first)
        turn(0, True, False)
        with engine.Fori(1, turns - 1) as t:
            turn(t, False, False)
        turn(turns - 1, False, True)

    with Stage(nc, name) as s:
        ident, zeroed, ident_ready = s.sb("ident", [P, P]), s.sem("zeroed"), s.sem("ident_ready")
        pek_in, pev_in = s.sb("pek_in", [P, 2, DH]), s.sb("pev_in", [P, 2, DH])
        pek0, pev0 = s.sb("pek0", [P, DH]), s.sb("pev0", [P, DH])
        pek_d, pev_d = s.sb("pek_d", [P, 2, DH]), s.sb("pev_d", [P, 2, DH])
        pek_parts, pek_rest = s.sb("pek_parts", [DH, 3, MAX_REL], BF16), s.sb("pek_rest", [DH, MAX_REL])
        pek_s = s.sb("pek_s", [STACK, MAX_REL], BF16)
        edge0, edge1 = s.sb("edge0", [P, P]), s.sb("edge1", [P, P])
        spare = s.sb("spare", [P, 1])
        qs, ks = s.sb("qs", [STACK, HEADS, L], BF16), s.sb("ks", [STACK, HEADS, L], BF16)
        vh = s.sb("vh", [P, HEADS, UNITS_HEAD, DH])
        r_sb = s.sb("r_sb", [P, SLOTS, MAX_REL])
        bias = s.sb("bias", [P, SLOTS, NEAR])
        p = s.sb("p", [P, PSLOTS, 2 * P + L])
        w = s.sb("w", [P, SLOTS, MAX_REL])
        top = s.sb("top", [P, 2, 5])
        negtop = s.sb("negtop", [P, SLOTS])
        den = s.sb("den", [P, SLOTS, 4])
        rden = s.sb("rden", [P, 2, 4])
        pt = s.sb("pt", [P, 2, UNITS_HEAD, GROUP])
        wt = s.sb("wt", [P, 2, 2, GROUP])
        ot = s.sb("ot", [P, GROUP])
        osum = s.sb("osum", [P, 2, 4, DH])
        oh = s.sb("oh", [P, HEADS, UNITS_HEAD, DH])
        ps_r = s.ps("ps_r", [P, GROUP])
        ps_s = s.ps("ps_s", [P, 3, GROUP])
        ps_p = s.ps("ps_p", [P, 2, 4, P])
        ps_w = s.ps("ps_w", [P, GROUP])
        ps_o = s.ps("ps_o", [P, GROUP])

        c_loaded, setup, pek_turned, edges_set, edges_stored, stacked = (
            s.sem(n) for n in ("c_loaded", "setup", "pek_turned", "edges_set", "edges_stored", "stacked"))
        head_loaded, v_loaded, head_stored = (s.sems(n, HEADS) for n in ("head_loaded", "v_loaded", "head_stored"))
        r_out, r_stored, bias_loaded, expd, p_stored, w_loaded = (
            s.sems(n, SLOTS) for n in ("r_out", "r_stored", "bias_loaded", "expd", "p_stored", "w_loaded"))
        scored, score_out = s.sems("scored", 3), s.sems("score_out", 3)
        turned, turned_out = s.sems("turned", 2), s.sems("turned_out", 2)
        w_turned = s.sems("w_turned", SLOTS)
        pv_done, o_done = s.sems("pv_done", HEADS), s.sems("o_done", HEADS)
        (r_done, neg_done, w_out, o_out, o_back, o_summed, inverted) = (
            s.sem(n) for n in ("r_done", "neg_done", "w_out", "o_out", "o_back", "o_summed", "inverted"))
        S_USES, P_USES = uses, [n_turned // 2, n_turned // 2]
        att_v = att.rearrange("(b i p) (h d) -> b p i h d", b=B, p=P, d=DH)
        passed = s.sem("passed")
        HEAD_DMAS = 2 * len(LEFT)
        block = s.block()

        def copied_by_vector(i):
            return VECTOR_CHUNKS[i // 4]

        def group_read(engine, t, g, valid):
            if valid(4 * (g - 2)):
                engine.wait_ge(pv_done[((g - 2) // GPH) % HEADS], group_count(t, g - 2))

        def copy_p(engine, copy, t, m, c, valid):
            i, g = m % UNITS_HEAD, m // 4
            b0, blocks = blocks_of(i)[c]
            bank, count = bank_count(t, turned_at, P_USES, m, c)
            group_read(engine, t, g, valid)
            engine.wait_ge(turned[bank], count)
            copy(pt[:, g % 2, b0:b0 + blocks, (i % 4) * P:(i % 4 + 1) * P], ps_p[:, bank, 0:blocks, :])\
                .then_inc(turned_out[bank], 1)

        @block.sync
        def _(sp):
            sp.dma_start(pek_in[:, :, :], pek[1:1 + MAX_REL, :].rearrange("(k p) d -> p k d", p=P)).then_inc(c_loaded, 16)
            sp.dma_start(pev_in[:, :, :], pev[1:1 + MAX_REL, :].rearrange("(k p) d -> p k d", p=P)).then_inc(c_loaded, 16)
            sp.dma_start(pek0[:, :], bass.AP(pek.tensor, pek.offset, [[0, P], [1, DH]])).then_inc(c_loaded, 16)
            sp.dma_start(pev0[:, :], bass.AP(pev.tensor, pev.offset, [[0, P], [1, DH]])).then_inc(c_loaded, 16)

            def load_v(k, batch, h):
                sp.dma_start(vh[:, k, :, :], v[batch, h, :, :, :]).then_inc(v_loaded[k], 16)

            def load_qk(k, batch, h):
                for n in range(len(LEFT)):
                    sp.dma_start(qs[n * DH:(n + 1) * DH, k, :],
                                 qk[0, LEFT[n], bass.ds(h * DH, DH), batch, :]).then_inc(head_loaded[k], 16)
                    sp.dma_start(ks[n * DH:(n + 1) * DH, k, :],
                                 qk[1, RIGHT[n], bass.ds(h * DH, DH), batch, :]).then_inc(head_loaded[k], 16)

            for k in range(HEADS):
                load_qk(k, 0, k)
                load_v(k, 0, k)
            sp.wait_ge(edges_set, 2)
            for slot in range(SLOTS):
                sp.dma_start(bias_rows[slot, :, 0:P], edge0[:, :]).then_inc(edges_stored, 16)
                sp.dma_start(bias_rows[slot, :, NEAR:NEAR + P], edge1[:, :]).then_inc(edges_stored, 16)
            sp.wait_ge(setup, 5)
            for n in range(len(LEFT)):
                sp.dma_start(pek_s[n * DH:(n + 1) * DH, :], pek_parts[:, RIGHT[n], :]).then_inc(stacked, 16)
            sp.wait_ge(edges_stored, 16 * 2 * SLOTS)

            def turn(t, first, last):
                low, high = (0 if first else -3), UNITS // SLOTS + 3
                cnt = {j: t * (UNITS // SLOTS) + j for j in range(low, high)}
                cnt16 = {j: t * (16 * UNITS // SLOTS) + 16 * j for j in range(low, high)}

                def wait_both(*pairs):
                    values = [v if isinstance(v, int) else sp.to_reg(v) for _, v in pairs]
                    for (what, _), value in zip(pairs, values):
                        sp.wait_ge(what, value)

                nxt = None if last else sp.snap(t + 1)
                if not last:
                    batch_n, head_n = sp.snap(nxt // (H // HEADS)), sp.snap((nxt % (H // HEADS)) * HEADS)
                batch, head = sp.snap(t // (H // HEADS)), sp.snap((t % (H // HEADS)) * HEADS)

                def store_r(m):
                    sl, j = m % SLOTS, m // SLOTS
                    reused = not (first and m < SLOTS)
                    wait_both((r_out[sl], cnt[j + 1]), *[(bias_loaded[sl], cnt16[j])] * reused)
                    sp.dma_start(bias_rows[sl, :, P:P + MAX_REL], r_sb[:, sl, :]).then_inc(r_stored[sl], 16)

                def load_bias(m):
                    sl, j, i = m % SLOTS, m // SLOTS, m % UNITS_HEAD
                    skip = NEAR - min(i + 1, 3) * P
                    rows = bias_rows[sl, :, :]
                    reused = not (first and m < SLOTS)
                    wait_both((r_stored[sl], cnt16[j + 1]), *[(expd[sl], cnt[j])] * reused)
                    sp.dma_start(bias[:, sl, skip:], bass.AP(rows.tensor, rows.offset + P - 1 + skip,
                                                            [[4 * P - 1, P], [1, NEAR - skip]])).then_inc(bias_loaded[sl], 16)

                def store_p(m):
                    sl, j, i = m % SLOTS, m // SLOTS, m % UNITS_HEAD
                    reused = not (first and m < SLOTS)
                    wait_both((expd[sl], cnt[j + 1]), *[(w_loaded[sl], cnt16[j])] * reused)
                    sp.dma_start(prob_rows[sl, :, :], p[:, m % PSLOTS, i * P:i * P + NEAR]).then_inc(p_stored[sl], 16)

                def load_w(m):
                    sl, j = m % SLOTS, m // SLOTS
                    rows = prob_rows[sl, :, :]
                    reused = not (first and m < SLOTS)
                    wait_both((p_stored[sl], cnt16[j + 1]), *[(w_turned[sl], cnt[j])] * reused)
                    sp.dma_start(w[:, sl, :], bass.AP(rows.tensor, rows.offset + 1, [[NEAR + 1, P], [1, MAX_REL]]))\
                        .then_inc(w_loaded[sl], 16)

                todo = {"store_r": store_r, "load_bias": load_bias, "store_p": store_p, "load_w": load_w}

                def head_over(m):
                    k = (m // UNITS_HEAD) % HEADS
                    prev = m < 0
                    wait_both((o_done[k], groups[0 if prev else 1]))
                    sp.sem_inc(passed, 1)
                    bb, hh = (batch_p, head_p) if prev else (batch, head)
                    sp.dma_start(att_v[bb, :, :, hh + k, :], oh[:, k, :, :]).then_inc(head_stored[k], 16)

                groups = {0: sp.snap(t * GPH), 1: sp.snap(t * GPH + GPH)}
                if not first:
                    batch_p = sp.snap((t - 1) // (H // HEADS))
                    head_p = sp.snap(((t - 1) % (H // HEADS)) * HEADS)
                for n in range(-LEAD if first else 0, UNITS + (TAIL + 3 if last else 0)):
                    for what, lag in (("store_r", RELATE), ("load_bias", SHIFT), ("store_p", STORE), ("load_w", LOAD)):
                        m = n - lag
                        if (m >= 0 or not first) and (m < UNITS or not last):
                            todo[what](m)
                    m = n - COMBINE - 2
                    if m % UNITS_HEAD == UNITS_HEAD - 1 and (m >= 0 or not first) and (m < UNITS or not last):
                        head_over(m)
                    m = n - STORE
                    if m % UNITS_HEAD == UNITS_HEAD - 1 and 0 <= m < UNITS and not last:
                        k = m // UNITS_HEAD
                        wait_both((expd[m % SLOTS], cnt[m // SLOTS + 1]))
                        sp.sem_inc(passed, 1)
                        load_qk(k, batch_n, head_n + k)
                    elif m == -1 and not first:
                        wait_both((expd[m % SLOTS], cnt[0]))
                        sp.sem_inc(passed, 1)
                        load_qk(HEADS - 1, batch, head + HEADS - 1)
                    m = n - WEIGH - 1
                    if m % UNITS_HEAD == UNITS_HEAD - 1 and 0 <= m < UNITS and not last:
                        k = m // UNITS_HEAD
                        wait_both((pv_done[k], groups[1]))
                        sp.sem_inc(passed, 1)
                        load_v(k, batch_n, head_n + k)
                    elif m == -1 and not first:
                        wait_both((pv_done[HEADS - 1], groups[0]))
                        sp.sem_inc(passed, 1)
                        load_v(HEADS - 1, batch, head + HEADS - 1)

            turn(0, True, False)
            with sp.Fori(1, turns - 1) as t:
                turn(t, False, False)
            turn(turns - 1, False, True)
            for k in range(HEADS):
                sp.wait_ge(head_stored[k], 16 * turns)

        @block.gpsimd
        def _(pool):
            make_identity(nc, pool, ident, zeroed, ident_ready)
            nc.gpsimd.memset(edge0[:, :], 0.0).then_inc(edges_set, 1)
            nc.gpsimd.memset(edge1[:, :], MASKED).then_inc(edges_set, 1)

        @block.vector
        def _(dve):
            nc.vector.memset(p[:, :, 0:2 * P], 0.0)
            nc.vector.memset(ps_o[:, :], 0.0)
            dve.wait_ge(c_loaded, 64)
            nc.vector.tensor_tensor(pek_d[:, :, :], pek_in[:, :, :], pek0[:, None, :].to_broadcast([P, 2, DH]),
                                    ALU.subtract).then_inc(setup, 1)
            nc.vector.tensor_tensor(pev_d[:, :, :], pev_in[:, :, :], pev0[:, None, :].to_broadcast([P, 2, DH]),
                                    ALU.subtract).then_inc(setup, 1)
            dve.wait_ge(pek_turned, 1)
            nc.vector.tensor_copy(pek_parts[:, 0, :], ps_r[0:DH, 0:MAX_REL]).then_inc(setup, 1)
            dve.wait_ge(setup, 3)
            nc.vector.tensor_tensor(pek_rest[:, :], ps_r[0:DH, 0:MAX_REL], pek_parts[:, 0, :], ALU.subtract).then_inc(pek_turned, 1)
            dve.wait_ge(pek_turned, 2)
            nc.vector.tensor_copy(pek_parts[:, 1, :], pek_rest[:, :]).then_inc(setup, 1)
            dve.wait_ge(setup, 4)
            nc.vector.tensor_tensor(pek_parts[:, 2, :], pek_rest[:, :], pek_parts[:, 1, :], ALU.subtract).then_inc(setup, 1)

            def score_chunk(t, m, c, valid):
                sl, i = m % SLOTS, m % UNITS_HEAD
                far = far_chunks(i)
                bank, count = bank_count(t, score_at, S_USES, m, c)
                before = m - PSLOTS
                if c == 0 and valid(before):
                    b0, c0 = bank_count(t, turned_at, P_USES, before, len(blocks_of(before % UNITS_HEAD)) - 1)
                    dve.wait_ge(turned[b0], c0)
                    dve.wait_ge(p_stored[before % SLOTS], 16 * use(t, before))
                if c < len(far):
                    k0, keys = far[c]
                    dve.wait_ge(scored[bank], count)
                    nc.vector.tensor_scalar(p[:, m % PSLOTS, 2 * P + k0:2 * P + k0 + keys], ps_s[:, bank, 0:keys], 0.0, -3e38,
                                            ALU.add, ALU.max, accum_out=top[:, m % 2, c:c + 1])\
                        .then_inc(score_out[bank], 1)
                    return
                keys = min(i + 1, 3) * P
                k0 = (i + 1) * P - keys
                dve.wait_ge(bias_loaded[sl], 16 * use(t, m))
                dve.wait_ge(scored[bank], count)
                nc.vector.memset(spare[:, :], 0.0)
                nc.vector.tensor_tensor_reduce(out=p[:, m % PSLOTS, 2 * P + k0:2 * P + k0 + keys], in0=ps_s[:, bank, 0:keys],
                                               in1=bias[:, sl, NEAR - keys:NEAR], scale=1.0, scalar=-3e38,
                                               op0=ALU.add, op1=ALU.max, accum_out=top[:, m % 2, c:c + 1])\
                    .then_inc(score_out[bank], 1)
                dve.wait_ge(score_out[bank], count)
                nc.vector.tensor_reduce(negtop[:, sl:sl + 1], top[:, m % 2, 0:c + 1], AX.X, ALU.max, negate=True)\
                    .then_inc(neg_done, 1)

            def combine(t, g):
                k, gi = (g // GPH) % HEADS, g % GPH
                tiles = 3 if gi == 0 else 4
                dve.wait_ge(o_back, t * (UNITS // 4) + (g + 1))
                view = ps_o[:, :].rearrange("p (i c x) -> p i x c", i=4, x=CT)[:, :, 0:DH, 0:tiles]
                nc.vector.tensor_reduce(osum[:, g % 2, :, :], view, AX.X, ALU.add).then_inc(o_summed, 1)
                nc.vector.reciprocal(rden[:, g % 2, :], den[:, g % SLOTS, :]).then_inc(inverted, 1)
                dve.wait_ge(o_summed, t * (UNITS // 4) + (g + 1))
                dve.wait_ge(inverted, t * (UNITS // 4) + (g + 1))
                if gi == 0:
                    dve.wait_ge(head_stored[k], 16 * of_turn(t, 4 * g)[0])
                nc.vector.tensor_tensor(oh[:, k, 4 * gi:4 * gi + 4, :], osum[:, g % 2, :, :],
                                        rden[:, g % 2, :, None].to_broadcast([P, 4, DH]), ALU.mult).then_inc(o_done[k], 1)

            def steps(t, n, valid, first):
                m = n - TURN
                scores = len(far_chunks(n % UNITS_HEAD)) + 1 if n >= 0 and valid(n) else 0
                chunks = len(blocks_of(m % UNITS_HEAD)) if valid(m) else 0
                for c in range(max(scores, chunks)):
                    if c < scores:
                        score_chunk(t, n, c, valid)
                    if c < chunks and c in copied_by_vector(m % UNITS_HEAD):
                        copy_p(dve, nc.vector.tensor_copy, t, m, c, valid)
                m = n - COMBINE
                if m % 4 == 3 and valid(m):
                    combine(t, m // 4)

            emit(dve, steps)

        @block.scalar
        def _(act):
            def copy(out, in_):
                return nc.scalar.activation(out, in_, ACT.Copy)

            def exponentials(t, m, valid):
                tt, mm = of_turn(t, m)
                sl, i, g = m % SLOTS, m % UNITS_HEAD, m // 4
                act.wait_ge(neg_done, tt * UNITS + (mm + 1))
                if valid(4 * (g - SLOTS)):
                    act.wait_ge(inverted, t * (UNITS // 4) + (g - SLOTS + 1))
                row = p[:, m % PSLOTS, 2 * P:2 * P + (i + 1) * P]
                nc.scalar.activation(row, row, ACT.Exp, bias=negtop[:, sl:sl + 1],
                                     accum_out=den[:, g % SLOTS, i % 4:i % 4 + 1]).then_inc(expd[sl], 1)

            def steps(t, n, valid, first):
                m = n - RELATE
                if valid(m):
                    sl = m % SLOTS
                    tt, mm = of_turn(t, m)
                    act.wait_ge(r_done, tt * UNITS + (mm + 1))
                    if valid(m - SLOTS):
                        act.wait_ge(r_stored[sl], 16 * use(t, m - SLOTS))
                    copy(r_sb[:, sl, :], ps_r[:, 0:MAX_REL]).then_inc(r_out[sl], 1)
                m = n - TURN
                if valid(m):
                    for c in range(len(blocks_of(m % UNITS_HEAD))):
                        if c not in copied_by_vector(m % UNITS_HEAD):
                            copy_p(act, copy, t, m, c, valid)
                m = n - TURN_W
                if valid(m):
                    i, g = m % UNITS_HEAD, m // 4
                    group_read(act, t, g, valid)
                    act.wait_ge(w_turned[m % SLOTS], use(t, m))
                    copy(wt[:, g % 2, :, (i % 4) * P:(i % 4 + 1) * P], ps_w[:, 0:2 * P].rearrange("p (k q) -> p k q", k=2))\
                        .then_inc(w_out, 1)
                m = n - EXP
                if valid(m):
                    exponentials(t, m, valid)
                m = n - COPY_O
                if m % 4 == 3 and valid(m):
                    g = m // 4
                    act.wait_ge(pv_done[(g // GPH) % HEADS], group_count(t, g))
                    copy(ot[:, :], ps_o[:, :]).then_inc(o_out, 1)

            emit(act, steps)

        @block.tensor
        def _(pe):
            pe.wait_ge(ident_ready, 1)
            pe.wait_ge(setup, 2)
            for c in range(2):
                last = nc.tensor.transpose(ps_r[0:DH, c * P:(c + 1) * P], pek_d[:, c, :], ident[:, :])
            last.then_inc(pek_turned, 1)
            pe.wait_ge(stacked, 16 * len(LEFT))
            pe.wait_ge(pek_turned, 2)

            def relate(t, m, valid):
                tt, mm = of_turn(t, m)
                k, i = mm // UNITS_HEAD, m % UNITS_HEAD
                if i == 0:
                    pe.wait_ge(head_loaded[k], (16 * HEAD_DMAS) * tt + 16 * HEAD_DMAS)
                if valid(m - 1):
                    pe.wait_ge(r_out[(m - 1) % SLOTS], use(t, m - 1))
                nc.tensor.matmul(ps_r[:, 0:MAX_REL], qs[:, k, i * P:(i + 1) * P], pek_s[:, :], start=True, stop=True)\
                    .then_inc(r_done, 1)

            def score_chunk(t, m, c, valid):
                k, i = (m // UNITS_HEAD) % HEADS, m % UNITS_HEAD
                far = far_chunks(i)
                bank, count = bank_count(t, score_at, S_USES, m, c)
                near = min(i + 1, 3) * P
                k0, keys = far[c] if c < len(far) else ((i + 1) * P - near, near)
                pe.wait_ge(score_out[bank], count - 1)
                nc.tensor.matmul(ps_s[:, bank, 0:keys], qs[:, k, i * P:(i + 1) * P], ks[:, k, k0:k0 + keys],
                                 start=True, stop=True).then_inc(scored[bank], 1)

            def turn_chunk(t, m, c, valid):
                i = m % UNITS_HEAD
                b0, blocks = blocks_of(i)[c]
                bank, count = bank_count(t, turned_at, P_USES, m, c)
                if c == 0:
                    pe.wait_ge(expd[m % SLOTS], use(t, m))
                pe.wait_ge(turned_out[bank], count - 1)
                for b in range(blocks):
                    last = nc.tensor.transpose(ps_p[:, bank, b, :], p[:, m % PSLOTS, 2 * P + (b0 + b) * P:2 * P + (b0 + b + 1) * P],
                                               ident[:, :])
                last.then_inc(turned[bank], 1)

            def turn_w(t, m, valid):
                tt, mm = of_turn(t, m)
                pe.wait_ge(w_loaded[m % SLOTS], 16 * use(t, m))
                pe.wait_ge(w_out, tt * UNITS + mm)
                for c in range(2):
                    last = nc.tensor.transpose(ps_w[:, c * P:(c + 1) * P], w[:, m % SLOTS, c * P:(c + 1) * P], ident[:, :])
                last.then_inc(w_turned[m % SLOTS], 1)

            def weigh_v(t, g, valid):
                tt, mm = of_turn(t, 4 * g)
                k, gi = mm // UNITS_HEAD, g % GPH
                need = {}
                for m in range(4 * g, 4 * g + 4):
                    for c in range(len(blocks_of(m % UNITS_HEAD))):
                        bank, count = bank_count(t, turned_at, P_USES, m, c)
                        need[bank] = count
                for bank, count in need.items():
                    pe.wait_ge(turned_out[bank], count)
                pe.wait_ge(w_out, tt * UNITS + (mm + 4))
                if gi == 0:
                    pe.wait_ge(v_loaded[k], 16 * tt + 16)
                pe.wait_ge(o_summed, tt * (UNITS // 4) + mm // 4)
                v_of = lambda b: (vh[:, k, b, :], pt[:, g % 2, b, :], max(0, b - 4 * gi) * P)
                near = [(pev_d[:, c, :], wt[:, g % 2, c, :], 0) for c in range(2)]
                if gi == 0:
                    parts = [v_of(0), near[0], near[1], v_of(3), v_of(1), v_of(2)]
                    tiles = 3
                else:
                    parts = [v_of(b) for b in range(4 * gi + 4)] + near
                    tiles = 4
                for n, (left, right, q0) in enumerate(parts):
                    ct = n % tiles
                    last = nc.tensor.matmul(ps_o[ct * CT:ct * CT + DH, q0:GROUP], left, right[:, q0:GROUP],
                                            start=n < tiles, stop=n >= len(parts) - tiles, skip_group_check=True)
                last.then_inc(pv_done[k], 1)

            def turn_o(t, g):
                tt, mm = of_turn(t, 4 * g)
                pe.wait_ge(o_out, tt * (UNITS // 4) + (mm // 4 + 1))
                for q in range(4):
                    last = nc.tensor.transpose(ps_o[:, q * P:(q + 1) * P], ot[:, q * P:(q + 1) * P], ident[:, :])
                last.then_inc(o_back, 1)

            def steps(t, n, valid, first):
                if valid(n - RELATE):
                    relate(t, n - RELATE, valid)
                m = n - TURN_W
                if valid(m):
                    turn_w(t, m, valid)
                m = n - TURN
                scores = len(far_chunks(n % UNITS_HEAD)) + 1 if n >= 0 and valid(n) else 0
                chunks = len(blocks_of(m % UNITS_HEAD)) if valid(m) else 0
                for c in range(max(scores, chunks)):
                    if c < scores:
                        score_chunk(t, n, c, valid)
                    if c < chunks:
                        turn_chunk(t, m, c, valid)
                m = n - WEIGH
                if m % 4 == 3 and valid(m):
                    weigh_v(t, m // 4, valid)
                m = n - TURN_O
                if m % 4 == 3 and valid(m):
                    turn_o(t, m // 4)

            emit(pe, steps)


def output_stage(nc, name, x, att, out, wo_t):
    turns = NTOK // GROUP // 2
    with Stage(nc, name) as s:
        ident, zeroed, ident_ready = s.sb("ident", [P, P]), s.sem("zeroed"), s.sem("ident_ready")
        w, w_loaded = s.sb("w", [P, CK, D]), s.sem("w_loaded")
        ag, xg, xo = (s.sb(n, [P, 2, TILES, D]) for n in ("ag", "xg", "xo"))
        at = s.sb("at", [P, 2, CK, GROUP])
        ps_t = s.ps("ps_t", [P, 2, CK, GROUP])
        ps_y = s.ps("ps_y", [P, 2, TILES, D])
        loaded, turned, turned_out, y_done, x_out, stored = (
            s.sems(n, 2) for n in ("loaded", "turned", "turned_out", "y_done", "x_out", "stored"))
        block = s.block()
        av, xv, ov = (a.rearrange("(u k i p) c -> u k p i c", p=P, i=TILES, k=2) for a in (att, x, out))

        @block.sync
        def _(sp):
            def load(k, u):
                sp.dma_start(ag[:, k, :, :], av[u, k, :, :, :]).then_inc(loaded[k], 16)
                sp.dma_start(xg[:, k, :, :], xv[u, k, :, :, :]).then_inc(loaded[k], 16)

            load(0, 0)
            sp.dma_start(w[:, :, :], wo_t.rearrange("(k p) f -> p k f", p=P)).then_inc(w_loaded, 16)
            load(1, 0)

            def turn(t, last):
                for k in range(2):
                    sp.wait_ge(x_out[k], t + 1)
                    sp.dma_start(ov[t, k, :, :, :], xo[:, k, :, :]).then_inc(stored[k], 16)
                    if not last:
                        load(k, t + 1)

            turn(0, False)
            with sp.Fori(1, turns - 1) as t:
                turn(t, False)
            turn(turns - 1, True)
            for k in range(2):
                sp.wait_ge(stored[k], 16 * turns)

        @block.gpsimd
        def _(pool):
            make_identity(nc, pool, ident, zeroed, ident_ready)

        @block.scalar
        def _(act):
            def turn(t):
                for k in range(2):
                    act.wait_ge(turned[k], t + 1)
                    act.wait_ge(y_done[k], t)
                    nc.scalar.activation(at[:, k, :, :], ps_t[:, k, :, :], ACT.Copy).then_inc(turned_out[k], 1)

            for_turns(act, turns, turn)

        @block.vector
        def _(dve):
            def turn(t):
                for k in range(2):
                    dve.wait_ge(y_done[k], t + 1)
                    dve.wait_ge(stored[k], t * 16)
                    nc.vector.tensor_tensor(xo[:, k, :, :], ps_y[:, k, :, :], xg[:, k, :, :], ALU.add)\
                        .then_inc(x_out[k], 1)

            for_turns(dve, turns, turn)

        @block.tensor
        def _(pe):
            pe.wait_ge(ident_ready, 1)
            pe.wait_ge(w_loaded, 16)
            def turn(t):
                for k in range(2):
                    pe.wait_ge(loaded[k], t * 32 + 32)
                    pe.wait_ge(turned_out[k], t)
                    for i in range(TILES):
                        for ck in range(CK):
                            last = nc.tensor.transpose(ps_t[:, k, ck, i * P:(i + 1) * P], ag[:, k, i, ck * P:(ck + 1) * P],
                                                       ident[:, :])
                    last.then_inc(turned[k], 1)
                for k in range(2):
                    pe.wait_ge(turned_out[k], t + 1)
                    pe.wait_ge(x_out[k], t)
                    for i in range(TILES):
                        for ck in range(CK):
                            last = nc.tensor.matmul(ps_y[:, k, i, :], at[:, k, ck, i * P:(i + 1) * P], w[:, ck, :],
                                                    start=ck == 0, stop=ck == CK - 1)
                    last.then_inc(y_done[k], 1)

            for_turns(pe, turns, turn)


def hybrid_layer_kernel(nc, a, out):
    def scratch(name, shape, dt=F32):
        return nc.dram_tensor(name, shape, dt, kind="Internal").ap()

    x0 = a["x"].rearrange("b l c -> (b l) c")
    x1, x2, x3 = (scratch(f"x{n}", (NTOK, D)) for n in (1, 2, 3))
    qk_a = scratch("qk_a", (2, 3, D, B, L + 2 * PAD), BF16)
    v_a = scratch("v_a", (B, L + 2 * PAD, D))
    qk_b = scratch("qk_b", (2, 3, D, B, L), BF16)
    v_b = scratch("v_b", (B, H, P, L // P, DH))
    att = scratch("att", (NTOK, D))
    bias_rows = scratch("bias_rows", (8, P, 4 * P))
    prob_rows = scratch("prob_rows", (8, P, 3 * P))
    ffn = [a[n] for n in ("sw1", "sb1", "sw3", "sb3", "sw2", "sb2", "w1", "b1", "w2", "b2")]

    project_stage(nc, "pa", x0, a["a_wq_t"], a["a_wk_t"], a["a_wv_t"], qk_a, v_a)
    window_stage(nc, "wa", x0, x1, qk_a, v_a, a["a_wo_t"], a["bo"])
    ffn_stage(nc, "fa", x1, x2, *ffn)
    project_stage(nc, "pb", x2, a["b_wq_t"], a["b_wk_t"], a["b_wv_t"], qk_b, v_b, a["pek"][0:1, :], a["pev"][0:1, :])
    causal_stage(nc, "ca", att, qk_b, v_b, a["pek"], a["pev"], bias_rows, prob_rows)
    output_stage(nc, "ob", x2, att, x3, a["b_wo_t"])
    ffn_stage(nc, "fb", x3, out.rearrange("b l c -> (b l) c"), *ffn)


def kernel(**inputs):
    import numpy as _np
    import concourse.bacc as _bacc
    from concourse import mybir as _mybir
    from concourse.bass_utils import run_bass_kernel_spmd as _run

    i = {n.removeprefix("L0_"): _np.asarray(v) for n, v in inputs.items()}
    laid = {"x": i["attn_a_x"], "bo": i["attn_a_bo"], "pek": i["attn_b_pek"], "pev": i["attn_b_pev"]}
    for part in "ab":
        for m in ("Wq", "Wk", "Wv", "Wo"):
            laid[f"{part}_{m.lower()}_t"] = i[f"attn_{part}_{m}"].T
    for n in ("sw1", "sb1", "sw3", "sb3", "sw2", "sb2", "w1", "b1", "w2", "b2"):
        laid[n] = i[f"ffn_{n}"]

    nc = _bacc.Bacc("TRN2", target_bir_lowering=False, num_devices=1)
    arrays, aps = {}, {}
    for n, v in laid.items():
        arrays[f"in_{n}"] = _np.ascontiguousarray(v)
        aps[n] = nc.dram_tensor(f"in_{n}", v.shape, _mybir.dt.from_np(v.dtype), kind="ExternalInput").ap()
    out = nc.dram_tensor("out", (B, L, D), _mybir.dt.float32, kind="ExternalOutput").ap()
    hybrid_layer_kernel(nc, aps, out)
    return _run(nc, [arrays], core_ids=[0]).results[0]["out"]
```

```python
from contextlib import ExitStack

import concourse.bass as bass
from concourse import mybir

ALU = mybir.AluOpType
ACT = mybir.ActivationFunctionType
AX = mybir.AxisListType
F32 = mybir.dt.float32
BF16 = mybir.dt.bfloat16

P = 128
B, L, D = 2, 2048, 256
NTOK = B * L
CK = D // P
H = 16
DH = D // H
WINDOW = 64
PAD = WINDOW // 2
GROUP = 512
TILES = GROUP // P
MAX_REL = 256
LN_EPS = 1e-5
SCORE_SCALE = float(DH) ** -0.5
MASKED = -1e30
LEFT = (0, 0, 0, 1, 1, 2)
RIGHT = (0, 1, 2, 0, 1, 0)
STACK = len(LEFT) * DH


class Stage:

    def __init__(self, nc, name):
        self.nc, self.name, self.ctx, self.semaphores = nc, name, ExitStack(), []

    def __enter__(self):
        self.ctx.__enter__()
        return self

    def __exit__(self, *e):
        self.ctx.__exit__(*e)
        self.nc.clear_and_free_semaphores(self.semaphores)
        self.nc.all_engine_barrier()

    def sb(self, name, shape, dt=F32):
        return self.ctx.enter_context(self.nc.sbuf_tensor(f"{self.name}_{name}", shape, dt))

    def ps(self, name, shape, dt=F32):
        return self.ctx.enter_context(self.nc.psum_tensor(f"{self.name}_{name}", shape, dt))

    def sem(self, name):
        self.semaphores.append(self.nc.alloc_semaphore(f"{self.name}_{name}"))
        return self.semaphores[-1]

    def sems(self, name, n):
        return [self.sem(f"{name}{i}") for i in range(n)]

    def block(self):
        return self.ctx.enter_context(self.nc.Block())


def for_turns(engine, turns, turn):
    turn(0)
    with engine.Fori(1, turns) as t:
        turn(t)


def make_identity(nc, pool, ident, zeroed, ready):
    nc.gpsimd.memset(ident[:, :], 0.0).then_inc(zeroed, 1)
    pool.wait_ge(zeroed, 1)
    nc.gpsimd.affine_select(out=ident[:, :], in_=ident[:, :], compare_op=ALU.not_equal, fill=1.0,
                            base=0, pattern=[[-1, P]], channel_multiplier=1).then_inc(ready, 1)


def project_stage(nc, name, x, wq_t, wk_t, wv_t, qk, v, pek0=None, pev0=None):
    rel = pek0 is not None
    off = 0 if rel else PAD
    turns = NTOK // GROUP // 2
    with Stage(nc, name) as s:
        ident, zeroed, ident_ready = s.sb("ident", [P, P]), s.sem("zeroed"), s.sem("ident_ready")
        w = s.sb("w", [P, 3, CK, D])
        w_loaded = s.sem("w_loaded")
        eps = s.sb("eps", [P, 1])
        kbias = s.sb("kbias", [P, 2])
        vbias = s.sb("vbias", [P, DH])
        const_set = s.sem("const_set")
        xg = s.sb("xg", [P, 2, TILES, D])
        stats = s.sb("stats", [P, 2, TILES, 6])
        mv = s.sb("mv", [P, 2, TILES, 2])
        spare = s.sb("spare", [P, 1])
        std = s.sb("std", [P, 2, TILES])
        rstd = s.sb("rstd", [P, 2, TILES])
        xn = s.sb("xn", [P, 2, TILES, D])
        xt = s.sb("xt", [P, 2, CK, GROUP])
        parts = s.sb("parts", [P, 2, 4, 3, GROUP], BF16)
        rest = s.sb("rest", [P, 4, GROUP])
        vout = s.sb("vout", [P, 2, H, TILES, DH + 1]) if rel else s.sb("vout", [P, 2, TILES, D])
        ps_t = s.ps("ps_t", [P, CK, GROUP])
        ps_qk = s.ps("ps_qk", [P, 4, GROUP])
        ps_v = s.ps("ps_v", [P, TILES, D])

        x_loaded, stats_done, mv_done, std_done, rstd_done, normed = (
            s.sems(n, 2) for n in ("x_loaded", "stats_done", "mv_done", "std_done", "rstd_done", "normed"))
        turned, turned_out_a, turned_out_v = (s.sems(n, 2) for n in ("turned", "turned_out_a", "turned_out_v"))
        qk_done, high_done, rest_done, mid_done, low_done, parts_stored = (
            [s.sems(f"{n}{k}", 4) for k in range(2)]
            for n in ("qk_done", "high_done", "rest_done", "mid_done", "low_done", "parts_stored"))
        v_done, v_out, v_stored = (s.sems(n, 2) for n in ("v_done", "v_out", "v_stored"))
        edges_stored = s.sem("edges_stored")
        edge = s.sb("edge", [P, D])
        block = s.block()
        xv = x.rearrange("(u k i p) c -> u k p i c", p=P, i=TILES, k=2)

        @block.sync
        def _(sp):
            for n, src in enumerate((wq_t, wk_t, wv_t)):
                sp.dma_start(w[:, n, :, :], src.rearrange("(k p) f -> p k f", p=P)).then_inc(w_loaded, 16)
            if rel:
                for hh in range(P // DH):
                    sp.dma_start(kbias[hh * DH:(hh + 1) * DH, 1:2], pek0.rearrange("a d -> d a")).then_inc(w_loaded, 16)
                sp.dma_start(vbias[:, :], bass.AP(pev0.tensor, pev0.offset, [[0, P], [1, DH]])).then_inc(w_loaded, 16)
            for k in range(2):
                sp.dma_start(xg[:, k, :, :], xv[0, k, :, :, :]).then_inc(x_loaded[k], 16)
            def turn(t):
                done = sp.snap(t + 1)
                col = sp.snap((t % 2) * (2 * GROUP) + off)
                batch = sp.snap(t // 2)
                tile = sp.snap((t % 2) * (2 * TILES))
                ahead = sp.snap((t + 1) % turns)
                for k in range(2):
                    sp.wait_ge(normed[k], done)
                    sp.dma_start(xg[:, k, :, :], xv[ahead, k, :, :, :]).then_inc(x_loaded[k], 16)
                for k in range(2):
                    for q in range(4):
                        a, ck = q // 2, q % 2
                        sp.wait_ge(low_done[k][q], done)
                        dst = qk[a, :, ck * P:(ck + 1) * P, batch, bass.ds(col + k * GROUP, GROUP)]
                        sp.dma_start(dst.rearrange("a f c -> f a c"), parts[:, k, q, :, :])\
                            .then_inc(parts_stored[k][q], 16)
                    sp.wait_ge(v_out[k], done)
                    if rel:
                        dst = v[batch, :, :, bass.ds(tile + k * TILES, TILES), :]
                        sp.dma_start(dst.rearrange("h p i d -> p h i d"), vout[:, k, :, :, :]).then_inc(v_stored[k], 16)
                    else:
                        dst = v[batch, bass.ds(col + k * GROUP, GROUP), :]
                        sp.dma_start(dst.rearrange("(i p) c -> p i c", p=P), vout[:, k, :, :]).then_inc(v_stored[k], 16)

            for_turns(sp, turns, turn)
            for k in range(2):
                sp.wait_ge(x_loaded[k], 16 * (turns + 1))
                for q in range(4):
                    sp.wait_ge(parts_stored[k][q], 16 * turns)
                sp.wait_ge(v_stored[k], 16 * turns)

        n_consts = 16 * (3 + (P // DH + 1) * rel)

        @block.gpsimd
        def _(pool):
            make_identity(nc, pool, ident, zeroed, ident_ready)
            nc.gpsimd.memset(eps[:, :], LN_EPS).then_inc(const_set, 1)
            if not rel:
                nc.gpsimd.memset(kbias[:, :], 0.0).then_inc(const_set, 1)
                nc.gpsimd.memset(edge[:, :], 0.0).then_inc(const_set, 1)
                pool.wait_ge(const_set, 3)
                for bb in range(B):
                    for c0 in (0, PAD + L):
                        for a in range(2):
                            for part in range(3):
                                for ck in range(CK):
                                    pool.dma_start(qk[a, part, ck * P:(ck + 1) * P, bb, c0:c0 + PAD],
                                                   edge[:, 0:PAD // 2].bitcast(BF16)).then_inc(edges_stored, 16)
                        pool.dma_start(v[bb, c0:c0 + PAD, :], edge[0:PAD, :]).then_inc(edges_stored, 16)
            else:
                nc.gpsimd.memset(vout[:, :, :, :, DH:DH + 1], 1.0).then_inc(const_set, 1)
                nc.gpsimd.memset(kbias[:, 0:1], 0.0).then_inc(const_set, 1)
            def turn(t):
                done = pool.snap(t + 1)
                for k in range(2):
                    for q in range(4):
                        pool.wait_ge(mid_done[k][q], done)
                        nc.gpsimd.tensor_tensor(parts[:, k, q, 2, :], rest[:, q, :], parts[:, k, q, 1, :],
                                                ALU.subtract).then_inc(low_done[k][q], 1)

            for_turns(pool, turns, turn)
            if not rel:
                pool.wait_ge(edges_stored, 16 * B * 2 * (2 * 3 * CK + 1))

        @block.vector
        def _(dve):
            dve.wait_ge(w_loaded, n_consts)
            dve.wait_ge(const_set, 3)
            def turn(t):
                done, loaded = dve.snap(t + 1), dve.snap(t * 16 + 16)
                before = dve.snap(t * 16)
                for k in range(2):
                    dve.wait_ge(x_loaded[k], loaded)
                    for i in range(TILES):
                        last = nc.vector.bn_stats(stats[:, k, i, :], xg[:, k, i, :])
                    last.then_inc(stats_done[k], 1)
                    dve.wait_ge(stats_done[k], done)
                    nc.vector.memset(spare[:, :], 0.0)
                    for i in range(TILES):
                        last = nc.vector.bn_aggr(mv[:, k, i, :], stats[:, k, i, :])
                    last.then_inc(mv_done[k], 1)
                    dve.wait_ge(std_done[k], done)
                    nc.vector.reciprocal(rstd[:, k, :], std[:, k, :]).then_inc(rstd_done[k], 1)
                    dve.wait_ge(rstd_done[k], done)
                    dve.wait_ge(turned[k], t)
                    for i in range(TILES):
                        last = nc.vector.tensor_scalar(xn[:, k, i, :], xg[:, k, i, :], mv[:, k, i, 0:1],
                                                       rstd[:, k, i:i + 1], ALU.subtract, ALU.mult)
                    last.then_inc(normed[k], 1)
                    dve.wait_ge(turned[k], done)
                    nc.vector.tensor_copy(xt[:, k, 1, :], ps_t[:, 1, :]).then_inc(turned_out_v[k], 1)
                    for q in range(4):
                        dve.wait_ge(high_done[k][q], done)
                        if k:
                            dve.wait_ge(low_done[0][q], done)
                        else:
                            dve.wait_ge(low_done[1][q], t)
                        scale_or_bias, op = (SCORE_SCALE, ALU.mult) if q < 2 else (kbias[:, 1:2], ALU.add)
                        nc.vector.scalar_tensor_tensor(rest[:, q, :], ps_qk[:, q, :], scale_or_bias,
                                                       parts[:, k, q, 0, :], op, ALU.subtract)\
                            .then_inc(rest_done[k][q], 1)
                    dve.wait_ge(v_done[k], done)
                    dve.wait_ge(v_stored[k], before)
                    for i in range(TILES):
                        if rel:
                            last = nc.vector.tensor_tensor(vout[:, k, :, i, 0:DH],
                                                           ps_v[:, i, :].rearrange("p (h d) -> p h d", d=DH),
                                                           vbias[:, None, :].to_broadcast([P, H, DH]), ALU.add)
                        else:
                            last = nc.vector.tensor_copy(vout[:, k, i, :], ps_v[:, i, :])
                    last.then_inc(v_out[k], 1)

            for_turns(dve, turns, turn)

        @block.scalar
        def _(act):
            act.wait_ge(w_loaded, n_consts)
            act.wait_ge(const_set, 3)
            def turn(t):
                done, before = act.snap(t + 1), act.snap(t * 16)
                for k in range(2):
                    act.wait_ge(mv_done[k], done)
                    nc.scalar.activation(std[:, k, :], mv[:, k, :, 1], ACT.Sqrt, bias=eps[:, 0:1]).then_inc(std_done[k], 1)
                    act.wait_ge(turned[k], done)
                    nc.scalar.activation(xt[:, k, 0, :], ps_t[:, 0, :], ACT.Copy).then_inc(turned_out_a[k], 1)
                    for q in range(4):
                        act.wait_ge(qk_done[k][q], done)
                        act.wait_ge(parts_stored[k][q], before)
                        nc.scalar.activation(parts[:, k, q, 0, :], ps_qk[:, q, :], ACT.Identity,
                                             bias=kbias[:, q // 2:q // 2 + 1], scale=SCORE_SCALE if q < 2 else 1.0)\
                            .then_inc(high_done[k][q], 1)
                    for q in range(4):
                        act.wait_ge(rest_done[k][q], done)
                        nc.scalar.activation(parts[:, k, q, 1, :], rest[:, q, :], ACT.Copy).then_inc(mid_done[k][q], 1)

            for_turns(act, turns, turn)

        @block.tensor
        def _(pe):
            pe.wait_ge(ident_ready, 1)
            pe.wait_ge(w_loaded, n_consts)
            def turn(t):
                done = pe.snap(t + 1)
                for k in range(2):
                    pe.wait_ge(normed[k], done)
                    for out in (turned_out_a, turned_out_v):
                        pe.wait_ge(out[1 - k], t if k == 0 else done)
                    for i in range(TILES):
                        for ck in range(CK):
                            last = nc.tensor.transpose(ps_t[:, ck, i * P:(i + 1) * P],
                                                       xn[:, k, i, ck * P:(ck + 1) * P], ident[:, :])
                    last.then_inc(turned[k], 1)
                    pe.wait_ge(turned_out_a[k], done)
                    pe.wait_ge(turned_out_v[k], done)
                    for q in range(4):
                        a, fc = q // 2, q % 2
                        pe.wait_ge(rest_done[1 - k][q], t if k == 0 else done)
                        for ck in range(CK):
                            last = nc.tensor.matmul(ps_qk[:, q, :], w[:, a, ck, fc * P:(fc + 1) * P],
                                                    xt[:, k, ck, :], start=ck == 0, stop=ck == CK - 1)
                        last.then_inc(qk_done[k][q], 1)
                    pe.wait_ge(v_out[1 - k], t if k == 0 else done)
                    for i in range(TILES):
                        for ck in range(CK):
                            last = nc.tensor.matmul(ps_v[:, i, :], xt[:, k, ck, i * P:(i + 1) * P],
                                                    w[:, 2, ck, :], start=ck == 0, stop=ck == CK - 1)
                    last.then_inc(v_done[k], 1)

            for_turns(pe, turns, turn)
EXPERTS = 8
HS = 512
HR = 256
RUN = GROUP // EXPERTS
HC, RC = HS // P, HR // P
RESIDUE = [3 * j % EXPERTS for j in range(EXPERTS)]


def ffn_stage(nc, name, x, out, sw1, sb1, sw3, sb3, sw2, sb2, w1, b1, w2, b2):
    turns = NTOK // GROUP // 2
    with Stage(nc, name) as s:
        ident, zeroed, ident_ready = s.sb("ident", [P, P]), s.sem("zeroed"), s.sem("ident_ready")
        w_loaded = s.sem("w_loaded")
        sw1_sb, sw3_sb = s.sb("sw1", [P, CK, HS]), s.sb("sw3", [P, CK, HS])
        sw2_in, sw2_sb = s.sb("sw2_in", [P, HC, D]), s.sb("sw2", [P, HC, D])
        w1_sb, w2_sb = s.sb("w1", [P, EXPERTS, CK, HR]), s.sb("w2", [P, EXPERTS, RC, D])
        sb1_sb, sb3_sb = s.sb("sb1", [P, HC]), s.sb("sb3", [P, HC])
        b1_sb = s.sb("b1", [P, EXPERTS, RC])
        b2_sb, sb2_sb = s.sb("b2", [P, CK, EXPERTS]), s.sb("sb2", [P, CK])
        bias, bias2, sb2x = s.sb("bias", [P, CK, EXPERTS]), s.sb("bias2", [P, CK, EXPERTS]), s.sb("sb2x", [P, CK])
        eps, spare = s.sb("eps", [P, 1]), s.sb("spare", [P, 1])
        const_set, bias_steps, doubled = s.sem("const_set"), s.sem("bias_steps"), s.sem("doubled")
        xg = s.sb("xg", [P, 2, TILES, D])
        xo = s.sb("xo", [P, 2, TILES, D])
        stats = s.sb("stats", [P, 2, TILES, 6])
        mv = s.sb("mv", [P, 2, TILES, 2])
        std, rstd = s.sb("std", [P, 2, TILES]), s.sb("rstd", [P, 2, TILES])
        xn = s.sb("xn", [P, 2, TILES, D])
        xt = s.sb("xt", [P, 2, CK, GROUP])
        sil = s.sb("sil", [P, 2, GROUP])
        gated = s.sb("gated", [P, HC, GROUP])
        hidden = s.sb("hidden", [P, EXPERTS, RC, 2 * RUN])
        yt = s.sb("yt", [P, CK, GROUP])
        ps_t = s.ps("ps_t", [P, CK, GROUP])
        ps_h = s.ps("ps_h", [P, 4, GROUP])
        ps_y = s.ps("ps_y", [P, CK, GROUP])

        x_loaded, stats_done, mv_done, std_done, rstd_done, normed = (
            s.sems(n, 2) for n in ("x_loaded", "stats_done", "mv_done", "std_done", "rstd_done", "normed"))
        turned, turned_out_a, turned_out_v = (s.sems(n, 2) for n in ("turned", "turned_out_a", "turned_out_v"))
        up_done, sil_done, gated_done = ([s.sems(f"{n}{k}", HC) for k in range(2)]
                                         for n in ("up_done", "sil_done", "gated_done"))
        eup_done, hidden_done = ([s.sems(f"{n}{k}", EXPERTS) for k in range(2)] for n in ("eup_done", "hidden_done"))
        down_done, y_out, back_done, res_done, stored = (
            s.sems(n, 2) for n in ("down_done", "y_out", "back_done", "res_done", "stored"))
        block = s.block()
        xv = x.rearrange("(u k n r) c -> u k r n c", k=2, n=RUN, r=EXPERTS)
        ov = out.rearrange("(u k n r) c -> u k r n c", k=2, n=RUN, r=EXPERTS)

        def pair(a, e):
            v = a.rearrange("p (j n) -> p j n", n=RUN)
            return v[:, e:e + 2, :] if e < EXPERTS - 1 else v[:, EXPERTS - 1::-(EXPERTS - 1), :]

        @block.sync
        def _(sp):
            def load(k, u):
                for j in range(EXPERTS):
                    sp.dma_start(xg[(j % 2) * RUN:(j % 2 + 1) * RUN, k, j // 2, :], xv[u, k, RESIDUE[j], :, :])\
                        .then_inc(x_loaded[k], 16)

            load(0, 0)
            sp.dma_start(sw1_sb[:, :, :], sw1.rearrange("(k p) f -> p k f", p=P)).then_inc(w_loaded, 16)
            sp.dma_start(sw3_sb[:, :, :], sw3.rearrange("(k p) f -> p k f", p=P)).then_inc(w_loaded, 16)
            sp.dma_start(w1_sb[:, :, :, :], w1.rearrange("e (k p) f -> p e k f", p=P)).then_inc(w_loaded, 16)
            sp.dma_start(sb1_sb[:, :], sb1.rearrange("(k p) -> p k", p=P),
                             allow_slow_non_contiguous=True).then_inc(w_loaded, 16)
            sp.dma_start(sb3_sb[:, :], sb3.rearrange("(k p) -> p k", p=P),
                             allow_slow_non_contiguous=True).then_inc(w_loaded, 16)
            sp.dma_start(sb2_sb[:, :], sb2.rearrange("(k p) -> p k", p=P),
                             allow_slow_non_contiguous=True).then_inc(w_loaded, 16)
            for c in range(RC):
                sp.dma_start(b1_sb[:, :, c], b1[:, c * P:(c + 1) * P].rearrange("e p -> p e"),
                             allow_slow_non_contiguous=True).then_inc(w_loaded, 16)
                sp.dma_start(b2_sb[:, c, :], b2[:, c * P:(c + 1) * P].rearrange("e p -> p e"),
                             allow_slow_non_contiguous=True).then_inc(w_loaded, 16)
            sp.dma_start(sw2_in[:, :, :], sw2.rearrange("(k p) f -> p k f", p=P)).then_inc(w_loaded, 16)
            sp.dma_start(w2_sb[:, :, :, :], w2.rearrange("e (k p) f -> p e k f", p=P)).then_inc(w_loaded, 16)
            load(1, 0)
            def turn(t):
                done = sp.snap(t + 1)
                ahead = sp.snap((t + 1) % turns)
                for k in range(2):
                    sp.wait_ge(res_done[k], done)
                    for j in range(EXPERTS):
                        sp.dma_start(ov[t, k, RESIDUE[j], :, :], xo[(j % 2) * RUN:(j % 2 + 1) * RUN, k, j // 2, :])\
                            .then_inc(stored[k], 16)
                    load(k, ahead)

            for_turns(sp, turns, turn)
            for k in range(2):
                sp.wait_ge(x_loaded[k], 16 * EXPERTS * (turns + 1))
                sp.wait_ge(stored[k], 16 * EXPERTS * turns)

        n_weights = 16 * (8 + 2 * RC)

        @block.gpsimd
        def _(pool):
            make_identity(nc, pool, ident, zeroed, ident_ready)
            nc.gpsimd.memset(eps[:, :], LN_EPS).then_inc(const_set, 1)
            pool.wait_ge(w_loaded, n_weights)
            nc.gpsimd.tensor_scalar(sw2_sb[:, :, :], sw2_in[:, :, :], 2.0, None, ALU.mult).then_inc(doubled, 1)

        @block.vector
        def _(dve):
            dve.wait_ge(w_loaded, n_weights)
            nc.vector.tensor_scalar(sb2x[:, :], sb2_sb[:, :], 2.0, None, ALU.mult).then_inc(bias_steps, 1)
            nc.vector.tensor_tensor(bias2[:, :, 1:EXPERTS], b2_sb[:, :, 1:EXPERTS], b2_sb[:, :, 0:EXPERTS - 1],
                                    ALU.add).then_inc(bias_steps, 1)
            nc.vector.tensor_tensor(bias2[:, :, 0:1], b2_sb[:, :, 0:1], b2_sb[:, :, EXPERTS - 1:EXPERTS],
                                    ALU.add).then_inc(bias_steps, 1)
            dve.wait_ge(bias_steps, 3)
            nc.vector.tensor_tensor(bias[:, :, :], bias2[:, :, :], sb2x[:, :, None].to_broadcast([P, CK, EXPERTS]),
                                    ALU.add).then_inc(bias_steps, 1)
            dve.wait_ge(bias_steps, 4)

            def normalise(t, done, loaded, k):
                dve.wait_ge(x_loaded[k], loaded)
                for i in range(TILES):
                    last = nc.vector.bn_stats(stats[:, k, i, :], xg[:, k, i, :])
                last.then_inc(stats_done[k], 1)
                dve.wait_ge(stats_done[k], done)
                nc.vector.memset(spare[:, :], 0.0)
                for i in range(TILES):
                    last = nc.vector.bn_aggr(mv[:, k, i, :], stats[:, k, i, :])
                last.then_inc(mv_done[k], 1)
                dve.wait_ge(std_done[k], done)
                nc.vector.reciprocal(rstd[:, k, :], std[:, k, :]).then_inc(rstd_done[k], 1)
                dve.wait_ge(rstd_done[k], done)
                dve.wait_ge(turned[k], t)
                for i in range(TILES):
                    last = nc.vector.tensor_scalar(xn[:, k, i, :], xg[:, k, i, :], mv[:, k, i, 0:1],
                                                   rstd[:, k, i:i + 1], ALU.subtract, ALU.mult)
                last.then_inc(normed[k], 1)

            def finish(t, done, before, k):
                dve.wait_ge(down_done[k], done)
                for fc in range(CK):
                    last = nc.vector.tensor_tensor(yt[:, fc, :].rearrange("p (j n) -> p j n", n=RUN),
                                                   ps_y[:, fc, :].rearrange("p (j n) -> p j n", n=RUN),
                                                   bias[:, fc, :, None].to_broadcast([P, EXPERTS, RUN]), ALU.add)
                last.then_inc(y_out[k], 1)

            def residual(t, done, before, k):
                dve.wait_ge(back_done[k], done)
                dve.wait_ge(stored[k], before)
                nc.vector.scalar_tensor_tensor(xo[:, k, :, :], ps_t[:, :, :].rearrange("p a (b c) -> p (a b) c", c=D),
                                               0.25, xg[:, k, :, :], ALU.mult, ALU.add).then_inc(res_done[k], 1)

            def turn(t):
                done, loaded = dve.snap(t + 1), dve.snap(t * (16 * EXPERTS) + 16 * EXPERTS)
                before = dve.snap(t * (16 * EXPERTS))
                for k in range(2):
                    normalise(t, done, loaded, k)
                    if k:
                        finish(t, done, before, 0)
                        residual(t, done, before, 0)
                    dve.wait_ge(turned[k], done)
                    nc.vector.tensor_copy(xt[:, k, 1, :], ps_t[:, 1, :]).then_inc(turned_out_v[k], 1)
                    for c in range(HC):
                        dve.wait_ge(sil_done[k][c], done)
                        if c == 0:
                            dve.wait_ge(down_done[1 - k], done if k else t)
                        nc.vector.scalar_tensor_tensor(gated[:, c, :], ps_h[:, 2 * (c % 2) + 1, :], sb3_sb[:, c:c + 1],
                                                       sil[:, c % 2, :], ALU.add, ALU.mult).then_inc(gated_done[k][c], 1)
                finish(t, done, before, 1)
                residual(t, done, before, 1)

            for_turns(dve, turns, turn)

        @block.scalar
        def _(act):
            act.wait_ge(w_loaded, n_weights)
            act.wait_ge(const_set, 1)
            def turn(t):
                done = act.snap(t + 1)
                for k in range(2):
                    act.wait_ge(mv_done[k], done)
                    nc.scalar.activation(std[:, k, :], mv[:, k, :, 1], ACT.Sqrt, bias=eps[:, 0:1]).then_inc(std_done[k], 1)
                    act.wait_ge(turned[k], done)
                    nc.scalar.activation(xt[:, k, 0, :], ps_t[:, 0, :], ACT.Copy).then_inc(turned_out_a[k], 1)
                    for c in range(HC):
                        act.wait_ge(up_done[k][c], done)
                        if c >= 2:
                            act.wait_ge(gated_done[k][c - 2], done)
                        else:
                            act.wait_ge(gated_done[1 - k][c + 2], done if k else t)
                        nc.scalar.activation(sil[:, c % 2, :], ps_h[:, 2 * (c % 2), :], ACT.Silu,
                                             bias=sb1_sb[:, c:c + 1]).then_inc(sil_done[k][c], 1)
                    act.wait_ge(down_done[1 - k], done if k else t)
                    for e in range(EXPERTS):
                        act.wait_ge(eup_done[k][e], done)
                        for c in range(RC):
                            last = nc.scalar.activation(hidden[:, e, c, :], ps_h[:, e % 4, c * 2 * RUN:(c + 1) * 2 * RUN],
                                                        ACT.Gelu, bias=b1_sb[:, e, c:c + 1])
                        last.then_inc(hidden_done[k][e], 1)

            for_turns(act, turns, turn)

        @block.tensor
        def _(pe):
            pe.wait_ge(ident_ready, 1)
            pe.wait_ge(w_loaded, n_weights)
            pe.wait_ge(doubled, 1)

            def turn_in(t, done, k):
                pe.wait_ge(normed[k], done)
                pe.wait_ge(res_done[1 - k], done if k else t)
                for i in range(TILES):
                    for ck in range(CK):
                        last = nc.tensor.transpose(ps_t[:, ck, i * P:(i + 1) * P], xn[:, k, i, ck * P:(ck + 1) * P],
                                                   ident[:, :])
                last.then_inc(turned[k], 1)

            def up(t, done, k):
                pe.wait_ge(turned_out_a[k], done)
                pe.wait_ge(turned_out_v[k], done)
                for c in range(HC):
                    if c < 2:
                        for e in (4 + 2 * c, 5 + 2 * c):
                            pe.wait_ge(hidden_done[1 - k][e], done if k else t)
                    else:
                        pe.wait_ge(gated_done[k][c - 2], done)
                    for n, w in enumerate((sw1_sb, sw3_sb)):
                        for ck in range(CK):
                            last = nc.tensor.matmul(ps_h[:, 2 * (c % 2) + n, :], w[:, ck, c * P:(c + 1) * P],
                                                    xt[:, k, ck, :], start=ck == 0, stop=ck == CK - 1)
                    last.then_inc(up_done[k][c], 1)
                for e in range(EXPERTS):
                    if e < 4:
                        pe.wait_ge(gated_done[k][2 + e // 2], done)
                    else:
                        pe.wait_ge(hidden_done[k][e - 4], done)
                    for c in range(RC):
                        for ck in range(CK):
                            last = nc.tensor.matmul(ps_h[:, e % 4, c * 2 * RUN:(c + 1) * 2 * RUN],
                                                    w1_sb[:, e, ck, c * P:(c + 1) * P], pair(xt[:, k, ck, :], e),
                                                    start=ck == 0, stop=ck == CK - 1)
                    last.then_inc(eup_done[k][e], 1)

            def down(t, done, k):
                pe.wait_ge(y_out[1 - k], done if k else t)
                pe.wait_ge(gated_done[k][HC - 1], done)
                for fc in range(CK):
                    for c in range(HC):
                        nc.tensor.matmul(ps_y[:, fc, :], sw2_sb[:, c, fc * P:(fc + 1) * P], gated[:, c, :],
                                         start=c == 0, stop=False, skip_group_check=True)
                for e in range(EXPERTS):
                    pe.wait_ge(hidden_done[k][e], done)
                    for fc in range(CK):
                        for c in range(RC):
                            last = nc.tensor.matmul(pair(ps_y[:, fc, :], e), w2_sb[:, e, c, fc * P:(fc + 1) * P],
                                                    hidden[:, e, c, :], start=False,
                                                    stop=e == EXPERTS - 1 and c == RC - 1, skip_group_check=True)
                last.then_inc(down_done[k], 1)

            def turn_back(t, done, k):
                pe.wait_ge(y_out[k], done)
                for i in range(TILES):
                    for fc in range(CK):
                        last = nc.tensor.transpose(ps_t[:, i // 2, (i % 2) * D + fc * P:(i % 2) * D + (fc + 1) * P],
                                                   yt[:, fc, i * P:(i + 1) * P], ident[:, :])
                last.then_inc(back_done[k], 1)

            def turn(t):
                done = pe.snap(t + 1)
                turn_in(t, done, 0)
                up(t, done, 0)
                down(t, done, 0)
                turn_back(t, done, 0)
                turn_in(t, done, 1)
                up(t, done, 1)
                down(t, done, 1)
                turn_back(t, done, 1)

            for_turns(pe, turns, turn)


def window_stage(nc, name, x, out, qk, v, wo_t, bo):
    turns = NTOK // GROUP // 2
    HG = 4
    PER_TILE = H // HG
    ITEMS = 2 * TILES * PER_TILE
    HALF = P // 2
    WIN = GROUP // HALF
    KEYS = GROUP + WINDOW
    VW = 32
    with Stage(nc, name) as s:
        ident, zeroed, ident_ready = s.sb("ident", [P, P]), s.sem("zeroed"), s.sem("ident_ready")
        identb, zeroedb = s.sb("identb", [P, P], BF16), s.sem("zeroedb")
        mask = s.sb("mask", [P, HG, P], BF16)
        mask_steps = s.sem("mask_steps")
        wo_sb, bo_sb = s.sb("wo", [P, CK, D]), s.sb("bo", [P, D])
        w_loaded = s.sem("w_loaded")
        qs = s.sb("qs", [STACK, 2, H, GROUP], BF16)
        ks = s.sb("ks", [STACK, 2, H, KEYS], BF16)
        vin = s.sb("vin", [P, 2, WIN, D])
        vp = s.sb("vp", [P, 2, WIN, H, VW])
        xg = s.sb("xg", [P, 2, TILES, D])
        xb = s.sb("xb", [P, 2, TILES, D])
        sc = s.sb("sc", [P, 2, HG, P])
        pr = s.sb("pr", [P, 2, HG, P])
        pt = s.sb("pt", [P, 2, HG, P])
        ot = s.sb("ot", [P, 2, P])
        top = s.sb("top", [P, 2, HG])
        rden = s.sb("rden", [P, 2, HG])
        att = s.sb("att", [P, 2, D])
        attt = s.sb("attt", [P, CK, P])
        xo = s.sb("xo", [P, 2, D])
        ps_s = s.ps("ps_s", [P, 2, HG, P])
        ps_p = s.ps("ps_p", [P, 2, HG, P])
        ps_o = s.ps("ps_o", [P, GROUP])
        ps_b = s.ps("ps_b", [P, GROUP])
        ps_w = s.ps("ps_w", [P, GROUP])
        ps_y = s.ps("ps_y", [P, GROUP])
        qk_loaded, v_loaded, x_loaded = (s.sems(n, 2) for n in ("qk_loaded", "v_loaded", "x_loaded"))
        v_ready, xb_ready = (s.sems(n, 2) for n in ("v_ready", "xb_ready"))
        vset = s.sem("vset")
        (scored, topped, less_top, expd, p_turned, p_out, pv_done, o_out, o_back, inverted, att_done) = (
            s.sem(n) for n in ("scored", "topped", "less_top", "expd", "p_turned", "p_out", "pv_done", "o_out",
                               "o_back", "inverted", "att_done"))
        w_turned, w_out, w_done, x_out = (s.sem(n) for n in ("w_turned", "w_out", "w_done", "x_out"))
        x_stored = s.sems("x_stored", 2)
        block = s.block()
        xv = x.rearrange("(u k i p) c -> u k p i c", p=P, i=TILES, k=2)
        ov = out.rearrange("(u k i p) c -> u k p i c", p=P, i=TILES, k=2)
        TT = 2 * TILES

        def u_batch(u):
            return u // 2

        def u_col(u):
            return (u % 2) * (2 * GROUP)

        @block.sync
        def _(sp):
            sp.dma_start(wo_sb[:, :, :], wo_t.rearrange("(k p) f -> p k f", p=P)).then_inc(w_loaded, 16)
            sp.dma_start(bo_sb[:, :], bass.AP(bo.tensor, bo.offset, [[0, P], [1, D]])).then_inc(w_loaded, 16)

            def load_q_k_x(k, u):
                batch, col = u_batch(u), u_col(u)
                for n in range(len(LEFT)):
                    sp.dma_start(qs[n * DH:(n + 1) * DH, k, :, :],
                                 qk[0, LEFT[n], :, batch, bass.ds(col + (PAD + k * GROUP), GROUP)]
                                 .rearrange("(h d) c -> d h c", d=DH)).then_inc(qk_loaded[k], 16)
                    sp.dma_start(ks[n * DH:(n + 1) * DH, k, :, :],
                                 qk[1, RIGHT[n], :, batch, bass.ds(col + k * GROUP, KEYS)]
                                 .rearrange("(h d) c -> d h c", d=DH)).then_inc(qk_loaded[k], 16)
                sp.dma_start(xg[:, k, :, :], xv[u, k, :, :, :]).then_inc(x_loaded[k], 16)

            def load_v(k, u):
                batch, col = u_batch(u), u_col(u)
                for odd in range(2):
                    sp.dma_start(vin[:, k, odd::2, :],
                                 v[batch, bass.ds(col + (k * GROUP + odd * HALF), GROUP), :]
                                 .rearrange("(w p) c -> p w c", p=P)).then_inc(v_loaded[k], 16)

            for k in range(2):
                load_q_k_x(k, 0)
                load_v(k, 0)

            def turn(t, last):
                tiles_out = [sp.snap(t * TT + i + 1) for i in range(TT)]
                done = sp.snap(t + 1)
                ahead = None if last else sp.snap(t + 1)
                for i in range(TT):
                    sp.wait_ge(x_out, tiles_out[i])
                    sp.dma_start(ov[t, i // TILES, :, i % TILES, :], xo[:, i % 2, :])\
                        .then_inc(x_stored[i % 2], 16)
                    if i % TILES == TILES - 1 and not last:
                        k = i // TILES
                        sp.wait_ge(v_ready[k], done)
                        load_q_k_x(k, ahead)
                        load_v(k, ahead)

            turn(0, False)
            with sp.Fori(1, turns - 1) as t:
                turn(t, False)
            turn(turns - 1, True)
            for slot in range(2):
                sp.wait_ge(x_stored[slot], 16 * turns * TILES)

        @block.gpsimd
        def _(pool):
            make_identity(nc, pool, ident, zeroed, ident_ready)
            make_identity(nc, pool, identb, zeroedb, ident_ready)
            nc.gpsimd.memset(mask[:, :, :], 0.0).then_inc(mask_steps, 1)
            nc.gpsimd.memset(vp[:, :, :, :, :], 0.0).then_inc(vset, 1)
            pool.wait_ge(vset, 1)
            step = 1
            for half in range(2):
                for base, sign in ((0, 1), (WINDOW - 1, -1)):
                    m = mask[half * HALF:(half + 1) * HALF, :, :]
                    pool.wait_ge(mask_steps, step)
                    nc.gpsimd.affine_select(out=m, in_=m, compare_op=ALU.is_ge, fill=MASKED, base=base,
                                            pattern=[[0, HG], [sign, P]], channel_multiplier=-sign)\
                        .then_inc(mask_steps, 1)
                    step += 1
            pool.wait_ge(mask_steps, step)
            nc.gpsimd.memset(vp[:, :, :, :, DH:DH + 1], 1.0).then_inc(vset, 1)
            pool.wait_ge(w_loaded, 32)
            def turn(t):
                tiles, done, loaded, loaded_v = (pool.snap(t * TT), pool.snap(t + 1), pool.snap(t * 16 + 16),
                                                 pool.snap(t * 32 + 32))
                for k in range(2):
                    pool.wait_ge(x_out, tiles)
                    pool.wait_ge(v_loaded[k], loaded_v)
                    pool.wait_ge(x_loaded[k], loaded)
                    nc.gpsimd.tensor_tensor(xb[:, k, :, :], xg[:, k, :, :],
                                            bo_sb[:, None, :].to_broadcast([P, TILES, D]), ALU.add)\
                        .then_inc(xb_ready[k], 1)
                    nc.gpsimd.tensor_copy(vp[:, k, :, :, 0:DH], vin[:, k, :, :].rearrange("p w (h d) -> p w h d", d=DH))\
                        .then_inc(v_ready[k], 1)

            for_turns(pool, turns, turn)

        def steps(lags, tile_lags):
            for n in range(ITEMS + 8):
                for what, lag in lags:
                    if 0 <= n - lag < ITEMS:
                        yield what, n - lag
                for what, lag in tile_lags:
                    m = n - lag
                    if 0 <= m < ITEMS and m % PER_TILE == PER_TILE - 1:
                        yield what, m // PER_TILE

        @block.vector
        def _(dve):
            def turn(t):
                base, tbase, done = dve.snap(t * ITEMS), dve.snap(t * TT), dve.snap(t + 1)
                sbase = dve.snap(t * (16 * TILES))

                def maximum(n):
                    dve.wait_ge(scored, base + n + 1)
                    nc.vector.tensor_reduce(top[:, n % 2, :], ps_s[:, n % 2, :, :], AX.X, ALU.max).then_inc(topped, 1)
                    dve.wait_ge(topped, base + n + 1)
                    if n >= 2:
                        dve.wait_ge(expd, base + n - 1)
                    nc.vector.tensor_tensor(sc[:, n % 2, :, :], ps_s[:, n % 2, :, :],
                                            top[:, n % 2, :, None].to_broadcast([P, HG, P]), ALU.subtract)\
                        .then_inc(less_top, 1)

                def weigh(n):
                    i, hg = n // PER_TILE, n % PER_TILE
                    view = ps_b[:, 0:P].rearrange("p (h d) -> p h d", d=VW)
                    dve.wait_ge(o_back, base + n + 1)
                    nc.vector.reciprocal(rden[:, n % 2, :], view[:, :, DH]).then_inc(inverted, 1)
                    dve.wait_ge(inverted, base + n + 1)
                    if hg == 0 and i >= 2:
                        dve.wait_ge(w_turned, tbase + i - 1)
                    nc.vector.tensor_tensor(att[:, i % 2, hg * HG * DH:(hg + 1) * HG * DH]
                                            .rearrange("p (h d) -> p h d", d=DH), view[:, :, 0:DH],
                                            rden[:, n % 2, :, None].to_broadcast([P, HG, DH]), ALU.mult)\
                        .then_inc(att_done, 1)

                def add_x(i):
                    dve.wait_ge(w_done, tbase + i + 1)
                    dve.wait_ge(xb_ready[i // TILES], done)
                    dve.wait_ge(x_stored[i % 2], sbase + 16 * (i // 2))
                    nc.vector.tensor_tensor(xo[:, i % 2, :], ps_y[:, 0:D], xb[:, i // TILES, i % TILES, :], ALU.add)\
                        .then_inc(x_out, 1)

                todo = {"max": maximum, "weigh": weigh, "add": add_x}
                for what, n in steps((("max", 0), ("weigh", 4)), (("add", 6),)):
                    todo[what](n)

            for_turns(dve, turns, turn)

        @block.scalar
        def _(act):
            def turn(t):
                base, tbase = act.snap(t * ITEMS), act.snap(t * TT)

                def exp(n):
                    act.wait_ge(less_top, base + n + 1)
                    if n >= 2:
                        act.wait_ge(p_turned, base + n - 1)
                    nc.scalar.activation(pr[:, n % 2, :, :], sc[:, n % 2, :, :], ACT.Exp)\
                        .then_inc(expd, 1)

                def copy_p(n):
                    act.wait_ge(p_turned, base + n + 1)
                    if n >= 2:
                        act.wait_ge(pv_done, base + n - 1)
                    nc.scalar.activation(pt[:, n % 2, :, :], ps_p[:, n % 2, :, :], ACT.Copy).then_inc(p_out, 1)

                def copy_o(n):
                    act.wait_ge(pv_done, base + n + 1)
                    if n >= 2:
                        act.wait_ge(o_back, base + n - 1)
                    nc.scalar.activation(ot[:, n % 2, :], ps_o[:, 0:P], ACT.Copy).then_inc(o_out, 1)

                def copy_att(i):
                    act.wait_ge(w_turned, tbase + i + 1)
                    act.wait_ge(w_done, tbase + i)
                    nc.scalar.activation(attt[:, :, :], ps_w[:, 0:D].rearrange("p (k q) -> p k q", k=CK), ACT.Copy)\
                        .then_inc(w_out, 1)

                todo = {"exp": exp, "copy_p": copy_p, "copy_o": copy_o, "copy_att": copy_att}
                for what, n in steps((("exp", 0), ("copy_p", 2), ("copy_o", 3)), (("copy_att", 5),)):
                    todo[what](n)

            for_turns(act, turns, turn)

        @block.tensor
        def _(pe):
            pe.wait_ge(ident_ready, 2)
            pe.wait_ge(mask_steps, 5)
            pe.wait_ge(vset, 2)
            pe.wait_ge(w_loaded, 32)
            def turn(t):
                base, tbase, done = pe.snap(t * ITEMS), pe.snap(t * TT), pe.snap(t + 1)
                n_qk = 16 * 2 * len(LEFT)
                qk_here = pe.snap(t * n_qk + n_qk)

                def score(n):
                    i, hg = n // PER_TILE, n % PER_TILE
                    k = i // TILES
                    if n % (TILES * PER_TILE) == 0:
                        pe.wait_ge(qk_loaded[k], qk_here)
                    if n >= 2:
                        pe.wait_ge(less_top, base + n - 1)
                    nc.tensor.matmul(ps_s[:, n % 2, :, :], identb[:, :], mask[:, :, :], start=True, stop=False,
                                     skip_group_check=True)
                    for h in range(HG):
                        for half in range(2):
                            q0 = (i % TILES) * P + half * HALF
                            last = nc.tensor.matmul(ps_s[half * HALF:(half + 1) * HALF, n % 2, h, :],
                                                    qs[:, k, hg * HG + h, q0:q0 + HALF],
                                                    ks[:, k, hg * HG + h, q0:q0 + P],
                                                    start=False, stop=h == HG - 1, skip_group_check=True)
                    last.then_inc(scored, 1)

                def turn_p(n):
                    pe.wait_ge(expd, base + n + 1)
                    if n >= 2:
                        pe.wait_ge(p_out, base + n - 1)
                    for h in range(HG):
                        last = nc.tensor.transpose(ps_p[:, n % 2, h, :], pr[:, n % 2, h, :], ident[:, :])
                    last.then_inc(p_turned, 1)

                def weigh_v(n):
                    i, hg = n // PER_TILE, n % PER_TILE
                    k = i // TILES
                    pe.wait_ge(p_out, base + n + 1)
                    if n % (TILES * PER_TILE) == 0:
                        pe.wait_ge(v_ready[k], done)
                    pe.wait_ge(o_out, base + n)
                    for half in range(2):
                        for h in range(HG):
                            last = nc.tensor.matmul(ps_o[h * VW:(h + 1) * VW, half * HALF:(half + 1) * HALF],
                                                    vp[:, k, 2 * (i % TILES) + half, hg * HG + h, :],
                                                    pt[:, n % 2, h, half * HALF:(half + 1) * HALF],
                                                    start=True, stop=True)
                    last.then_inc(pv_done, 1)

                def turn_o(n):
                    pe.wait_ge(o_out, base + n + 1)
                    pe.wait_ge(att_done, base + n)
                    nc.tensor.transpose(ps_b[:, 0:P], ot[:, n % 2, :], ident[:, :]).then_inc(o_back, 1)

                def turn_att(i):
                    pe.wait_ge(att_done, base + (i + 1) * PER_TILE)
                    pe.wait_ge(w_out, tbase + i)
                    for ck in range(CK):
                        last = nc.tensor.transpose(ps_w[:, ck * P:(ck + 1) * P], att[:, i % 2, ck * P:(ck + 1) * P],
                                                   ident[:, :])
                    last.then_inc(w_turned, 1)

                def project(i):
                    pe.wait_ge(w_out, tbase + i + 1)
                    pe.wait_ge(x_out, tbase + i)
                    for ck in range(CK):
                        last = nc.tensor.matmul(ps_y[:, 0:D], attt[:, ck, :], wo_sb[:, ck, :],
                                                start=ck == 0, stop=ck == CK - 1)
                    last.then_inc(w_done, 1)

                todo = {"score": score, "turn_p": turn_p, "weigh_v": weigh_v, "turn_o": turn_o,
                        "turn_att": turn_att, "project": project}
                for what, n in steps((("score", 0), ("turn_p", 2), ("weigh_v", 3), ("turn_o", 4)),
                                     (("turn_att", 5), ("project", 6))):
                    todo[what](n)

            for_turns(pe, turns, turn)


LAGS = dict(relate=-7, shift=-6, exp=1, store=2, turn=3, load=3, turn_w=6,
            split=1, spread=2, far=3, weigh=5, copy_o=9, turn_o=11, combine=11)

SHARED_AT = 1
VECTOR_TURNED = (0, 1, 2, 3, 4, 5, 6, 7)
VECTOR_W = (1, 2, 3, 4, 5, 6)
VECTOR_O = (0, 4)


def causal_stage(nc, name, att, qk, v, pek, pev, bias_rows, prob_rows):
    NEAR = 3 * P
    DV = DH + 1
    UNITS_HEAD = L // P
    HEADS = 2
    UNITS = HEADS * UNITS_HEAD
    turns = B * H // HEADS
    SLOTS = 8
    GPH = UNITS_HEAD // 4
    GROUPS = UNITS // 4
    CT = 32
    MAX_ROW = STACK
    ROWS = STACK + 3
    LEAD, TAIL = -LAGS["relate"], LAGS["combine"] + 3

    def far_chunks(i):
        keys = max(0, (i - 2) * P)
        return [(c, min(GROUP, keys - c)) for c in range(0, keys, GROUP)]

    def far_blocks(gi):
        return [(b, max(0, b - 4 * gi + 3) * P) for b in range(4 * gi + 1)]

    def quarter(items, s):
        return items[len(items) * s // 4:len(items) * (s + 1) // 4]

    S_BANKS, F_BANKS = 3, 2
    score_at, far_at, S_USES, F_USES = {}, {}, [0] * S_BANKS, [0] * F_BANKS
    for m in range(UNITS):
        for c in range(len(far_chunks(m % UNITS_HEAD)) + 1):
            bank = sum(S_USES) % S_BANKS
            score_at[m, c] = bank, S_USES[bank]
            S_USES[bank] += 1
    for g in range(GROUPS):
        for b, _ in far_blocks(g % GPH):
            bank = sum(F_USES) % F_BANKS
            far_at[g, b] = bank, F_USES[bank]
            F_USES[bank] += 1
    PT_AT = [sum(4 * j + 4 for j in range(gi)) for gi in range(GPH + 1)]

    def use(t, m):
        return t * (UNITS // SLOTS) + (m // SLOTS + 1)

    def units(t, m):
        return (t + m // UNITS) * UNITS + (m % UNITS + 1)

    def groups(t, g):
        return (t + g // GROUPS) * GROUPS + (g % GROUPS + 1)

    def head_of(g):
        return (g // GPH) % HEADS

    def head_turns(t, g):
        return t + g // GROUPS

    def group_count(t, g):
        return head_turns(t, g) * GPH + (g % GPH + 1)

    def score_bank(t, m, c):
        bank, n = score_at[m % UNITS, c]
        return bank, (t + m // UNITS) * S_USES[bank] + (n + 1)

    def far_bank(t, g, b):
        bank, n = far_at[g % GROUPS, b]
        return bank, (t + g // GROUPS) * F_USES[bank] + (n + 1)

    def emit(engine, steps):
        def turn(t, first, last):
            for n in range(-LEAD if first else 0, UNITS + (TAIL if last else 0)):
                steps(t, n, lambda m: (m >= 0 or not first) and (m < UNITS or not last))
        turn(0, True, False)
        with engine.Fori(1, turns - 1) as t:
            turn(t, False, False)
        turn(turns - 1, False, True)

    def group_at(n, what, valid, part=0):
        m = n - LAGS[what] - part
        return m // 4 if m % 4 == 3 and valid(m) else None

    with Stage(nc, name) as s:
        ident, zeroed, ident_ready = s.sb("ident", [P, P]), s.sem("zeroed"), s.sem("ident_ready")
        ident_b = s.sb("ident_b", [P, P], BF16)
        pek_in, pev_in = s.sb("pek_in", [P, 2, DH]), s.sb("pev_in", [P, 2, DH])
        pek0, pev0 = s.sb("pek0", [P, DH]), s.sb("pev0", [P, DH])
        pek_d, pev_d = s.sb("pek_d", [P, 2, DH]), s.sb("pev_d", [P, 2, DV])
        pek_parts, pek_rest = s.sb("pek_parts", [DH, 3, MAX_REL], BF16), s.sb("pek_rest", [DH, MAX_REL])
        pek_s = s.sb("pek_s", [STACK, MAX_REL], BF16)
        edge0, edge1 = s.sb("edge0", [P, P]), s.sb("edge1", [P, P])
        spare = s.sb("spare", [P, 1])
        qs, ks = s.sb("qs", [ROWS, HEADS, L], BF16), s.sb("ks", [ROWS, HEADS, L], BF16)
        vh = s.sb("vh", [P, HEADS, UNITS_HEAD, DV])
        r_sb = s.sb("r_sb", [P, SLOTS, MAX_REL])
        bias = s.sb("bias", [P, SLOTS, NEAR])
        p = s.sb("p", [P, SLOTS, NEAR])
        w = s.sb("w", [P, SLOTS, MAX_REL])
        top = s.sb("top", [P, 2, 5])
        negtop = s.sb("negtop", [P, SLOTS])
        neg_parts, neg_rest = s.sb("neg_parts", [P, 2, 4, 3], BF16), s.sb("neg_rest", [P, 4])
        rden = s.sb("rden", [P, 2, 4])
        pt = s.sb("pt", [P, PT_AT[GPH], GROUP])
        wt = s.sb("wt", [P, GPH, 2, GROUP])
        ot = s.sb("ot", [P, GROUP])
        osum = s.sb("osum", [P, 2, 4, DV])
        oh = s.sb("oh", [P, HEADS, UNITS_HEAD, DH])
        ps_rw = s.ps("ps_rw", [P, 2, MAX_REL])
        ps_s = s.ps("ps_s", [P, S_BANKS, GROUP])
        ps_f = s.ps("ps_f", [P, F_BANKS, GROUP])
        ps_p = s.ps("ps_p", [P, GROUP])
        ps_o = s.ps("ps_o", [P, GROUP])

        c_loaded, setup, pek_turned, edges_set, edges_stored, stacked = (
            s.sem(n) for n in ("c_loaded", "setup", "pek_turned", "edges_set", "edges_stored", "stacked"))
        q_loaded, k_loaded, v_loaded, head_stored = (s.sems(n, HEADS) for n in ("q_loaded", "k_loaded", "v_loaded", "head_stored"))
        r_out, r_stored, bias_loaded, expd, p_stored, w_loaded = (
            s.sems(n, SLOTS) for n in ("r_out", "r_stored", "bias_loaded", "expd", "p_stored", "w_loaded"))
        scored, score_out = s.sems("scored", S_BANKS), s.sems("score_out", S_BANKS)
        far_done, far_out = s.sems("far_done", F_BANKS), s.sems("far_out", F_BANKS)
        w_turned = s.sems("w_turned", SLOTS)
        pv_done, o_done = s.sems("pv_done", HEADS), s.sems("o_done", HEADS)
        (r_done, neg_done, neg_split, spread_done, spread_out, turned, turned_out, w_out, o_out, o_back, o_summed,
         inverted) = (s.sem(n) for n in ("r_done", "neg_done", "neg_split", "spread_done", "spread_out", "turned",
                                         "turned_out", "w_out", "o_out", "o_back", "o_summed", "inverted"))
        att_v = att.rearrange("(b i p) (h d) -> b p i h d", b=B, p=P, d=DH)
        passed = s.sem("passed")
        LEFT_RUNS = ((0, 0, 3, 0), (3, 1, 2, 0), (5, 2, 1, 0))
        RIGHT_RUNS = ((0, 0, 3, 1), (3, 0, 2, 1), (5, 0, 1, 1))
        SIDE_DMAS = len(LEFT_RUNS)
        part_pitch = D * B * L
        block = s.block()

        def group_read(engine, t, g, valid):
            if valid(4 * (g - GPH)):
                engine.wait_ge(pv_done[head_of(g - GPH)], group_count(t, g - GPH))

        def copy_turned(engine, copy, t, m, valid):
            i, g = m % UNITS_HEAD, m // 4
            blocks = min(i + 1, 3)
            group_read(engine, t, g, valid)
            engine.wait_ge(turned, units(t, m))
            b0 = PT_AT[g % GPH] + i + 1 - blocks
            copy(pt[:, b0:b0 + blocks, (i % 4) * P:(i % 4 + 1) * P], ps_p[:, 0:blocks * P].rearrange("p (b q) -> p b q", q=P))\
                .then_inc(turned_out, 1)

        def copy_w(engine, copy, t, m, valid):
            g = m // 4
            group_read(engine, t, g, valid)
            copy(wt[:, g % GPH, :, (m % 4) * P:(m % 4 + 1) * P], ps_rw[:, 1, :].rearrange("p (k q) -> p k q", k=2))\
                .then_inc(w_out, 1)

        def copy_o(engine, copy, t, g):
            engine.wait_ge(pv_done[head_of(g)], group_count(t, g))
            copy(ot[:, :], ps_o[:, :]).then_inc(o_out, 1)

        @block.sync
        def _(sp):
            sp.dma_start(pek_in[:, :, :], pek[1:1 + MAX_REL, :].rearrange("(k p) d -> p k d", p=P)).then_inc(c_loaded, 16)
            sp.dma_start(pev_in[:, :, :], pev[1:1 + MAX_REL, :].rearrange("(k p) d -> p k d", p=P)).then_inc(c_loaded, 16)
            sp.dma_start(pek0[:, :], bass.AP(pek.tensor, pek.offset, [[0, P], [1, DH]])).then_inc(c_loaded, 16)
            sp.dma_start(pev0[:, :], bass.AP(pev.tensor, pev.offset, [[0, P], [1, DH]])).then_inc(c_loaded, 16)

            def load_v(k, batch, h):
                sp.dma_start(vh[:, k, :, :], v[batch, h, :, :, :]).then_inc(v_loaded[k], 16)

            def load_rows(part, k, batch, h):
                to, (n, first, copies, step) = (qs, ks)[part // 3], (LEFT_RUNS + RIGHT_RUNS)[part]
                src = qk[part // 3, first, bass.ds(h * DH, DH), batch, :]
                sp.dma_start(to[n * DH:(n + copies) * DH, k, :],
                             bass.AP(src.tensor, src.offset, [[step * part_pitch, copies], list(src.ap[0]), [1, L]]))\
                    .then_inc((q_loaded if part < 3 else k_loaded)[k], 16)

            for k in range(HEADS):
                for part in range(6):
                    load_rows(part, k, 0, k)
                load_v(k, 0, k)
            sp.wait_ge(edges_set, 2)
            for slot in range(SLOTS):
                sp.dma_start(bias_rows[slot, :, 0:P], edge0[:, :]).then_inc(edges_stored, 16)
                sp.dma_start(bias_rows[slot, :, NEAR:NEAR + P], edge1[:, :]).then_inc(edges_stored, 16)
            sp.wait_ge(setup, 5)
            for n in range(len(LEFT)):
                sp.dma_start(pek_s[n * DH:(n + 1) * DH, :], pek_parts[:, RIGHT[n], :]).then_inc(stacked, 16)
            sp.wait_ge(edges_stored, 16 * 2 * SLOTS)

            def turn(t, first, last):
                low, high = (0 if first else -3), UNITS // SLOTS + 3
                cnt = {j: t * (UNITS // SLOTS) + j for j in range(low, high)}
                cnt16 = {j: t * (16 * UNITS // SLOTS) + 16 * j for j in range(low, high)}

                def wait_both(*pairs):
                    values = [v if isinstance(v, int) else sp.to_reg(v) for _, v in pairs]
                    for (what, _), value in zip(pairs, values):
                        sp.wait_ge(what, value)

                nxt = None if last else sp.snap(t + 1)
                if not last:
                    batch_n, head_n = sp.snap(nxt // (H // HEADS)), sp.snap((nxt % (H // HEADS)) * HEADS)
                batch, head = sp.snap(t // (H // HEADS)), sp.snap((t % (H // HEADS)) * HEADS)

                def store_r(m):
                    sl, j = m % SLOTS, m // SLOTS
                    reused = not (first and m < SLOTS)
                    wait_both((r_out[sl], cnt[j + 1]), *[(bias_loaded[sl], cnt16[j])] * reused)
                    sp.dma_start(bias_rows[sl, :, P:P + MAX_REL], r_sb[:, sl, :]).then_inc(r_stored[sl], 16)

                def load_bias(m):
                    sl, j, i = m % SLOTS, m // SLOTS, m % UNITS_HEAD
                    skip = NEAR - min(i + 1, 3) * P
                    rows = bias_rows[sl, :, :]
                    reused = not (first and m < SLOTS)
                    wait_both((r_stored[sl], cnt16[j + 1]), *[(expd[sl], cnt[j])] * reused)
                    sp.dma_start(bias[:, sl, skip:], bass.AP(rows.tensor, rows.offset + P - 1 + skip,
                                                            [[4 * P - 1, P], [1, NEAR - skip]])).then_inc(bias_loaded[sl], 16)

                def store_p(m):
                    sl, j, i = m % SLOTS, m // SLOTS, m % UNITS_HEAD
                    reused = not (first and m < SLOTS)
                    wait_both((expd[sl], cnt[j + 1]), *[(w_loaded[sl], cnt16[j])] * reused)
                    sp.dma_start(prob_rows[sl, :, :], p[:, sl, :]).then_inc(p_stored[sl], 16)

                def load_w(m):
                    sl, j = m % SLOTS, m // SLOTS
                    rows = prob_rows[sl, :, :]
                    reused = not (first and m < SLOTS)
                    wait_both((p_stored[sl], cnt16[j + 1]), *[(w_turned[sl], cnt[j])] * reused)
                    sp.dma_start(w[:, sl, :], bass.AP(rows.tensor, rows.offset + 1, [[NEAR + 1, P], [1, MAX_REL]]))\
                        .then_inc(w_loaded[sl], 16)

                todo = {"store_r": store_r, "load_bias": load_bias, "store_p": store_p, "load_w": load_w}

                def head_over(m):
                    k = (m // UNITS_HEAD) % HEADS
                    prev = m < 0
                    wait_both((o_done[k], head_groups[0 if prev else 1]))
                    sp.sem_inc(passed, 1)
                    bb, hh = (batch_p, head_p) if prev else (batch, head)
                    sp.dma_start(att_v[bb, :, :, hh + k, :], oh[:, k, :, :]).then_inc(head_stored[k], 16)

                head_groups = {0: sp.snap(t * GPH), 1: sp.snap(t * GPH + GPH)}
                if not first:
                    batch_p = sp.snap((t - 1) // (H // HEADS))
                    head_p = sp.snap(((t - 1) % (H // HEADS)) * HEADS)
                for n in range(-LEAD if first else 0, UNITS + (TAIL + 3 if last else 0)):
                    for what, step in (("store_r", "relate"), ("load_bias", "shift"), ("store_p", "store"), ("load_w", "load")):
                        m = n - LAGS[step]
                        if (m >= 0 or not first) and (m < UNITS or not last):
                            todo[what](m)
                    m = n - LAGS["combine"] - 2
                    if m % UNITS_HEAD == UNITS_HEAD - 1 and (m >= 0 or not first) and (m < UNITS or not last):
                        head_over(m)
                    for part in range(4):
                        m = n - LAGS["far"] - 4 - part
                        if m % UNITS_HEAD == UNITS_HEAD - 1 and ((0 <= m < UNITS and not last) or (m < 0 and not first)):
                            prev = m < 0
                            k = HEADS - 1 if prev else m // UNITS_HEAD
                            if part == 0:
                                over = []
                                for b in (4 * (GPH - 1) - 1, 4 * (GPH - 1)):
                                    bank, place = far_at[k * GPH + GPH - 1, b]
                                    over.append((far_done[bank], (t - 1 if prev else t) * F_USES[bank] + (place + 1)))
                                wait_both(*over)
                                sp.sem_inc(passed, 1)
                            for x in ((0, 1, 2), (3,), (4,), (5,))[part]:
                                load_rows(x, k, *((batch, head + k) if prev else (batch_n, head_n + k)))
                    m = n - LAGS["weigh"] - 4
                    if m % UNITS_HEAD == UNITS_HEAD - 1 and ((0 <= m < UNITS and not last) or (m < 0 and not first)):
                        prev = m < 0
                        k = HEADS - 1 if prev else m // UNITS_HEAD
                        wait_both((pv_done[k], head_groups[0 if prev else 1]))
                        sp.sem_inc(passed, 1)
                        load_v(k, *((batch, head + k) if prev else (batch_n, head_n + k)))

            turn(0, True, False)
            with sp.Fori(1, turns - 1) as t:
                turn(t, False, False)
            turn(turns - 1, False, True)
            for k in range(HEADS):
                sp.wait_ge(head_stored[k], 16 * turns)

        @block.gpsimd
        def _(pool):
            make_identity(nc, pool, ident, zeroed, ident_ready)
            nc.gpsimd.memset(edge0[:, :], 0.0).then_inc(edges_set, 1)
            nc.gpsimd.memset(edge1[:, :], MASKED).then_inc(edges_set, 1)

        @block.vector
        def _(dve):
            nc.vector.memset(ps_o[:, :], 0.0)
            nc.vector.memset(ks[MAX_ROW:ROWS, :, :], 1.0)
            dve.wait_ge(ident_ready, 1)
            nc.vector.tensor_copy(ident_b[:, :], ident[:, :]).then_inc(ident_ready, 1)
            nc.vector.memset(pev_d[:, :, DH:DV], 0.0)
            dve.wait_ge(c_loaded, 64)
            nc.vector.tensor_tensor(pek_d[:, :, :], pek_in[:, :, :], pek0[:, None, :].to_broadcast([P, 2, DH]),
                                    ALU.subtract).then_inc(setup, 1)
            nc.vector.tensor_tensor(pev_d[:, :, 0:DH], pev_in[:, :, :], pev0[:, None, :].to_broadcast([P, 2, DH]),
                                    ALU.subtract).then_inc(setup, 1)
            dve.wait_ge(pek_turned, 1)
            nc.vector.tensor_copy(pek_parts[:, 0, :], ps_rw[0:DH, 0, :]).then_inc(setup, 1)
            dve.wait_ge(setup, 3)
            nc.vector.tensor_tensor(pek_rest[:, :], ps_rw[0:DH, 0, :], pek_parts[:, 0, :], ALU.subtract).then_inc(pek_turned, 1)
            dve.wait_ge(pek_turned, 2)
            nc.vector.tensor_copy(pek_parts[:, 1, :], pek_rest[:, :]).then_inc(setup, 1)
            dve.wait_ge(setup, 4)
            nc.vector.tensor_tensor(pek_parts[:, 2, :], pek_rest[:, :], pek_parts[:, 1, :], ALU.subtract).then_inc(setup, 1)

            def score_chunk(t, m, c, valid):
                sl, i = m % SLOTS, m % UNITS_HEAD
                far = far_chunks(i)
                bank, count = score_bank(t, m, c)
                if c < len(far):
                    dve.wait_ge(scored[bank], count)
                    nc.vector.tensor_reduce(top[:, m % 2, c:c + 1], ps_s[:, bank, 0:far[c][1]], AX.X, ALU.max)\
                        .then_inc(score_out[bank], 1)
                    return
                keys = min(i + 1, 3) * P
                before = m - SLOTS
                if valid(before):
                    dve.wait_ge(turned, units(t, before))
                    dve.wait_ge(p_stored[sl], 16 * use(t, before))
                if keys < NEAR:
                    nc.vector.memset(p[:, sl, 0:NEAR - keys], 0.0)
                dve.wait_ge(bias_loaded[sl], 16 * use(t, m))
                dve.wait_ge(scored[bank], count)
                nc.vector.memset(spare[:, :], 0.0)
                nc.vector.tensor_tensor_reduce(out=p[:, sl, NEAR - keys:NEAR], in0=ps_s[:, bank, 0:keys],
                                               in1=bias[:, sl, NEAR - keys:NEAR], scale=1.0, scalar=-3e38,
                                               op0=ALU.add, op1=ALU.max, accum_out=top[:, m % 2, c:c + 1])\
                    .then_inc(score_out[bank], 1)
                dve.wait_ge(score_out[bank], count)
                nc.vector.tensor_reduce(negtop[:, sl:sl + 1], top[:, m % 2, 0:c + 1], AX.X, ALU.max, negate=True)\
                    .then_inc(neg_done, 1)

            def split_max(t, g, step, valid):
                neg = negtop[:, 4 * (g % 2):4 * (g % 2) + 4]
                part = lambda n: neg_parts[:, g % 2, :, n]
                if step == 0:
                    dve.wait_ge(neg_done, units(t, 4 * g + 3))
                    if valid(4 * (g - 2)):
                        dve.wait_ge(spread_done, groups(t, g - 2))
                    nc.vector.tensor_copy(part(0), neg).then_inc(neg_split, 1)
                    return
                dve.wait_ge(neg_split, head_turns(t, g) * (4 * GROUPS) + (4 * (g % GROUPS) + step))
                if step == 1:
                    nc.vector.tensor_tensor(neg_rest[:, :], neg, part(0), ALU.subtract).then_inc(neg_split, 1)
                elif step == 2:
                    nc.vector.tensor_copy(part(1), neg_rest[:, :]).then_inc(neg_split, 1)
                else:
                    nc.vector.tensor_tensor(part(2), neg_rest[:, :], part(1), ALU.subtract).then_inc(neg_split, 1)

            def combine(t, g):
                k, gi = head_of(g), g % GPH
                tiles = 3 if gi == 0 else 4
                dve.wait_ge(o_back, groups(t, g))
                view = ps_p[:, :].rearrange("p (i c x) -> p i x c", i=4, x=CT)[:, :, 0:DV, 0:tiles]
                nc.vector.tensor_reduce(osum[:, g % 2, :, :], view, AX.X, ALU.add).then_inc(o_summed, 1)
                dve.wait_ge(o_summed, groups(t, g))
                nc.vector.reciprocal(rden[:, g % 2, :], osum[:, g % 2, :, DH]).then_inc(inverted, 1)
                dve.wait_ge(inverted, groups(t, g))
                if gi == 0:
                    dve.wait_ge(head_stored[k], 16 * head_turns(t, g))
                nc.vector.tensor_tensor(oh[:, k, 4 * gi:4 * gi + 4, :], osum[:, g % 2, :, 0:DH],
                                        rden[:, g % 2, :, None].to_broadcast([P, 4, DH]), ALU.mult).then_inc(o_done[k], 1)

            def steps(t, n, valid):
                mw = n - LAGS["turn_w"]
                if valid(mw) and n % UNITS_HEAD in VECTOR_W:
                    related = n - LAGS["relate"]
                    if valid(related):
                        dve.wait_ge(r_out[related % SLOTS], use(t, related))
                    dve.wait_ge(w_turned[mw % SLOTS], use(t, mw))
                    copy_w(dve, nc.vector.tensor_copy, t, mw, valid)
                g = group_at(n, "copy_o", valid)
                if g is not None and n % UNITS_HEAD in VECTOR_O:
                    copy_o(dve, nc.vector.tensor_copy, t, g)
                m = n - LAGS["turn"]
                chunks = len(far_chunks(n % UNITS_HEAD)) + 1 if n >= 0 and valid(n) else 0
                split, back = group_at(n, "split", valid), group_at(n, "combine", valid)
                for c in range(max(4, chunks)):
                    if c < chunks:
                        score_chunk(t, n, c, valid)
                    if c < 4 and split is not None:
                        split_max(t, split, c, valid)
                    if c == 0 and back is not None:
                        combine(t, back)
                if valid(m) and n % UNITS_HEAD in VECTOR_TURNED:
                    copy_turned(dve, nc.vector.tensor_copy, t, m, valid)

            emit(dve, steps)

        @block.scalar
        def _(act):
            def copy(out, in_):
                return nc.scalar.activation(out, in_, ACT.Copy)

            def steps(t, n, valid):
                m, mw = n - LAGS["relate"], n - LAGS["turn_w"]
                if valid(m):
                    act.wait_ge(r_done, units(t, m))
                if valid(mw):
                    act.wait_ge(w_turned[mw % SLOTS], use(t, mw))
                if valid(m):
                    sl = m % SLOTS
                    if valid(m - SLOTS):
                        act.wait_ge(r_stored[sl], 16 * use(t, m - SLOTS))
                    copy(r_sb[:, sl, :], ps_rw[:, 0, :]).then_inc(r_out[sl], 1)
                if valid(mw) and n % UNITS_HEAD not in VECTOR_W:
                    copy_w(act, copy, t, mw, valid)
                g = group_at(n, "copy_o", valid)
                if g is not None and n % UNITS_HEAD not in VECTOR_O:
                    copy_o(act, copy, t, g)
                for part in range(4):
                    g = group_at(n, "far", valid, part)
                    if g is None:
                        continue
                    if part == 0:
                        group_read(act, t, g, valid)
                    for b, q0 in quarter(far_blocks(g % GPH), part):
                        bank, count = far_bank(t, g, b)
                        act.wait_ge(far_done[bank], count)
                        nc.scalar.activation(pt[:, PT_AT[g % GPH] + b, q0:GROUP], ps_f[:, bank, q0:GROUP], ACT.Exp)\
                            .then_inc(far_out[bank], 1)
                g = group_at(n, "spread", valid)
                if g is not None:
                    act.wait_ge(spread_done, groups(t, g))
                    gi = g % GPH
                    copy(qs[MAX_ROW:ROWS, head_of(g), gi * GROUP:(gi + 1) * GROUP], ps_p[MAX_ROW:ROWS, :]).then_inc(spread_out, 1)
                m = n - LAGS["turn"]
                if valid(m) and n % UNITS_HEAD not in VECTOR_TURNED:
                    copy_turned(act, copy, t, m, valid)
                m = n - LAGS["exp"]
                if valid(m):
                    sl, keys = m % SLOTS, min(m % UNITS_HEAD + 1, 3) * P
                    act.wait_ge(neg_done, units(t, m))
                    row = p[:, sl, NEAR - keys:NEAR]
                    nc.scalar.activation(row, row, ACT.Exp, bias=negtop[:, sl:sl + 1]).then_inc(expd[sl], 1)

            emit(act, steps)

        @block.tensor
        def _(pe):
            pe.wait_ge(ident_ready, 2)
            pe.wait_ge(setup, 2)
            for c in range(2):
                last = nc.tensor.transpose(ps_rw[0:DH, 0, c * P:(c + 1) * P], pek_d[:, c, :], ident[:, :])
            last.then_inc(pek_turned, 1)
            pe.wait_ge(stacked, 16 * len(LEFT))
            pe.wait_ge(pek_turned, 2)

            def relate_and_turn_w(t, m, mw, valid):
                k, i = (m // UNITS_HEAD) % HEADS, m % UNITS_HEAD
                if valid(m) and i == 0:
                    pe.wait_ge(q_loaded[k], (16 * SIDE_DMAS) * (t + m // UNITS) + 16 * SIDE_DMAS)
                if valid(m - 1):
                    pe.wait_ge(r_out[(m - 1) % SLOTS], use(t, m - 1))
                if valid(mw - 1):
                    pe.wait_ge(w_out, units(t, mw - 1))
                if valid(m):
                    nc.tensor.matmul(ps_rw[:, 0, :], qs[0:STACK, k, i * P:(i + 1) * P], pek_s[:, :], start=True, stop=True)\
                        .then_inc(r_done, 1)
                if valid(mw):
                    pe.wait_ge(w_loaded[mw % SLOTS], 16 * use(t, mw))
                    for c in range(2):
                        last = nc.tensor.transpose(ps_rw[:, 1, c * P:(c + 1) * P], w[:, mw % SLOTS, c * P:(c + 1) * P],
                                                   ident[:, :])
                    last.then_inc(w_turned[mw % SLOTS], 1)

            def score_chunk(t, m, c):
                k, i = (m // UNITS_HEAD) % HEADS, m % UNITS_HEAD
                far = far_chunks(i)
                bank, count = score_bank(t, m, c)
                near = min(i + 1, 3) * P
                if i == 0:
                    pe.wait_ge(k_loaded[k], (16 * SIDE_DMAS) * t + 16 * SIDE_DMAS)
                k0, keys = far[c] if c < len(far) else ((i + 1) * P - near, near)
                pe.wait_ge(score_out[bank], count - 1)
                nc.tensor.matmul(ps_s[:, bank, 0:keys], qs[0:STACK, k, i * P:(i + 1) * P], ks[0:STACK, k, k0:k0 + keys],
                                 start=True, stop=True).then_inc(scored[bank], 1)

            def turn_near(t, m, n, valid):
                blocks = min(m % UNITS_HEAD + 1, 3)
                pe.wait_ge(expd[m % SLOTS], use(t, m))
                spread, turned_back = group_at(n, "spread", valid), group_at(n, "turn_o", valid)
                if spread is not None:
                    pe.wait_ge(spread_out, groups(t, spread))
                elif turned_back is not None:
                    pe.wait_ge(o_summed, groups(t, turned_back))
                elif valid(m - 1):
                    pe.wait_ge(turned_out, units(t, m - 1))
                for b in range(blocks):
                    last = nc.tensor.transpose(ps_p[:, b * P:(b + 1) * P], p[:, m % SLOTS, (3 - blocks + b) * P:(4 - blocks + b) * P],
                                               ident[:, :])
                last.then_inc(turned, 1)

            def spread_max(t, g):
                pe.wait_ge(neg_split, head_turns(t, g) * (4 * GROUPS) + (4 * (g % GROUPS) + 4))
                pe.wait_ge(turned_out, units(t, 4 * g + 2 + LAGS["spread"] - LAGS["turn"]))
                for u in range(4):
                    last = nc.tensor.matmul(ps_p[MAX_ROW:ROWS, u * P:(u + 1) * P], neg_parts[:, g % 2, u, :], ident_b[:, :],
                                            start=True, stop=True)
                last.then_inc(spread_done, 1)

            def far_block(t, g, b, q0):
                k, gi = head_of(g), g % GPH
                bank, count = far_bank(t, g, b)
                if b == 0:
                    pe.wait_ge(spread_out, groups(t, g))
                pe.wait_ge(far_out[bank], count - 1)
                nc.tensor.matmul(ps_f[:, bank, q0:GROUP], ks[:, k, b * P:(b + 1) * P], qs[:, k, gi * GROUP + q0:(gi + 1) * GROUP],
                                 start=True, stop=True).then_inc(far_done[bank], 1)

            def weigh_parts(g):
                k, gi = head_of(g), g % GPH
                v_of = lambda b: (vh[:, k, b, :], pt[:, PT_AT[gi] + b, :], max(0, b - 4 * gi) * P, b)
                near = [(pev_d[:, c, :], wt[:, gi, c, :], 0, None) for c in range(2)]
                if gi == 0:
                    return [v_of(0), near[0], near[1], v_of(3), v_of(1), v_of(2)]
                return [v_of(b) for b in range(4 * gi + 4)] + near

            def weigh(t, g, part, n, valid):
                k, gi = head_of(g), g % GPH
                parts = weigh_parts(g)
                tiles = 3 if gi == 0 else 4
                if n == 0:
                    pe.wait_ge(turned_out, units(t, 4 * g + 3))
                    if valid(4 * (g - 1)):
                        pe.wait_ge(o_out, groups(t, g - 1))
                    if gi == 0:
                        pe.wait_ge(v_loaded[k], 16 * head_turns(t, g) + 16)
                left, right, q0, b = parts[n]
                if b is None:
                    pe.wait_ge(w_out, units(t, 4 * g + 3))
                elif b <= 4 * gi:
                    bank, count = far_bank(t, g, b)
                    pe.wait_ge(far_out[bank], count)
                ct = n % tiles
                done = nc.tensor.matmul(ps_o[ct * CT:ct * CT + DV, q0:GROUP], left, right[:, q0:GROUP],
                                        start=n < tiles, stop=n >= len(parts) - tiles, skip_group_check=True)
                if n == len(parts) - 1:
                    done.then_inc(pv_done[k], 1)

            def turn_o(t, g, valid):
                pe.wait_ge(o_out, groups(t, g))
                m = 4 * g + 2 + LAGS["turn_o"] - LAGS["turn"]
                if valid(m):
                    pe.wait_ge(turned_out, units(t, m))
                else:
                    pe.wait_ge(turned_out, units(t, UNITS - 1))
                    pe.wait_ge(o_summed, groups(t, g - 1))
                for q in range(4):
                    last = nc.tensor.transpose(ps_p[:, q * P:(q + 1) * P], ot[:, q * P:(q + 1) * P], ident[:, :])
                last.then_inc(o_back, 1)

            def steps(t, n, valid):
                relate_and_turn_w(t, n - LAGS["relate"], n - LAGS["turn_w"], valid)
                scores, fars, weighs = [], [], []
                if n >= 0 and valid(n):
                    scores = list(range(len(far_chunks(n % UNITS_HEAD)) + 1))
                for part in range(4):
                    g = group_at(n, "far", valid, part)
                    if g is not None:
                        fars = [(g, b, q0) for b, q0 in quarter(far_blocks(g % GPH), part)]
                    g = group_at(n, "weigh", valid, part)
                    if g is not None:
                        places = list(range(len(weigh_parts(g))))
                        if g % GPH:
                            weighs += [(g, part, x) for x in quarter(places, part)]
                        elif part == 3:
                            weighs += [(g, part, x) for x in places]
                m = n - LAGS["turn"]
                first_weighs = [what for what in weighs if what[1] == 0]
                weighs = [what for what in weighs if what[1] > 0]
                steps_here = max(1, len(scores), len(fars), len(weighs))
                for c in range(steps_here):
                    if c < len(scores):
                        score_chunk(t, n, c)
                    if c < len(fars):
                        far_block(t, *fars[c])
                    if c < len(weighs):
                        weigh(t, *weighs[c], valid)
                    if c == (steps_here - 1) * SHARED_AT // 4:
                        g = group_at(n, "spread", valid)
                        if g is not None:
                            spread_max(t, g)
                        g = group_at(n, "turn_o", valid)
                        if g is not None:
                            turn_o(t, g, valid)
                if valid(m):
                    turn_near(t, m, n, valid)
                for what in first_weighs:
                    weigh(t, *what, valid)

            emit(pe, steps)


def output_stage(nc, name, x, att, out, wo_t):
    turns = NTOK // GROUP // 2
    with Stage(nc, name) as s:
        ident, zeroed, ident_ready = s.sb("ident", [P, P]), s.sem("zeroed"), s.sem("ident_ready")
        w, w_loaded = s.sb("w", [P, CK, D]), s.sem("w_loaded")
        ag, xg, xo = (s.sb(n, [P, 2, TILES, D]) for n in ("ag", "xg", "xo"))
        at = s.sb("at", [P, 2, CK, GROUP])
        ps_t = s.ps("ps_t", [P, 2, CK, GROUP])
        ps_y = s.ps("ps_y", [P, 2, TILES, D])
        loaded, turned, turned_out, y_done, x_out, stored = (
            s.sems(n, 2) for n in ("loaded", "turned", "turned_out", "y_done", "x_out", "stored"))
        block = s.block()
        av, xv, ov = (a.rearrange("(u k i p) c -> u k p i c", p=P, i=TILES, k=2) for a in (att, x, out))

        @block.sync
        def _(sp):
            def load(k, u):
                sp.dma_start(ag[:, k, :, :], av[u, k, :, :, :]).then_inc(loaded[k], 16)
                sp.dma_start(xg[:, k, :, :], xv[u, k, :, :, :]).then_inc(loaded[k], 16)

            load(0, 0)
            sp.dma_start(w[:, :, :], wo_t.rearrange("(k p) f -> p k f", p=P)).then_inc(w_loaded, 16)
            load(1, 0)

            def turn(t, last):
                for k in range(2):
                    sp.wait_ge(x_out[k], t + 1)
                    sp.dma_start(ov[t, k, :, :, :], xo[:, k, :, :]).then_inc(stored[k], 16)
                    if not last:
                        load(k, t + 1)

            turn(0, False)
            with sp.Fori(1, turns - 1) as t:
                turn(t, False)
            turn(turns - 1, True)
            for k in range(2):
                sp.wait_ge(stored[k], 16 * turns)

        @block.gpsimd
        def _(pool):
            make_identity(nc, pool, ident, zeroed, ident_ready)

        @block.scalar
        def _(act):
            def turn(t):
                for k in range(2):
                    act.wait_ge(turned[k], t + 1)
                    act.wait_ge(y_done[k], t)
                    nc.scalar.activation(at[:, k, :, :], ps_t[:, k, :, :], ACT.Copy).then_inc(turned_out[k], 1)

            for_turns(act, turns, turn)

        @block.vector
        def _(dve):
            def turn(t):
                for k in range(2):
                    dve.wait_ge(y_done[k], t + 1)
                    dve.wait_ge(stored[k], t * 16)
                    nc.vector.tensor_tensor(xo[:, k, :, :], ps_y[:, k, :, :], xg[:, k, :, :], ALU.add)\
                        .then_inc(x_out[k], 1)

            for_turns(dve, turns, turn)

        @block.tensor
        def _(pe):
            pe.wait_ge(ident_ready, 1)
            pe.wait_ge(w_loaded, 16)
            def turn(t):
                for k in range(2):
                    pe.wait_ge(loaded[k], t * 32 + 32)
                    pe.wait_ge(turned_out[k], t)
                    for i in range(TILES):
                        for ck in range(CK):
                            last = nc.tensor.transpose(ps_t[:, k, ck, i * P:(i + 1) * P], ag[:, k, i, ck * P:(ck + 1) * P],
                                                       ident[:, :])
                    last.then_inc(turned[k], 1)
                for k in range(2):
                    pe.wait_ge(turned_out[k], t + 1)
                    pe.wait_ge(x_out[k], t)
                    for i in range(TILES):
                        for ck in range(CK):
                            last = nc.tensor.matmul(ps_y[:, k, i, :], at[:, k, ck, i * P:(i + 1) * P], w[:, ck, :],
                                                    start=ck == 0, stop=ck == CK - 1)
                    last.then_inc(y_done[k], 1)

            for_turns(pe, turns, turn)


def hybrid_layer_kernel(nc, a, out):
    def scratch(name, shape, dt=F32):
        return nc.dram_tensor(name, shape, dt, kind="Internal").ap()

    x0 = a["x"].rearrange("b l c -> (b l) c")
    x1, x2, x3 = (scratch(f"x{n}", (NTOK, D)) for n in (1, 2, 3))
    qk_a = scratch("qk_a", (2, 3, D, B, L + 2 * PAD), BF16)
    v_a = scratch("v_a", (B, L + 2 * PAD, D))
    qk_b = scratch("qk_b", (2, 3, D, B, L), BF16)
    v_b = scratch("v_b", (B, H, P, L // P, DH + 1))
    att = scratch("att", (NTOK, D))
    bias_rows = scratch("bias_rows", (8, P, 4 * P))
    prob_rows = scratch("prob_rows", (8, P, 3 * P))
    ffn = [a[n] for n in ("sw1", "sb1", "sw3", "sb3", "sw2", "sb2", "w1", "b1", "w2", "b2")]

    project_stage(nc, "pa", x0, a["a_wq_t"], a["a_wk_t"], a["a_wv_t"], qk_a, v_a)
    window_stage(nc, "wa", x0, x1, qk_a, v_a, a["a_wo_t"], a["bo"])
    ffn_stage(nc, "fa", x1, x2, *ffn)
    project_stage(nc, "pb", x2, a["b_wq_t"], a["b_wk_t"], a["b_wv_t"], qk_b, v_b, a["pek"][0:1, :], a["pev"][0:1, :])
    causal_stage(nc, "ca", att, qk_b, v_b, a["pek"], a["pev"], bias_rows, prob_rows)
    output_stage(nc, "ob", x2, att, x3, a["b_wo_t"])
    ffn_stage(nc, "fb", x3, out.rearrange("b l c -> (b l) c"), *ffn)


def kernel(**inputs):
    import numpy as _np
    import concourse.bacc as _bacc
    from concourse import mybir as _mybir
    from concourse.bass_utils import run_bass_kernel_spmd as _run

    i = {n.removeprefix("L0_"): _np.asarray(v) for n, v in inputs.items()}
    laid = {"x": i["attn_a_x"], "bo": i["attn_a_bo"], "pek": i["attn_b_pek"], "pev": i["attn_b_pev"]}
    for part in "ab":
        for m in ("Wq", "Wk", "Wv", "Wo"):
            laid[f"{part}_{m.lower()}_t"] = i[f"attn_{part}_{m}"].T
    for n in ("sw1", "sb1", "sw3", "sb3", "sw2", "sb2", "w1", "b1", "w2", "b2"):
        laid[n] = i[f"ffn_{n}"]

    nc = _bacc.Bacc("TRN2", target_bir_lowering=False, num_devices=1)
    arrays, aps = {}, {}
    for n, v in laid.items():
        arrays[f"in_{n}"] = _np.ascontiguousarray(v)
        aps[n] = nc.dram_tensor(f"in_{n}", v.shape, _mybir.dt.from_np(v.dtype), kind="ExternalInput").ap()
    out = nc.dram_tensor("out", (B, L, D), _mybir.dt.float32, kind="ExternalOutput").ap()
    hybrid_layer_kernel(nc, aps, out)
    return _run(nc, [arrays], core_ids=[0]).results[0]["out"]
```

```python
from contextlib import ExitStack

import concourse.bass as bass
import numpy as np
from concourse import mybir

ALU = mybir.AluOpType
ACT = mybir.ActivationFunctionType
AX = mybir.AxisListType
F32 = mybir.dt.float32
BF16 = mybir.dt.bfloat16

P = 128
B, L, D = 2, 2048, 256
NTOK = B * L
CK = D // P
H = 16
DH = D // H
WINDOW = 64
PAD = WINDOW // 2
GROUP = 512
TILES = GROUP // P
MAX_REL = 256
LN_EPS = 1e-5
SCORE_SCALE = float(DH) ** -0.5
MASKED = -1e30
LEFT = (0, 0, 0, 1, 1, 2)
RIGHT = (0, 1, 2, 0, 1, 0)
STACK = len(LEFT) * DH
LEFT_RUNS = ((0, 0, 3, 0), (3, 1, 2, 0), (5, 2, 1, 0))
RIGHT_RUNS = ((0, 0, 3, 1), (3, 0, 2, 1), (5, 0, 1, 1))


class Stage:

    def __init__(self, nc, name):
        self.nc, self.name, self.ctx, self.semaphores = nc, name, ExitStack(), []

    def __enter__(self):
        self.ctx.__enter__()
        return self

    def __exit__(self, *e):
        self.ctx.__exit__(*e)
        self.nc.clear_and_free_semaphores(self.semaphores)
        self.nc.all_engine_barrier()

    def sb(self, name, shape, dt=F32):
        return self.ctx.enter_context(self.nc.sbuf_tensor(f"{self.name}_{name}", shape, dt))

    def ps(self, name, shape, dt=F32):
        return self.ctx.enter_context(self.nc.psum_tensor(f"{self.name}_{name}", shape, dt))

    def sem(self, name):
        self.semaphores.append(self.nc.alloc_semaphore(f"{self.name}_{name}"))
        return self.semaphores[-1]

    def sems(self, name, n):
        return [self.sem(f"{name}{i}") for i in range(n)]

    def block(self):
        return self.ctx.enter_context(self.nc.Block())


def for_turns(engine, turns, turn):
    turn(0)
    with engine.Fori(1, turns) as t:
        turn(t)


def for_turns_ends(engine, turns, turn):
    turn(0, True, False)
    with engine.Fori(1, turns - 1) as t:
        turn(t, False, False)
    turn(turns - 1, False, True)


def make_identity(nc, pool, ident, zeroed, ready):
    nc.gpsimd.memset(ident[:, :], 0.0).then_inc(zeroed, 1)
    pool.wait_ge(zeroed, 1)
    nc.gpsimd.affine_select(out=ident[:, :], in_=ident[:, :], compare_op=ALU.not_equal, fill=1.0,
                            base=0, pattern=[[-1, P]], channel_multiplier=1).then_inc(ready, 1)


def project_stage(nc, name, x, wq_t, wk_t, wv_t, qk, v, pek0=None, pev0=None):
    rel = pek0 is not None
    off = 0 if rel else PAD
    turns = NTOK // GROUP // 2
    with Stage(nc, name) as s:
        ident, zeroed, ident_ready = s.sb("ident", [P, P]), s.sem("zeroed"), s.sem("ident_ready")
        w = s.sb("w", [P, 3, CK, D])
        w_loaded, bias_loaded = s.sem("w_loaded"), s.sem("bias_loaded")
        eps = s.sb("eps", [P, 1])
        kbias = s.sb("kbias", [P, 2])
        vbias = s.sb("vbias", [P, DH])
        const_set = s.sem("const_set")
        xg = s.sb("xg", [P, 2, TILES, D])
        stats = s.sb("stats", [P, 2, TILES, 6])
        mv = s.sb("mv", [P, 2, TILES, 2])
        spare = s.sb("spare", [P, 1])
        std = s.sb("std", [P, 2, TILES])
        rstd = s.sb("rstd", [P, 2, TILES])
        xn = s.sb("xn", [P, 2, TILES, D])
        xt = s.sb("xt", [P, 2, CK, GROUP])
        parts = s.sb("parts", [P, 2, 4, 3, GROUP], BF16)
        rest = s.sb("rest", [P, 4, GROUP])
        vout = s.sb("vout", [P, 2, H, TILES, DH + 1]) if rel else s.sb("vout", [P, 2, TILES, H, DH + 1])
        ps_t = s.ps("ps_t", [P, CK, GROUP])
        ps_qk = s.ps("ps_qk", [P, 4, GROUP])
        ps_v = s.ps("ps_v", [P, TILES, D])

        x_loaded, stats_done, mv_done, std_done, rstd_done, normed = (
            s.sems(n, 2) for n in ("x_loaded", "stats_done", "mv_done", "std_done", "rstd_done", "normed"))
        turned, turned_out_a, turned_out_v = (s.sems(n, 2) for n in ("turned", "turned_out_a", "turned_out_v"))
        qk_done, high_done, rest_done, mid_done, low_done, parts_stored = (
            [s.sems(f"{n}{k}", 4) for k in range(2)]
            for n in ("qk_done", "high_done", "rest_done", "mid_done", "low_done", "parts_stored"))
        v_done, v_out, v_stored = (s.sems(n, 2) for n in ("v_done", "v_out", "v_stored"))
        edges_stored = s.sem("edges_stored")
        edge, edges_set = s.sb("edge", [P, 2 * 3 * CK, PAD], BF16), s.sem("edges_set")
        vedge = s.sb("vedge", [PAD, H, DH + 1])
        passed = s.sem("passed")
        block = s.block()
        xv = x.rearrange("(u k i p) c -> u k p i c", p=P, i=TILES, k=2)

        @block.sync
        def _(sp):
            sp.dma_start(xg[:, 0, :, :], xv[0, 0, :, :, :]).then_inc(x_loaded[0], 16)
            for n, src in enumerate((wq_t, wk_t, wv_t)):
                sp.dma_start(w[:, n, :, :], src.rearrange("(k p) f -> p k f", p=P)).then_inc(w_loaded, 16)
            if rel:
                for hh in range(P // DH):
                    sp.dma_start(kbias[hh * DH:(hh + 1) * DH, 1:2], pek0.rearrange("a d -> d a")).then_inc(bias_loaded, 16)
                sp.dma_start(vbias[:, :], bass.AP(pev0.tensor, pev0.offset, [[0, P], [1, DH]])).then_inc(bias_loaded, 16)
            sp.dma_start(xg[:, 1, :, :], xv[0, 1, :, :, :]).then_inc(x_loaded[1], 16)
            if not rel:
                sp.wait_ge(edges_set, 3)
                for bb in range(B):
                    for c0 in (0, PAD + L):
                        rows = qk[0, 0, 0:P, bb, c0:c0 + PAD]
                        sp.dma_start(bass.AP(rows.tensor, rows.offset,
                                             [list(rows.ap[0]), [P * rows.ap[0][0], 2 * 3 * CK], [1, PAD]]),
                                     edge[:, :, :]).then_inc(edges_stored, 16)
                        sp.dma_start(v[bb, c0:c0 + PAD, :], vedge[:, :, :].rearrange("p h d -> p (h d)")).then_inc(edges_stored, 16)

            def turn(t, first, last):
                done, ahead = sp.snap(t + 1), sp.snap(t + 1)
                col = sp.snap((t % 2) * (2 * GROUP) + off)
                batch = sp.snap(t // 2)
                tile = sp.snap((t % 2) * (2 * TILES))
                for k in range(2):
                    if not last:
                        sp.wait_ge(normed[k], done)
                        sp.dma_start(xg[:, k, :, :], xv[ahead, k, :, :, :]).then_inc(x_loaded[k], 16)
                    for q in range(4):
                        a, ck = q // 2, q % 2
                        sp.wait_ge(low_done[k][q], done)
                        sp.sem_inc(passed, 1)
                        dst = qk[a, :, ck * P:(ck + 1) * P, batch, bass.ds(col + k * GROUP, GROUP)]
                        sp.dma_start(dst.rearrange("a f c -> f a c"), parts[:, k, q, :, :])\
                            .then_inc(parts_stored[k][q], 16)
                    sp.wait_ge(v_out[k], done)
                    sp.sem_inc(passed, 1)
                    if rel:
                        dst = v[batch, :, :, bass.ds(tile + k * TILES, TILES), :]
                        sp.dma_start(dst.rearrange("h p i d -> p h i d"), vout[:, k, :, :, :]).then_inc(v_stored[k], 16)
                    else:
                        dst = v[batch, bass.ds(col + k * GROUP, GROUP), :]
                        sp.dma_start(dst.rearrange("(i p) c -> p i c", p=P),
                                     vout[:, k, :, :, :].rearrange("p i h d -> p i (h d)")).then_inc(v_stored[k], 16)

            for_turns_ends(sp, turns, turn)
            for k in range(2):
                for q in range(4):
                    sp.wait_ge(parts_stored[k][q], 16 * turns)
                sp.wait_ge(v_stored[k], 16 * turns)
            if not rel:
                sp.wait_ge(edges_stored, 16 * B * 2 * 2)

        n_bias = 16 * (P // DH + 1)

        @block.gpsimd
        def _(pool):
            make_identity(nc, pool, ident, zeroed, ident_ready)
            nc.gpsimd.memset(eps[:, :], LN_EPS).then_inc(const_set, 1)
            nc.gpsimd.memset(vout[:, :, :, :, DH:DH + 1], 1.0).then_inc(const_set, 1)
            if not rel:
                nc.gpsimd.memset(edge[:, :, :], 0.0).then_inc(edges_set, 1)
                nc.gpsimd.memset(vedge[:, :, 0:DH], 0.0).then_inc(edges_set, 1)
                nc.gpsimd.memset(vedge[:, :, DH:DH + 1], 1.0).then_inc(edges_set, 1)
                nc.gpsimd.memset(kbias[:, :], 0.0).then_inc(const_set, 1)
            else:
                nc.gpsimd.memset(kbias[:, 0:1], 0.0).then_inc(const_set, 1)
            def turn(t):
                done = pool.snap(t + 1)
                for k in range(2):
                    for q in range(4):
                        pool.wait_ge(mid_done[k][q], done)
                        nc.gpsimd.tensor_tensor(parts[:, k, q, 2, :], rest[:, q, :], parts[:, k, q, 1, :],
                                                ALU.subtract).then_inc(low_done[k][q], 1)

            for_turns(pool, turns, turn)

        def after(t, k):
            return t + 2 if k else t + 1

        n_set = 3

        @block.vector
        def _(dve):
            def stats_of(count, k):
                dve.wait_ge(x_loaded[k], count * 16)
                for i in range(TILES):
                    last = nc.vector.bn_stats(stats[:, k, i, :], xg[:, k, i, :])
                last.then_inc(stats_done[k], 1)

            def mean_and_variance(count, k):
                dve.wait_ge(stats_done[k], count)
                nc.vector.memset(spare[:, :], 0.0)
                for i in range(TILES):
                    last = nc.vector.bn_aggr(mv[:, k, i, :], stats[:, k, i, :])
                last.then_inc(mv_done[k], 1)

            def normalise(count, k):
                dve.wait_ge(std_done[k], count)
                nc.vector.reciprocal(rstd[:, k, :], std[:, k, :]).then_inc(rstd_done[k], 1)
                dve.wait_ge(rstd_done[k], count)
                for i in range(TILES):
                    last = nc.vector.tensor_scalar(xn[:, k, i, :], xg[:, k, i, :], mv[:, k, i, 0:1],
                                                   rstd[:, k, i:i + 1], ALU.subtract, ALU.mult)
                last.then_inc(normed[k], 1)

            def copy_xt(count, k):
                dve.wait_ge(turned[k], count)
                nc.vector.tensor_copy(xt[:, k, 1, :], ps_t[:, 1, :]).then_inc(turned_out_v[k], 1)

            def rest_of(t, k, q, first):
                dve.wait_ge(high_done[k][q], t + 1)
                if k:
                    dve.wait_ge(low_done[0][q], t + 1)
                elif not first:
                    dve.wait_ge(low_done[1][q], t)
                scale_or_bias, op = (SCORE_SCALE, ALU.mult) if q < 2 else (kbias[:, 1:2], ALU.add)
                nc.vector.scalar_tensor_tensor(rest[:, q, :], ps_qk[:, q, :], scale_or_bias,
                                               parts[:, k, q, 0, :], op, ALU.subtract).then_inc(rest_done[k][q], 1)

            stats_of(1, 0)
            mean_and_variance(1, 0)
            normalise(1, 0)
            copy_xt(1, 0)
            dve.wait_ge(const_set, n_set)
            if rel:
                dve.wait_ge(bias_loaded, n_bias)

            def turn(t, first, last):
                for k in range(2):
                    nxt = k == 0 or not last
                    if nxt:
                        stats_of(after(t, k), 1 - k)
                    rest_of(t, k, 0, first)
                    if nxt:
                        mean_and_variance(after(t, k), 1 - k)
                    rest_of(t, k, 1, first)
                    if nxt:
                        normalise(after(t, k), 1 - k)
                    rest_of(t, k, 2, first)
                    rest_of(t, k, 3, first)
                    if nxt:
                        copy_xt(after(t, k), 1 - k)
                    dve.wait_ge(v_done[k], t + 1)
                    if not first:
                        dve.wait_ge(v_stored[k], t * 16)
                    for i in range(TILES):
                        if rel:
                            done = nc.vector.tensor_tensor(vout[:, k, :, i, 0:DH],
                                                           ps_v[:, i, :].rearrange("p (h d) -> p h d", d=DH),
                                                           vbias[:, None, :].to_broadcast([P, H, DH]), ALU.add)
                        else:
                            done = nc.vector.tensor_copy(vout[:, k, i, :, 0:DH], ps_v[:, i, :].rearrange("p (h d) -> p h d", d=DH))
                    done.then_inc(v_out[k], 1)

            for_turns_ends(dve, turns, turn)

        @block.scalar
        def _(act):
            def deviation(count, k):
                act.wait_ge(mv_done[k], count)
                nc.scalar.activation(std[:, k, :], mv[:, k, :, 1], ACT.Sqrt, bias=eps[:, 0:1]).then_inc(std_done[k], 1)

            def copy_xt(count, k):
                act.wait_ge(turned[k], count)
                nc.scalar.activation(xt[:, k, 0, :], ps_t[:, 0, :], ACT.Copy).then_inc(turned_out_a[k], 1)

            def high(t, k, q, first):
                act.wait_ge(qk_done[k][q], t + 1)
                if not first:
                    act.wait_ge(parts_stored[k][q], t * 16)
                nc.scalar.activation(parts[:, k, q, 0, :], ps_qk[:, q, :], ACT.Identity,
                                     bias=kbias[:, q // 2:q // 2 + 1], scale=SCORE_SCALE if q < 2 else 1.0)\
                    .then_inc(high_done[k][q], 1)

            def middle(t, k, q):
                act.wait_ge(rest_done[k][q], t + 1)
                nc.scalar.activation(parts[:, k, q, 1, :], rest[:, q, :], ACT.Copy).then_inc(mid_done[k][q], 1)

            act.wait_ge(const_set, n_set)
            deviation(1, 0)
            copy_xt(1, 0)
            if rel:
                act.wait_ge(bias_loaded, n_bias)

            def turn(t, first, last):
                for k in range(2):
                    nxt = k == 0 or not last
                    high(t, k, 0, first)
                    high(t, k, 1, first)
                    if nxt:
                        deviation(after(t, k), 1 - k)
                    middle(t, k, 0)
                    high(t, k, 2, first)
                    middle(t, k, 1)
                    high(t, k, 3, first)
                    if nxt:
                        copy_xt(after(t, k), 1 - k)
                    middle(t, k, 2)
                    middle(t, k, 3)

            for_turns_ends(act, turns, turn)

        @block.tensor
        def _(pe):
            pe.wait_ge(ident_ready, 1)

            def turn_in(count, k):
                pe.wait_ge(normed[k], count)
                for i in range(TILES):
                    for ck in range(CK):
                        last = nc.tensor.transpose(ps_t[:, ck, i * P:(i + 1) * P],
                                                   xn[:, k, i, ck * P:(ck + 1) * P], ident[:, :])
                last.then_inc(turned[k], 1)

            turn_in(1, 0)
            pe.wait_ge(w_loaded, 16 * 3)

            def turn(t, first, last):
                for k in range(2):
                    pe.wait_ge(turned_out_a[k], t + 1)
                    pe.wait_ge(turned_out_v[k], t + 1)
                    for q in range(4):
                        a, fc = q // 2, q % 2
                        if k:
                            pe.wait_ge(rest_done[0][q], t + 1)
                        elif not first:
                            pe.wait_ge(rest_done[1][q], t)
                        for ck in range(CK):
                            done = nc.tensor.matmul(ps_qk[:, q, :], w[:, a, ck, fc * P:(fc + 1) * P],
                                                    xt[:, k, ck, :], start=ck == 0, stop=ck == CK - 1)
                        done.then_inc(qk_done[k][q], 1)
                    if k == 0 or not last:
                        turn_in(after(t, k), 1 - k)
                    if k:
                        pe.wait_ge(v_out[0], t + 1)
                    elif not first:
                        pe.wait_ge(v_out[1], t)
                    for i in range(TILES):
                        for ck in range(CK):
                            done = nc.tensor.matmul(ps_v[:, i, :], xt[:, k, ck, i * P:(i + 1) * P],
                                                    w[:, 2, ck, :], start=ck == 0, stop=ck == CK - 1)
                    done.then_inc(v_done[k], 1)

            for_turns_ends(pe, turns, turn)
EXPERTS = 8
HS = 512
HR = 256
RUN = GROUP // EXPERTS
HC, RC = HS // P, HR // P
RUNS = ((0, 0, 4, 0), (1, 0, 2, 5), (1, 2, 2, 1))


SB1, SB3, B1, SB2, B2, BIAS_ROWS = (sum((HC, HC, EXPERTS * RC, CK, EXPERTS * CK)[:n]) for n in range(6))


def ffn_stage(nc, name, x, out, sw1, sb1, sw3, sb3, sw2, sb2, w1, b1, w2, b2, att=None, wo_t=None):
    turns = NTOK // GROUP // 2
    with Stage(nc, name) as s:
        ident, zeroed, ident_ready = s.sb("ident", [P, P]), s.sem("zeroed"), s.sem("ident_ready")
        rows_loaded, rows_turned, cols_set = s.sem("rows_loaded"), s.sem("rows_turned"), s.sem("cols_set")
        up_loaded, w1_loaded, down_loaded, sw2_loaded = (
            s.sem(n) for n in ("up_loaded", "w1_loaded", "down_loaded", "sw2_loaded"))
        sw1_sb, sw3_sb = s.sb("sw1", [P, CK, HS]), s.sb("sw3", [P, CK, HS])
        sw2_in, sw2_sb = s.sb("sw2_in", [P, HC, D]), s.sb("sw2", [P, HC, D])
        w1_sb, w2_sb = s.sb("w1", [P, EXPERTS, CK, HR]), s.sb("w2", [P, EXPERTS, RC, D])
        rows, cols = s.sb("rows", [BIAS_ROWS, P]), s.sb("cols", [P, BIAS_ROWS])
        bias, bias2, sb2x = s.sb("bias", [P, CK, EXPERTS]), s.sb("bias2", [P, CK, EXPERTS]), s.sb("sb2x", [P, CK])
        eps, spare = s.sb("eps", [P, 1]), s.sb("spare", [P, 1])
        const_set, bias_steps, doubled = s.sem("const_set"), s.sem("bias_steps"), s.sem("doubled")
        xg = s.sb("xg", [P, 2, TILES, D])
        xr = s.sb("xr", [P, 2, TILES, D])
        xo = s.sb("xo", [P, 2, TILES, D])
        if att is not None:
            wo_sb, ag, at = s.sb("wo", [P, CK, D]), s.sb("ag", [P, 2, TILES, D]), s.sb("at", [P, CK, GROUP])
        xin = xg if att is None else xr
        stats = s.sb("stats", [P, 2, TILES, 6])
        mv = s.sb("mv", [P, 2, TILES, 2])
        std, rstd = s.sb("std", [P, 2, TILES]), s.sb("rstd", [P, 2, TILES])
        xn = s.sb("xn", [P, 2, TILES, D])
        xt = s.sb("xt", [P, 2, CK, GROUP])
        sil = s.sb("sil", [P, 2, GROUP])
        gated = s.sb("gated", [P, HC, GROUP])
        hidden = s.sb("hidden", [P, EXPERTS, RC, 2 * RUN])
        yt = s.sb("yt", [P, CK, GROUP])
        ps_t = s.ps("ps_t", [P, CK, GROUP])
        ps_h = s.ps("ps_h", [P, 4, GROUP])
        ps_y = s.ps("ps_y", [P, CK, GROUP])

        x_loaded, xr_loaded, stats_done, mv_done, std_done, rstd_done, normed = (
            s.sems(n, 2) for n in ("x_loaded", "xr_loaded", "stats_done", "mv_done", "std_done", "rstd_done", "normed"))
        turned, turned_out_a, turned_out_v = (s.sems(n, 2) for n in ("turned", "turned_out_a", "turned_out_v"))
        up_done, sil_done, gated_done = ([s.sems(f"{n}{k}", HC) for k in range(2)]
                                         for n in ("up_done", "sil_done", "gated_done"))
        eup_done, hidden_done = ([s.sems(f"{n}{k}", EXPERTS) for k in range(2)] for n in ("eup_done", "hidden_done"))
        down_done, y_out, back_done, res_done, stored = (
            s.sems(n, 2) for n in ("down_done", "y_out", "back_done", "res_done", "stored"))
        att_loaded, att_turned, at_out, projected, added = (
            s.sems(n, 2) for n in ("att_loaded", "att_turned", "at_out", "projected", "added"))
        wo_loaded = s.sem("wo_loaded")
        passed = s.sem("passed")
        block = s.block()
        xv = x.rearrange("(u k n r) c -> u k r n c", k=2, n=RUN, r=EXPERTS)
        ov = out.rearrange("(u k n r) c -> u k r n c", k=2, n=RUN, r=EXPERTS)
        av = att.rearrange("(u k n r) c -> u k r n c", k=2, n=RUN, r=EXPERTS) if att is not None else None

        def pair(a, e):
            v = a.rearrange("p (j n) -> p j n", n=RUN)
            return v[:, e:e + 2, :] if e < EXPERTS - 1 else v[:, EXPERTS - 1::-(EXPERTS - 1), :]

        def before(t, k):
            return t + 1 if k else t

        def after(t, k):
            return t + 2 if k else t + 1

        @block.sync
        def _(sp):
            def load(to, what, k, u, source=xv):
                for half, tile, n, residue in RUNS:
                    sp.dma_start(to[half * RUN:(half + 1) * RUN, k, tile:tile + n, :],
                                 source[u, k, residue:residue + 2 * n - 1:2, :, :].rearrange("r n c -> n r c"))\
                        .then_inc(what[k], 16)

            if att is not None:
                load(ag, att_loaded, 0, 0, av)
                sp.dma_start(wo_sb[:, :, :], wo_t.rearrange("(k p) f -> p k f", p=P)).then_inc(wo_loaded, 16)
            load(xg, x_loaded, 0, 0)
            for at, src in ((SB1, sb1), (SB3, sb3), (B1, b1), (SB2, sb2), (B2, b2)):
                n = int(np.prod(src.shape)) // P
                sp.dma_start(rows[at:at + n, :], bass.AP(src.tensor, src.offset, [[P, n], [1, P]])).then_inc(rows_loaded, 16)
            sp.dma_start(sw1_sb[:, :, :], sw1.rearrange("(k p) f -> p k f", p=P)).then_inc(up_loaded, 16)
            sp.dma_start(sw3_sb[:, :, :], sw3.rearrange("(k p) f -> p k f", p=P)).then_inc(up_loaded, 16)
            if att is not None:
                load(ag, att_loaded, 1, 0, av)
            load(xg, x_loaded, 1, 0)
            sp.dma_start(w1_sb[:, :, :, :], w1.rearrange("e (k p) f -> p e k f", p=P)).then_inc(w1_loaded, 16)
            sp.dma_start(sw2_in[:, :, :], sw2.rearrange("(k p) f -> p k f", p=P)).then_inc(sw2_loaded, 16)
            sp.dma_start(w2_sb[:, :, :, :], w2.rearrange("e (k p) f -> p e k f", p=P)).then_inc(down_loaded, 16)
            if att is None:
                load(xr, xr_loaded, 0, 0)

            def store(t, k):
                for half, tile, n, residue in RUNS:
                    sp.dma_start(ov[t, k, residue:residue + 2 * n - 1:2, :, :].rearrange("r n c -> n r c"),
                                 xo[half * RUN:(half + 1) * RUN, k, tile:tile + n, :]).then_inc(stored[k], 16)

            def turn(t, first, last):
                done, last_turn = sp.snap(t + 1), None if first else sp.snap(t - 1)
                this = sp.snap(t + 0)
                for k in range(2):
                    if not last:
                        sp.wait_ge((normed if att is None else added)[k], done)
                        sp.sem_inc(passed, 1)
                        if att is not None:
                            load(ag, att_loaded, k, done, av)
                        load(xg, x_loaded, k, done)
                    if k or not first:
                        sp.wait_ge(res_done[1 - k], before(this, k))
                        sp.sem_inc(passed, 1)
                        store(this if k else last_turn, 1 - k)
                    if att is None and (k == 0 or not last):
                        load(xr, xr_loaded, 1 - k, done if k else this)

            for_turns_ends(sp, turns, turn)
            sp.wait_ge(res_done[1], turns)
            store(turns - 1, 1)
            for k in range(2):
                sp.wait_ge(stored[k], 16 * len(RUNS) * turns)

        @block.gpsimd
        def _(pool):
            make_identity(nc, pool, ident, zeroed, ident_ready)
            nc.gpsimd.memset(eps[:, :], LN_EPS).then_inc(const_set, 1)
            pool.wait_ge(sw2_loaded, 16)
            nc.gpsimd.tensor_scalar(sw2_sb[:, :, :], sw2_in[:, :, :], 2.0, None, ALU.mult).then_inc(doubled, 1)

        @block.vector
        def _(dve):
            def stats_of(count, k):
                if att is not None:
                    dve.wait_ge(x_loaded[k], count * (16 * len(RUNS)))
                    dve.wait_ge(projected[k], count)
                    nc.vector.tensor_tensor(xr[:, k, :, :], ps_t[:, :, :].rearrange("p a (b c) -> p (a b) c", c=D),
                                            xg[:, k, :, :], ALU.add).then_inc(added[k], 1)
                    dve.wait_ge(added[k], count)
                else:
                    dve.wait_ge(x_loaded[k], count * (16 * len(RUNS)))
                for i in range(TILES):
                    last = nc.vector.bn_stats(stats[:, k, i, :], xin[:, k, i, :])
                last.then_inc(stats_done[k], 1)

            def mean_and_variance(count, k):
                dve.wait_ge(stats_done[k], count)
                nc.vector.memset(spare[:, :], 0.0)
                for i in range(TILES):
                    last = nc.vector.bn_aggr(mv[:, k, i, :], stats[:, k, i, :])
                last.then_inc(mv_done[k], 1)

            def normalise(count, k):
                dve.wait_ge(std_done[k], count)
                nc.vector.reciprocal(rstd[:, k, :], std[:, k, :]).then_inc(rstd_done[k], 1)
                dve.wait_ge(rstd_done[k], count)
                for i in range(TILES):
                    last = nc.vector.tensor_scalar(xn[:, k, i, :], xin[:, k, i, :], mv[:, k, i, 0:1],
                                                   rstd[:, k, i:i + 1], ALU.subtract, ALU.mult)
                last.then_inc(normed[k], 1)

            def copy_xt(count, k):
                dve.wait_ge(turned[k], count)
                nc.vector.tensor_copy(xt[:, k, 1, :], ps_t[:, 1, :]).then_inc(turned_out_v[k], 1)

            def gate(t, k, c):
                dve.wait_ge(sil_done[k][c], t + 1)
                nc.vector.scalar_tensor_tensor(gated[:, c, :], ps_h[:, 2 * (c % 2) + 1, :], cols[:, SB3 + c:SB3 + c + 1],
                                               sil[:, c % 2, :], ALU.add, ALU.mult).then_inc(gated_done[k][c], 1)

            def finish(count, k):
                dve.wait_ge(down_done[k], count)
                for fc in range(CK):
                    last = nc.vector.tensor_tensor(yt[:, fc, :].rearrange("p (j n) -> p j n", n=RUN),
                                                   ps_y[:, fc, :].rearrange("p (j n) -> p j n", n=RUN),
                                                   bias[:, fc, :, None].to_broadcast([P, EXPERTS, RUN]), ALU.add)
                last.then_inc(y_out[k], 1)

            def residual(count, stores, k):
                if att is None:
                    dve.wait_ge(xr_loaded[k], count * (16 * len(RUNS)))
                dve.wait_ge(back_done[k], count)
                if stores is not None:
                    dve.wait_ge(stored[k], stores * (16 * len(RUNS)))
                nc.vector.scalar_tensor_tensor(xo[:, k, :, :], ps_t[:, :, :].rearrange("p a (b c) -> p (a b) c", c=D),
                                               0.25, xr[:, k, :, :], ALU.mult, ALU.add).then_inc(res_done[k], 1)

            stats_of(1, 0)
            mean_and_variance(1, 0)
            dve.wait_ge(rows_turned, 1)
            nc.vector.tensor_copy(cols[:, :], ps_h[:, 0, 0:BIAS_ROWS]).then_inc(cols_set, 1)
            normalise(1, 0)
            dve.wait_ge(cols_set, 1)
            b2_cols = cols[:, B2:BIAS_ROWS].rearrange("p (e c) -> p c e", c=CK)[:, :, ::-1]
            nc.vector.tensor_scalar(sb2x[:, :], cols[:, SB2:SB2 + CK], 2.0, None, ALU.mult).then_inc(bias_steps, 1)
            nc.vector.tensor_tensor(bias2[:, :, 1:EXPERTS], b2_cols[:, :, 1:EXPERTS], b2_cols[:, :, 0:EXPERTS - 1],
                                    ALU.add).then_inc(bias_steps, 1)
            nc.vector.tensor_tensor(bias2[:, :, 0:1], b2_cols[:, :, 0:1], b2_cols[:, :, EXPERTS - 1:EXPERTS],
                                    ALU.add).then_inc(bias_steps, 1)
            dve.wait_ge(bias_steps, 3)
            nc.vector.tensor_tensor(bias[:, :, :], bias2[:, :, :], sb2x[:, :, None].to_broadcast([P, CK, EXPERTS]),
                                    ALU.add).then_inc(bias_steps, 1)
            dve.wait_ge(bias_steps, 4)
            copy_xt(1, 0)

            def turn(t, first, last):
                for k in range(2):
                    prev, nxt = k or not first, k == 0 or not last
                    if prev:
                        finish(before(t, k), 1 - k)
                    gate(t, k, 0)
                    gate(t, k, 1)
                    if prev:
                        if k:
                            residual(t + 1, None if first else t, 0)
                        else:
                            residual(t, t - 1 if last or not first else None, 1)
                    gate(t, k, 2)
                    gate(t, k, 3)
                    if nxt:
                        stats_of(after(t, k), 1 - k)
                        mean_and_variance(after(t, k), 1 - k)
                        normalise(after(t, k), 1 - k)
                        copy_xt(after(t, k), 1 - k)

            for_turns_ends(dve, turns, turn)
            finish(turns, 1)
            residual(turns, turns - 1, 1)

        @block.scalar
        def _(act):
            def deviation(count, k):
                act.wait_ge(mv_done[k], count)
                nc.scalar.activation(std[:, k, :], mv[:, k, :, 1], ACT.Sqrt, bias=eps[:, 0:1]).then_inc(std_done[k], 1)

            def copy_xt(count, k):
                act.wait_ge(turned[k], count)
                nc.scalar.activation(xt[:, k, 0, :], ps_t[:, 0, :], ACT.Copy).then_inc(turned_out_a[k], 1)

            def copy_at(count, k, multiplied):
                act.wait_ge(att_turned[k], count)
                if multiplied is not None:
                    act.wait_ge(projected[1 - k], multiplied)
                nc.scalar.activation(at[:, :, :], ps_t[:, :, :], ACT.Copy).then_inc(at_out[k], 1)

            act.wait_ge(const_set, 1)
            if att is not None:
                copy_at(1, 0, None)
            deviation(1, 0)
            copy_xt(1, 0)
            act.wait_ge(cols_set, 1)

            def turn(t, first, last):
                for k in range(2):
                    for c in range(HC):
                        act.wait_ge(up_done[k][c], t + 1)
                        if c >= 2:
                            act.wait_ge(gated_done[k][c - 2], t + 1)
                        elif k or not first:
                            act.wait_ge(gated_done[1 - k][c + 2], before(t, k))
                        nc.scalar.activation(sil[:, c % 2, :], ps_h[:, 2 * (c % 2), :], ACT.Silu,
                                             bias=cols[:, SB1 + c:SB1 + c + 1]).then_inc(sil_done[k][c], 1)
                        if c == 2 and att is not None and (k == 0 or not last):
                            copy_at(after(t, k), 1 - k, t + 1)
                    if k or not first:
                        act.wait_ge(down_done[1 - k], before(t, k))
                    for e in range(EXPERTS):
                        act.wait_ge(eup_done[k][e], t + 1)
                        for c in range(RC):
                            b = B1 + (EXPERTS - 1 - e) * RC + c
                            done = nc.scalar.activation(hidden[:, e, c, :], ps_h[:, e % 4, c * 2 * RUN:(c + 1) * 2 * RUN],
                                                        ACT.Gelu, bias=cols[:, b:b + 1])
                        done.then_inc(hidden_done[k][e], 1)
                    if k == 0 or not last:
                        deviation(after(t, k), 1 - k)
                        copy_xt(after(t, k), 1 - k)

            for_turns_ends(act, turns, turn)

        @block.tensor
        def _(pe):
            pe.wait_ge(ident_ready, 1)
            pe.wait_ge(rows_loaded, 16 * 5)
            nc.tensor.transpose(ps_h[:, 0, 0:BIAS_ROWS], rows[:, :], ident[0:BIAS_ROWS, 0:BIAS_ROWS]).then_inc(rows_turned, 1)

            def turn_att(count, k):
                pe.wait_ge(att_loaded[k], count * (16 * len(RUNS)))
                for i in range(TILES):
                    for ck in range(CK):
                        last = nc.tensor.transpose(ps_t[:, ck, i * P:(i + 1) * P], ag[:, k, i, ck * P:(ck + 1) * P],
                                                   ident[:, :])
                last.then_inc(att_turned[k], 1)

            def project(count, k):
                pe.wait_ge(at_out[k], count)
                for i in range(TILES):
                    for ck in range(CK):
                        last = nc.tensor.matmul(ps_t[:, i // 2, (i % 2) * D:(i % 2 + 1) * D],
                                                at[:, ck, i * P:(i + 1) * P], wo_sb[:, ck, :],
                                                start=ck == 0, stop=ck == CK - 1)
                last.then_inc(projected[k], 1)

            def turn_in(count, k):
                pe.wait_ge(normed[k], count)
                for i in range(TILES):
                    for ck in range(CK):
                        last = nc.tensor.transpose(ps_t[:, ck, i * P:(i + 1) * P], xn[:, k, i, ck * P:(ck + 1) * P],
                                                   ident[:, :])
                last.then_inc(turned[k], 1)

            def up_shared(t, k, c, first):
                if c < 2:
                    for e in (4 + 2 * c, 5 + 2 * c):
                        if k or not first:
                            pe.wait_ge(hidden_done[1 - k][e], before(t, k))
                else:
                    pe.wait_ge(gated_done[k][c - 2], t + 1)
                for n, w in enumerate((sw1_sb, sw3_sb)):
                    for ck in range(CK):
                        last = nc.tensor.matmul(ps_h[:, 2 * (c % 2) + n, :], w[:, ck, c * P:(c + 1) * P],
                                                xt[:, k, ck, :], start=ck == 0, stop=ck == CK - 1)
                last.then_inc(up_done[k][c], 1)

            def up_expert(t, k, e):
                if e < 4:
                    pe.wait_ge(gated_done[k][2 + e // 2], t + 1)
                else:
                    pe.wait_ge(hidden_done[k][e - 4], t + 1)
                for c in range(RC):
                    for ck in range(CK):
                        last = nc.tensor.matmul(ps_h[:, e % 4, c * 2 * RUN:(c + 1) * 2 * RUN],
                                                w1_sb[:, EXPERTS - 1 - e, ck, c * P:(c + 1) * P], pair(xt[:, k, ck, :], e),
                                                start=ck == 0, stop=ck == CK - 1)
                last.then_inc(eup_done[k][e], 1)

            def down_shared(k):
                for fc in range(CK):
                    for c in range(HC):
                        nc.tensor.matmul(ps_y[:, fc, :], sw2_sb[:, c, fc * P:(fc + 1) * P], gated[:, c, :],
                                         start=c == 0, stop=False, skip_group_check=True)

            def down_experts(t, k):
                for e in range(EXPERTS):
                    pe.wait_ge(hidden_done[k][e], t + 1)
                    for fc in range(CK):
                        for c in range(RC):
                            last = nc.tensor.matmul(pair(ps_y[:, fc, :], e), w2_sb[:, EXPERTS - 1 - e, c, fc * P:(fc + 1) * P],
                                                    hidden[:, e, c, :], start=False,
                                                    stop=e == EXPERTS - 1 and c == RC - 1, skip_group_check=True)
                last.then_inc(down_done[k], 1)

            def turn_back(count, k):
                pe.wait_ge(y_out[k], count)
                for i in range(TILES):
                    for fc in range(CK):
                        last = nc.tensor.transpose(ps_t[:, i // 2, (i % 2) * D + fc * P:(i % 2) * D + (fc + 1) * P],
                                                   yt[:, fc, i * P:(i + 1) * P], ident[:, :])
                last.then_inc(back_done[k], 1)

            if att is not None:
                turn_att(1, 0)
                pe.wait_ge(wo_loaded, 16)
                project(1, 0)
            turn_in(1, 0)
            pe.wait_ge(cols_set, 1)
            pe.wait_ge(up_loaded, 32)

            def turn(t, first, last):
                for k in range(2):
                    nxt = k == 0 or not last
                    pe.wait_ge(turned_out_a[k], t + 1)
                    pe.wait_ge(turned_out_v[k], t + 1)
                    for c in range(HC):
                        up_shared(t, k, c, first)
                        if c == 1 and (k or not first):
                            turn_back(before(t, k), 1 - k)
                        if c == 2 and att is not None and nxt:
                            if k or not first:
                                pe.wait_ge(res_done[1 - k], before(t, k))
                            turn_att(after(t, k), 1 - k)
                    if first and k == 0:
                        pe.wait_ge(w1_loaded, 16)
                    for e in range(EXPERTS):
                        up_expert(t, k, e)
                        if e == 0 and att is not None and nxt:
                            project(after(t, k), 1 - k)
                    if first and k == 0:
                        pe.wait_ge(doubled, 1)
                        pe.wait_ge(down_loaded, 16)
                    down_shared(k)
                    if nxt:
                        turn_in(after(t, k), 1 - k)
                    down_experts(t, k)

            for_turns_ends(pe, turns, turn)
            turn_back(turns, 1)


def window_stage(nc, name, x, out, qk, v, wo_t, bo):
    turns = NTOK // GROUP // 2
    HG = 4
    PER_TILE = H // HG
    ITEMS = 2 * TILES * PER_TILE
    HALF = P // 2
    WIN = GROUP // HALF
    KEYS = GROUP + WINDOW
    DV = DH + 1
    CT = 32
    with Stage(nc, name) as s:
        ident, zeroed, ident_ready = s.sb("ident", [P, P]), s.sem("zeroed"), s.sem("ident_ready")
        identb, zeroedb = s.sb("identb", [P, P], BF16), s.sem("zeroedb")
        mask = s.sb("mask", [P, HG, P], BF16)
        mask_steps = s.sem("mask_steps")
        wo_sb, bo_sb = s.sb("wo", [P, CK, D]), s.sb("bo", [P, D])
        w_loaded = s.sem("w_loaded")
        qs = s.sb("qs", [STACK, 2, H, GROUP], BF16)
        ks = s.sb("ks", [STACK, 2, H, KEYS], BF16)
        vh = s.sb("vh", [P, 2, WIN, H * DV])
        xg = s.sb("xg", [P, 2, TILES, D])
        xb = s.sb("xb", [P, 2, TILES, D])
        sc = s.sb("sc", [P, 2, HG, P])
        pr = s.sb("pr", [P, 2, HG, P])
        pt = s.sb("pt", [P, 2, HG, P])
        ot = s.sb("ot", [P, 2, P])
        top = s.sb("top", [P, 2, HG])
        rden = s.sb("rden", [P, 2, HG])
        att = s.sb("att", [P, 2, D])
        attt = s.sb("attt", [P, CK, P])
        xo = s.sb("xo", [P, 2, D])
        ps_s = s.ps("ps_s", [P, 2, HG, P])
        ps_p = s.ps("ps_p", [P, 2, HG, P])
        ps_o = s.ps("ps_o", [P, GROUP])
        ps_b = s.ps("ps_b", [P, GROUP])
        ps_w = s.ps("ps_w", [P, GROUP])
        ps_y = s.ps("ps_y", [P, GROUP])
        qk_loaded, v_loaded, x_loaded = (s.sems(n, 2) for n in ("qk_loaded", "v_loaded", "x_loaded"))
        xb_ready, o_cleared = s.sems("xb_ready", 2), s.sem("o_cleared")
        (scored, topped, less_top, expd, p_turned, p_out, pv_done, o_out, o_back, inverted, att_done) = (
            s.sem(n) for n in ("scored", "topped", "less_top", "expd", "p_turned", "p_out", "pv_done", "o_out",
                               "o_back", "inverted", "att_done"))
        w_turned, w_out, w_done, x_out = (s.sem(n) for n in ("w_turned", "w_out", "w_done", "x_out"))
        x_stored = s.sems("x_stored", 2)
        block = s.block()
        xv = x.rearrange("(u k i p) c -> u k p i c", p=P, i=TILES, k=2)
        ov = out.rearrange("(u k i p) c -> u k p i c", p=P, i=TILES, k=2)
        TT = 2 * TILES

        def items(t, n):
            return (t + n // ITEMS) * ITEMS + (n % ITEMS + 1)

        def tiles(t, i):
            return (t + i // TT) * TT + (i % TT + 1)

        def group_turns(t, i):
            return t + i // TT + 1

        def emit(engine, item_steps, tile_steps, do):
            end = max(lag for _, lag in tuple(item_steps) + tuple(tile_steps))

            def turn(t, first, last):
                valid = lambda n: (n >= 0 or not first) and (n < ITEMS or not last)
                for n in range(ITEMS + (end if last else 0)):
                    for what, lag in item_steps:
                        if valid(n - lag):
                            do[what](t, n - lag, valid)
                    for what, lag in tile_steps:
                        m = n - lag
                        if m % PER_TILE == PER_TILE - 1 and valid(m):
                            do[what](t, m // PER_TILE, lambda i: valid(i * PER_TILE))

            for_turns_ends(engine, turns, turn)

        def u_batch(u):
            return u // 2

        def u_col(u):
            return (u % 2) * (2 * GROUP)

        @block.sync
        def _(sp):
            sp.dma_start(wo_sb[:, :, :], wo_t.rearrange("(k p) f -> p k f", p=P)).then_inc(w_loaded, 16)
            sp.dma_start(bo_sb[:, :], bass.AP(bo.tensor, bo.offset, [[0, P], [1, D]])).then_inc(w_loaded, 16)

            def load_q_k_x(k, u):
                batch, col = u_batch(u), u_col(u)
                for n in range(len(LEFT)):
                    sp.dma_start(qs[n * DH:(n + 1) * DH, k, :, :],
                                 qk[0, LEFT[n], :, batch, bass.ds(col + (PAD + k * GROUP), GROUP)]
                                 .rearrange("(h d) c -> d h c", d=DH)).then_inc(qk_loaded[k], 16)
                    sp.dma_start(ks[n * DH:(n + 1) * DH, k, :, :],
                                 qk[1, RIGHT[n], :, batch, bass.ds(col + k * GROUP, KEYS)]
                                 .rearrange("(h d) c -> d h c", d=DH)).then_inc(qk_loaded[k], 16)
                sp.dma_start(xg[:, k, :, :], xv[u, k, :, :, :]).then_inc(x_loaded[k], 16)

            def load_v(k, u):
                batch, col = u_batch(u), u_col(u)
                for odd in range(2):
                    sp.dma_start(vh[:, k, odd::2, :],
                                 v[batch, bass.ds(col + (k * GROUP + odd * HALF), GROUP), :]
                                 .rearrange("(w p) c -> p w c", p=P)).then_inc(v_loaded[k], 16)

            for k in range(2):
                load_q_k_x(k, 0)
                load_v(k, 0)

            def turn(t, last):
                tiles_out = [sp.snap(t * TT + i + 1) for i in range(TT)]
                ahead = None if last else sp.snap(t + 1)
                for i in range(TT):
                    sp.wait_ge(x_out, tiles_out[i])
                    sp.dma_start(ov[t, i // TILES, :, i % TILES, :], xo[:, i % 2, :])\
                        .then_inc(x_stored[i % 2], 16)
                    if i % TILES == TILES - 1 and not last:
                        k = i // TILES
                        load_q_k_x(k, ahead)
                        load_v(k, ahead)

            turn(0, False)
            with sp.Fori(1, turns - 1) as t:
                turn(t, False)
            turn(turns - 1, True)
            for slot in range(2):
                sp.wait_ge(x_stored[slot], 16 * turns * TILES)

        @block.gpsimd
        def _(pool):
            make_identity(nc, pool, ident, zeroed, ident_ready)
            make_identity(nc, pool, identb, zeroedb, ident_ready)
            nc.gpsimd.memset(mask[:, :, :], 0.0).then_inc(mask_steps, 1)
            step = 1
            for half in range(2):
                for base, sign in ((0, 1), (WINDOW - 1, -1)):
                    m = mask[half * HALF:(half + 1) * HALF, :, :]
                    pool.wait_ge(mask_steps, step)
                    nc.gpsimd.affine_select(out=m, in_=m, compare_op=ALU.is_ge, fill=MASKED, base=base,
                                            pattern=[[0, HG], [sign, P]], channel_multiplier=-sign)\
                        .then_inc(mask_steps, 1)
                    step += 1
            pool.wait_ge(mask_steps, step)
            pool.wait_ge(w_loaded, 32)

            def turn(t, first, last):
                for k in range(2):
                    pool.wait_ge(x_loaded[k], t * 16 + 16)
                    if not first:
                        pool.wait_ge(x_out, tiles(t, (k + 1) * TILES - 1 - TT))
                    nc.gpsimd.tensor_tensor(xb[:, k, :, :], xg[:, k, :, :],
                                            bo_sb[:, None, :].to_broadcast([P, TILES, D]), ALU.add)\
                        .then_inc(xb_ready[k], 1)

            for_turns_ends(pool, turns, turn)

        @block.vector
        def _(dve):
            nc.vector.memset(ps_o[:, 0:P], 0.0).then_inc(o_cleared, 1)

            def maximum(t, n, valid):
                dve.wait_ge(scored, items(t, n))
                nc.vector.tensor_reduce(top[:, n % 2, :], ps_s[:, n % 2, :, :], AX.X, ALU.max).then_inc(topped, 1)
                dve.wait_ge(topped, items(t, n))
                if valid(n - 2):
                    dve.wait_ge(expd, items(t, n - 2))
                nc.vector.tensor_tensor(sc[:, n % 2, :, :], ps_s[:, n % 2, :, :],
                                        top[:, n % 2, :, None].to_broadcast([P, HG, P]), ALU.subtract)\
                    .then_inc(less_top, 1)

            def weigh(t, n, valid):
                i, hg = n // PER_TILE, n % PER_TILE
                view = ps_b[:, 0:P].rearrange("p (h d) -> p h d", d=CT)
                dve.wait_ge(o_back, items(t, n))
                nc.vector.reciprocal(rden[:, n % 2, :], view[:, :, DH]).then_inc(inverted, 1)
                dve.wait_ge(inverted, items(t, n))
                if hg == 0 and valid(n - 2 * PER_TILE):
                    dve.wait_ge(w_turned, tiles(t, i - 2))
                nc.vector.tensor_tensor(att[:, i % 2, hg * HG * DH:(hg + 1) * HG * DH]
                                        .rearrange("p (h d) -> p h d", d=DH), view[:, :, 0:DH],
                                        rden[:, n % 2, :, None].to_broadcast([P, HG, DH]), ALU.mult)\
                    .then_inc(att_done, 1)

            def add_x(t, i, valid):
                dve.wait_ge(w_done, tiles(t, i))
                dve.wait_ge(xb_ready[(i // TILES) % 2], group_turns(t, i))
                if valid(i - 2):
                    dve.wait_ge(x_stored[i % 2], (t + i // TT) * (16 * TT // 2) + (i % TT) // 2 * 16)
                nc.vector.tensor_tensor(xo[:, i % 2, :], ps_y[:, 0:D], xb[:, (i // TILES) % 2, i % TILES, :], ALU.add)\
                    .then_inc(x_out, 1)

            emit(dve, (("max", 0), ("weigh", 4)), (("add", 6),), {"max": maximum, "weigh": weigh, "add": add_x})

        @block.scalar
        def _(act):
            def exp(t, n, valid):
                act.wait_ge(less_top, items(t, n))
                if valid(n - 2):
                    act.wait_ge(p_turned, items(t, n - 2))
                nc.scalar.activation(pr[:, n % 2, :, :], sc[:, n % 2, :, :], ACT.Exp).then_inc(expd, 1)

            def copy_p(t, n, valid):
                act.wait_ge(p_turned, items(t, n))
                if valid(n - 2):
                    act.wait_ge(pv_done, items(t, n - 2))
                nc.scalar.activation(pt[:, n % 2, :, :], ps_p[:, n % 2, :, :], ACT.Copy).then_inc(p_out, 1)

            def copy_o(t, n, valid):
                act.wait_ge(pv_done, items(t, n))
                if valid(n - 2):
                    act.wait_ge(o_back, items(t, n - 2))
                nc.scalar.activation(ot[:, n % 2, :], ps_o[:, 0:P], ACT.Copy).then_inc(o_out, 1)

            def copy_att(t, i, valid):
                act.wait_ge(w_turned, tiles(t, i))
                if valid(i - 1):
                    act.wait_ge(w_done, tiles(t, i - 1))
                nc.scalar.activation(attt[:, :, :], ps_w[:, 0:D].rearrange("p (k q) -> p k q", k=CK), ACT.Copy)\
                    .then_inc(w_out, 1)

            emit(act, (("copy_p", 2), ("copy_o", 3), ("exp", 0)), (("copy_att", 5),),
                 {"exp": exp, "copy_p": copy_p, "copy_o": copy_o, "copy_att": copy_att})

        @block.tensor
        def _(pe):
            pe.wait_ge(ident_ready, 2)
            pe.wait_ge(mask_steps, 5)
            pe.wait_ge(o_cleared, 1)
            pe.wait_ge(w_loaded, 32)
            n_qk = 16 * 2 * len(LEFT)

            def score(t, n, valid):
                i, hg = n // PER_TILE, n % PER_TILE
                k = i // TILES
                if n % (TILES * PER_TILE) == 0:
                    pe.wait_ge(qk_loaded[k], t * n_qk + n_qk)
                if valid(n - 2):
                    pe.wait_ge(less_top, items(t, n - 2))
                nc.tensor.matmul(ps_s[:, n % 2, :, :], identb[:, :], mask[:, :, :], start=True, stop=False,
                                 skip_group_check=True)
                for h in range(HG):
                    for half in range(2):
                        q0 = (i % TILES) * P + half * HALF
                        last = nc.tensor.matmul(ps_s[half * HALF:(half + 1) * HALF, n % 2, h, :],
                                                qs[:, k, hg * HG + h, q0:q0 + HALF],
                                                ks[:, k, hg * HG + h, q0:q0 + P],
                                                start=False, stop=h == HG - 1, skip_group_check=True)
                last.then_inc(scored, 1)

            def turn_p(t, n, valid):
                pe.wait_ge(expd, items(t, n))
                if valid(n - 2):
                    pe.wait_ge(p_out, items(t, n - 2))
                for h in range(HG):
                    last = nc.tensor.transpose(ps_p[:, n % 2, h, :], pr[:, n % 2, h, :], ident[:, :])
                last.then_inc(p_turned, 1)

            def weigh_v(t, n, valid):
                i, hg = n // PER_TILE, n % PER_TILE
                k = (i // TILES) % 2
                pe.wait_ge(p_out, items(t, n))
                if n % (TILES * PER_TILE) == 0:
                    pe.wait_ge(v_loaded[k], group_turns(t, i) * 32)
                if valid(n - 1):
                    pe.wait_ge(o_out, items(t, n - 1))
                for half in range(2):
                    for h in range(HG):
                        head = hg * HG + h
                        last = nc.tensor.matmul(ps_o[h * CT:h * CT + DV, half * HALF:(half + 1) * HALF],
                                                vh[:, k, 2 * (i % TILES) + half, head * DV:(head + 1) * DV],
                                                pt[:, n % 2, h, half * HALF:(half + 1) * HALF],
                                                start=True, stop=True)
                last.then_inc(pv_done, 1)

            def turn_o(t, n, valid):
                pe.wait_ge(o_out, items(t, n))
                if valid(n - 1):
                    pe.wait_ge(att_done, items(t, n - 1))
                nc.tensor.transpose(ps_b[:, 0:P], ot[:, n % 2, :], ident[:, :]).then_inc(o_back, 1)

            def turn_att(t, i, valid):
                pe.wait_ge(att_done, items(t, i * PER_TILE + PER_TILE - 1))
                if valid(i - 1):
                    pe.wait_ge(w_out, tiles(t, i - 1))
                for ck in range(CK):
                    last = nc.tensor.transpose(ps_w[:, ck * P:(ck + 1) * P], att[:, i % 2, ck * P:(ck + 1) * P],
                                               ident[:, :])
                last.then_inc(w_turned, 1)

            def project(t, i, valid):
                pe.wait_ge(w_out, tiles(t, i))
                if valid(i - 1):
                    pe.wait_ge(x_out, tiles(t, i - 1))
                for ck in range(CK):
                    last = nc.tensor.matmul(ps_y[:, 0:D], attt[:, ck, :], wo_sb[:, ck, :],
                                            start=ck == 0, stop=ck == CK - 1)
                last.then_inc(w_done, 1)

            emit(pe, (("score", 0), ("turn_p", 2), ("weigh_v", 3), ("turn_o", 4)), (("turn_att", 5), ("project", 6)),
                 {"score": score, "turn_p": turn_p, "weigh_v": weigh_v, "turn_o": turn_o,
                  "turn_att": turn_att, "project": project})


SHIFT_SLOTS = 8
LAGS = dict(relate=-6, shift=-4, exp=1, store=2, turn=3, load=3, turn_w=6,
            split=1, spread=2, far=3, weigh=5, copy_o=9, turn_o=11, combine=11)

VECTOR_TURNED = (0, 1, 2, 3, 4, 5, 6, 7)
VECTOR_W = (2, 3, 5, 13)
VECTOR_O = (0, 4)
VECTOR_SPREAD = (1, 5)


def causal_stage(nc, name, att, qk, v, pek, pev, bias_rows, prob_rows):
    NEAR = 3 * P
    DV = DH + 1
    UNITS_HEAD = L // P
    HEADS = 2
    UNITS = HEADS * UNITS_HEAD
    turns = B * H // HEADS
    SLOTS = SHIFT_SLOTS
    GPH = UNITS_HEAD // 4
    GROUPS = UNITS // 4
    CT = 32
    MAX_ROW = STACK
    ROWS = STACK + 3
    LEAD, TAIL = -LAGS["relate"], LAGS["combine"] + 3

    def far_chunks(i):
        keys = max(0, (i - 2) * P)
        return [(c, min(GROUP, keys - c)) for c in range(0, keys, GROUP)]

    def far_blocks(gi):
        return [(b, max(0, b - 4 * gi + 3) * P) for b in range(4 * gi + 1)]

    def quarter(items, s):
        return items[len(items) * s // 4:len(items) * (s + 1) // 4]

    S_BANKS, F_BANKS = 3, 2
    score_at, far_at, S_USES, F_USES = {}, {}, [0] * S_BANKS, [0] * F_BANKS
    for m in range(UNITS):
        for c in range(len(far_chunks(m % UNITS_HEAD)) + 1):
            bank = sum(S_USES) % S_BANKS
            score_at[m, c] = bank, S_USES[bank]
            S_USES[bank] += 1
    for g in range(GROUPS):
        for b, _ in far_blocks(g % GPH):
            bank = sum(F_USES) % F_BANKS
            far_at[g, b] = bank, F_USES[bank]
            F_USES[bank] += 1
    PT_AT = [sum(4 * j + 4 for j in range(gi)) for gi in range(GPH + 1)]

    def use(t, m):
        return t * (UNITS // SLOTS) + (m // SLOTS + 1)

    def units(t, m):
        return (t + m // UNITS) * UNITS + (m % UNITS + 1)

    def groups(t, g):
        return (t + g // GROUPS) * GROUPS + (g % GROUPS + 1)

    def head_of(g):
        return (g // GPH) % HEADS

    def head_turns(t, g):
        return t + g // GROUPS

    def group_count(t, g):
        return head_turns(t, g) * GPH + (g % GPH + 1)

    def score_bank(t, m, c):
        bank, n = score_at[m % UNITS, c]
        return bank, (t + m // UNITS) * S_USES[bank] + (n + 1)

    def far_bank(t, g, b):
        bank, n = far_at[g % GROUPS, b]
        return bank, (t + g // GROUPS) * F_USES[bank] + (n + 1)

    def emit(engine, steps):
        def turn(t, first, last):
            for n in range(-LEAD if first else 0, UNITS + (TAIL if last else 0)):
                steps(t, n, lambda m: (m >= 0 or not first) and (m < UNITS or not last))
        turn(0, True, False)
        with engine.Fori(1, turns - 1) as t:
            turn(t, False, False)
        turn(turns - 1, False, True)

    def group_at(n, what, valid, part=0):
        m = n - LAGS[what] - part
        return m // 4 if m % 4 == 3 and valid(m) else None

    with Stage(nc, name) as s:
        ident, zeroed, ident_ready = s.sb("ident", [P, P]), s.sem("zeroed"), s.sem("ident_ready")
        ident_b = s.sb("ident_b", [P, P], BF16)
        pek_in, pev_in = s.sb("pek_in", [P, 2, DH]), s.sb("pev_in", [P, 2, DH])
        pek0, pev0 = s.sb("pek0", [P, DH]), s.sb("pev0", [P, DH])
        pek_d, pev_d = s.sb("pek_d", [P, 2, DH]), s.sb("pev_d", [P, 2, DV])
        pek_parts, pek_rest = s.sb("pek_parts", [DH, 3, MAX_REL], BF16), s.sb("pek_rest", [DH, MAX_REL])
        pek_s = s.sb("pek_s", [STACK, MAX_REL], BF16)
        edge0, edge1 = s.sb("edge0", [P, P]), s.sb("edge1", [P, P])
        spare = s.sb("spare", [P, 1])
        qs, ks = s.sb("qs", [ROWS, HEADS, L], BF16), s.sb("ks", [ROWS, HEADS, L], BF16)
        vh = s.sb("vh", [P, HEADS, UNITS_HEAD, DV])
        r_sb = s.sb("r_sb", [P, SLOTS, MAX_REL])
        bias = s.sb("bias", [P, SLOTS, NEAR])
        p = s.sb("p", [P, SLOTS, NEAR])
        w = s.sb("w", [P, SLOTS, MAX_REL])
        top = s.sb("top", [P, 2, 5])
        negtop = s.sb("negtop", [P, SLOTS])
        neg_parts, neg_rest = s.sb("neg_parts", [P, 2, 4, 3], BF16), s.sb("neg_rest", [P, 4])
        rden = s.sb("rden", [P, 2, 4])
        pt = s.sb("pt", [P, PT_AT[GPH], GROUP])
        wt = s.sb("wt", [P, GPH, 2, GROUP])
        ot = s.sb("ot", [P, GROUP])
        osum = s.sb("osum", [P, 2, 4, DV])
        oh = s.sb("oh", [P, HEADS, UNITS_HEAD, DH])
        ps_rw = s.ps("ps_rw", [P, 2, MAX_REL])
        ps_s = s.ps("ps_s", [P, S_BANKS, GROUP])
        ps_f = s.ps("ps_f", [P, F_BANKS, GROUP])
        ps_p = s.ps("ps_p", [P, GROUP])
        ps_o = s.ps("ps_o", [P, GROUP])

        c_loaded, setup, pek_turned, edges_set, edges_stored, stacked = (
            s.sem(n) for n in ("c_loaded", "setup", "pek_turned", "edges_set", "edges_stored", "stacked"))
        q_loaded, k_loaded, v_loaded, head_stored = (s.sems(n, HEADS) for n in ("q_loaded", "k_loaded", "v_loaded", "head_stored"))
        r_out, r_stored, bias_loaded, expd, p_stored, w_loaded = (
            s.sems(n, SLOTS) for n in ("r_out", "r_stored", "bias_loaded", "expd", "p_stored", "w_loaded"))
        scored, score_out = s.sems("scored", S_BANKS), s.sems("score_out", S_BANKS)
        far_done, far_out = s.sems("far_done", F_BANKS), s.sems("far_out", F_BANKS)
        w_turned = s.sems("w_turned", SLOTS)
        pv_done, o_done = s.sems("pv_done", HEADS), s.sems("o_done", HEADS)
        (r_done, neg_done, neg_split, spread_done, spread_out, turned, turned_out, w_out, o_out, o_back, o_summed,
         inverted) = (s.sem(n) for n in ("r_done", "neg_done", "neg_split", "spread_done", "spread_out", "turned",
                                         "turned_out", "w_out", "o_out", "o_back", "o_summed", "inverted"))
        att_v = att.rearrange("(b i p) (h d) -> b p i h d", b=B, p=P, d=DH)
        passed = s.sem("passed")
        SIDE_DMAS = len(LEFT_RUNS)
        part_pitch = D * B * L
        block = s.block()

        def group_read(engine, t, g, valid):
            if valid(4 * (g - GPH)):
                engine.wait_ge(pv_done[head_of(g - GPH)], group_count(t, g - GPH))

        def copy_turned(engine, copy, t, m, valid):
            i, g = m % UNITS_HEAD, m // 4
            blocks = min(i + 1, 3)
            group_read(engine, t, g, valid)
            engine.wait_ge(turned, units(t, m))
            b0 = PT_AT[g % GPH] + i + 1 - blocks
            copy(pt[:, b0:b0 + blocks, (i % 4) * P:(i % 4 + 1) * P], ps_p[:, 0:blocks * P].rearrange("p (b q) -> p b q", q=P))\
                .then_inc(turned_out, 1)

        def copy_w(engine, copy, t, m, valid):
            g = m // 4
            group_read(engine, t, g, valid)
            copy(wt[:, g % GPH, :, (m % 4) * P:(m % 4 + 1) * P], ps_rw[:, 1, :].rearrange("p (k q) -> p k q", k=2))\
                .then_inc(w_out, 1)

        def copy_spread(engine, copy, t, g):
            engine.wait_ge(spread_done, groups(t, g))
            gi = g % GPH
            copy(qs[MAX_ROW:ROWS, head_of(g), gi * GROUP:(gi + 1) * GROUP], ps_p[MAX_ROW:ROWS, :]).then_inc(spread_out, 1)

        def copy_o(engine, copy, t, g):
            engine.wait_ge(pv_done[head_of(g)], group_count(t, g))
            copy(ot[:, :], ps_o[:, :]).then_inc(o_out, 1)

        @block.sync
        def _(sp):
            sp.dma_start(pek_in[:, :, :], pek[1:1 + MAX_REL, :].rearrange("(k p) d -> p k d", p=P)).then_inc(c_loaded, 16)
            sp.dma_start(pev_in[:, :, :], pev[1:1 + MAX_REL, :].rearrange("(k p) d -> p k d", p=P)).then_inc(c_loaded, 16)
            sp.dma_start(pek0[:, :], bass.AP(pek.tensor, pek.offset, [[0, P], [1, DH]])).then_inc(c_loaded, 16)
            sp.dma_start(pev0[:, :], bass.AP(pev.tensor, pev.offset, [[0, P], [1, DH]])).then_inc(c_loaded, 16)

            def load_v(k, batch, h):
                sp.dma_start(vh[:, k, :, :], v[batch, h, :, :, :]).then_inc(v_loaded[k], 16)

            def load_rows(part, k, batch, h):
                to, (n, first, copies, step) = (qs, ks)[part // 3], (LEFT_RUNS + RIGHT_RUNS)[part]
                src = qk[part // 3, first, bass.ds(h * DH, DH), batch, :]
                sp.dma_start(to[n * DH:(n + copies) * DH, k, :],
                             bass.AP(src.tensor, src.offset, [[step * part_pitch, copies], list(src.ap[0]), [1, L]]))\
                    .then_inc((q_loaded if part < 3 else k_loaded)[k], 16)

            for part in range(6):
                load_rows(part, 0, 0, 0)
            sp.wait_ge(setup, 5)
            for n in range(len(LEFT)):
                sp.dma_start(pek_s[n * DH:(n + 1) * DH, :], pek_parts[:, RIGHT[n], :]).then_inc(stacked, 16)
            sp.wait_ge(edges_set, 2)
            for edge, at in ((edge0, 0), (edge1, NEAR)):
                sp.dma_start(bias_rows[:, :, at:at + P].rearrange("s p c -> p s c"),
                             edge[:, None, :].to_broadcast([P, SLOTS, P])).then_inc(edges_stored, 16)
            load_v(0, 0, 0)
            for part in range(6):
                load_rows(part, 1, 0, 1)
            load_v(1, 0, 1)
            sp.wait_ge(edges_stored, 16 * 2)

            def turn(t, first, last):
                low, high = (0 if first else -3), UNITS // SLOTS + 3
                cnt = {j: t * (UNITS // SLOTS) + j for j in range(low, high)}
                cnt16 = {j: t * (16 * UNITS // SLOTS) + 16 * j for j in range(low, high)}

                def wait_both(*pairs):
                    values = [v if isinstance(v, int) else sp.to_reg(v) for _, v in pairs]
                    for (what, _), value in zip(pairs, values):
                        sp.wait_ge(what, value)

                nxt = None if last else sp.snap(t + 1)
                if not last:
                    batch_n, head_n = sp.snap(nxt // (H // HEADS)), sp.snap((nxt % (H // HEADS)) * HEADS)
                batch, head = sp.snap(t // (H // HEADS)), sp.snap((t % (H // HEADS)) * HEADS)

                def store_r(m):
                    sl, j = m % SLOTS, m // SLOTS
                    reused = not (first and m < SLOTS)
                    wait_both((r_out[sl], cnt[j + 1]), *[(bias_loaded[sl], cnt16[j])] * reused)
                    sp.dma_start(bias_rows[sl, :, P:P + MAX_REL], r_sb[:, sl, :]).then_inc(r_stored[sl], 16)

                def load_bias(m):
                    sl, j, i = m % SLOTS, m // SLOTS, m % UNITS_HEAD
                    skip = NEAR - min(i + 1, 3) * P
                    rows = bias_rows[sl, :, :]
                    reused = not (first and m < SLOTS)
                    wait_both((r_stored[sl], cnt16[j + 1]), *[(expd[sl], cnt[j])] * reused)
                    sp.dma_start(bias[:, sl, skip:], bass.AP(rows.tensor, rows.offset + P - 1 + skip,
                                                            [[4 * P - 1, P], [1, NEAR - skip]])).then_inc(bias_loaded[sl], 16)

                def store_p(m):
                    sl, j, i = m % SLOTS, m // SLOTS, m % UNITS_HEAD
                    reused = not (first and m < SLOTS)
                    wait_both((expd[sl], cnt[j + 1]), *[(w_loaded[sl], cnt16[j])] * reused)
                    sp.dma_start(prob_rows[sl, :, :], p[:, sl, :]).then_inc(p_stored[sl], 16)

                def load_w(m):
                    sl, j = m % SLOTS, m // SLOTS
                    rows = prob_rows[sl, :, :]
                    reused = not (first and m < SLOTS)
                    wait_both((p_stored[sl], cnt16[j + 1]), *[(w_turned[sl], cnt[j])] * reused)
                    sp.dma_start(w[:, sl, :], bass.AP(rows.tensor, rows.offset + 1, [[NEAR + 1, P], [1, MAX_REL]]))\
                        .then_inc(w_loaded[sl], 16)

                todo = {"store_r": store_r, "load_bias": load_bias, "store_p": store_p, "load_w": load_w}

                def head_over(m):
                    k = (m // UNITS_HEAD) % HEADS
                    prev = m < 0
                    wait_both((o_done[k], head_groups[0 if prev else 1]))
                    sp.sem_inc(passed, 1)
                    bb, hh = (batch_p, head_p) if prev else (batch, head)
                    sp.dma_start(att_v[bb, :, :, hh + k, :], oh[:, k, :, :]).then_inc(head_stored[k], 16)

                head_groups = {0: sp.snap(t * GPH), 1: sp.snap(t * GPH + GPH)}
                if not first:
                    batch_p = sp.snap((t - 1) // (H // HEADS))
                    head_p = sp.snap(((t - 1) % (H // HEADS)) * HEADS)
                for n in range(-LEAD if first else 0, UNITS + (TAIL + 3 if last else 0)):
                    for what, step in (("store_r", "relate"), ("load_bias", "shift"), ("store_p", "store"), ("load_w", "load")):
                        m = n - LAGS[step]
                        if (m >= 0 or not first) and (m < UNITS or not last):
                            todo[what](m)
                    m = n - LAGS["combine"] - 2
                    if m % UNITS_HEAD == UNITS_HEAD - 1 and (m >= 0 or not first) and (m < UNITS or not last):
                        head_over(m)
                    for part in range(4):
                        m = n - LAGS["far"] - 4 - part
                        if m % UNITS_HEAD == UNITS_HEAD - 1 and ((0 <= m < UNITS and not last) or (m < 0 and not first)):
                            prev = m < 0
                            k = HEADS - 1 if prev else m // UNITS_HEAD
                            if part == 0:
                                over = []
                                for b in (4 * (GPH - 1) - 1, 4 * (GPH - 1)):
                                    bank, place = far_at[k * GPH + GPH - 1, b]
                                    over.append((far_done[bank], (t - 1 if prev else t) * F_USES[bank] + (place + 1)))
                                wait_both(*over)
                                sp.sem_inc(passed, 1)
                            for x in ((0, 1, 2), (3,), (4,), (5,))[part]:
                                load_rows(x, k, *((batch, head + k) if prev else (batch_n, head_n + k)))
                    m = n - LAGS["weigh"] - 4
                    if m % UNITS_HEAD == UNITS_HEAD - 1 and ((0 <= m < UNITS and not last) or (m < 0 and not first)):
                        prev = m < 0
                        k = HEADS - 1 if prev else m // UNITS_HEAD
                        wait_both((pv_done[k], head_groups[0 if prev else 1]))
                        sp.sem_inc(passed, 1)
                        load_v(k, *((batch, head + k) if prev else (batch_n, head_n + k)))

            turn(0, True, False)
            with sp.Fori(1, turns - 1) as t:
                turn(t, False, False)
            turn(turns - 1, False, True)
            for k in range(HEADS):
                sp.wait_ge(head_stored[k], 16 * turns)

        @block.gpsimd
        def _(pool):
            make_identity(nc, pool, ident, zeroed, ident_ready)
            nc.gpsimd.memset(edge0[:, :], 0.0).then_inc(edges_set, 1)
            nc.gpsimd.memset(edge1[:, :], MASKED).then_inc(edges_set, 1)

        @block.vector
        def _(dve):
            nc.vector.memset(ps_o[:, :], 0.0)
            nc.vector.memset(ks[MAX_ROW:ROWS, :, :], 1.0)
            dve.wait_ge(ident_ready, 1)
            nc.vector.tensor_copy(ident_b[:, :], ident[:, :]).then_inc(ident_ready, 1)
            nc.vector.memset(pev_d[:, :, DH:DV], 0.0)
            dve.wait_ge(c_loaded, 64)
            nc.vector.tensor_tensor(pek_d[:, :, :], pek_in[:, :, :], pek0[:, None, :].to_broadcast([P, 2, DH]),
                                    ALU.subtract).then_inc(setup, 1)
            nc.vector.tensor_tensor(pev_d[:, :, 0:DH], pev_in[:, :, :], pev0[:, None, :].to_broadcast([P, 2, DH]),
                                    ALU.subtract).then_inc(setup, 1)
            dve.wait_ge(pek_turned, 1)
            nc.vector.tensor_copy(pek_parts[:, 0, :], ps_rw[0:DH, 0, :]).then_inc(setup, 1)
            dve.wait_ge(setup, 3)
            nc.vector.tensor_tensor(pek_rest[:, :], ps_rw[0:DH, 0, :], pek_parts[:, 0, :], ALU.subtract).then_inc(pek_turned, 1)
            dve.wait_ge(pek_turned, 2)
            nc.vector.tensor_copy(pek_parts[:, 1, :], pek_rest[:, :]).then_inc(setup, 1)
            dve.wait_ge(setup, 4)
            nc.vector.tensor_tensor(pek_parts[:, 2, :], pek_rest[:, :], pek_parts[:, 1, :], ALU.subtract).then_inc(setup, 1)

            def score_chunk(t, m, c, valid):
                sl, i = m % SLOTS, m % UNITS_HEAD
                far = far_chunks(i)
                bank, count = score_bank(t, m, c)
                if c < len(far):
                    dve.wait_ge(scored[bank], count)
                    nc.vector.tensor_reduce(top[:, m % 2, c:c + 1], ps_s[:, bank, 0:far[c][1]], AX.X, ALU.max)\
                        .then_inc(score_out[bank], 1)
                    return
                keys = min(i + 1, 3) * P
                before = m - SLOTS
                if valid(before):
                    dve.wait_ge(turned, units(t, before))
                    dve.wait_ge(p_stored[sl], 16 * use(t, before))
                if keys < NEAR:
                    nc.vector.memset(p[:, sl, 0:NEAR - keys], 0.0)
                dve.wait_ge(bias_loaded[sl], 16 * use(t, m))
                dve.wait_ge(scored[bank], count)
                nc.vector.memset(spare[:, :], 0.0)
                nc.vector.tensor_tensor_reduce(out=p[:, sl, NEAR - keys:NEAR], in0=ps_s[:, bank, 0:keys],
                                               in1=bias[:, sl, NEAR - keys:NEAR], scale=1.0, scalar=-3e38,
                                               op0=ALU.add, op1=ALU.max, accum_out=top[:, m % 2, c:c + 1])\
                    .then_inc(score_out[bank], 1)
                dve.wait_ge(score_out[bank], count)
                nc.vector.tensor_reduce(negtop[:, sl:sl + 1], top[:, m % 2, 0:c + 1], AX.X, ALU.max, negate=True)\
                    .then_inc(neg_done, 1)

            def split_max(t, g, step, valid):
                neg = negtop[:, 4 * (g % 2):4 * (g % 2) + 4]
                part = lambda n: neg_parts[:, g % 2, :, n]
                if step == 0:
                    dve.wait_ge(neg_done, units(t, 4 * g + 3))
                    if valid(4 * (g - 2)):
                        dve.wait_ge(spread_done, groups(t, g - 2))
                    nc.vector.tensor_copy(part(0), neg).then_inc(neg_split, 1)
                    return
                dve.wait_ge(neg_split, head_turns(t, g) * (4 * GROUPS) + (4 * (g % GROUPS) + step))
                if step == 1:
                    nc.vector.tensor_tensor(neg_rest[:, :], neg, part(0), ALU.subtract).then_inc(neg_split, 1)
                elif step == 2:
                    nc.vector.tensor_copy(part(1), neg_rest[:, :]).then_inc(neg_split, 1)
                else:
                    nc.vector.tensor_tensor(part(2), neg_rest[:, :], part(1), ALU.subtract).then_inc(neg_split, 1)

            def combine(t, g):
                k, gi = head_of(g), g % GPH
                tiles = 3 if gi == 0 else 4
                dve.wait_ge(o_back, groups(t, g))
                view = ps_p[:, :].rearrange("p (i c x) -> p i x c", i=4, x=CT)[:, :, 0:DV, 0:tiles]
                nc.vector.tensor_reduce(osum[:, g % 2, :, :], view, AX.X, ALU.add).then_inc(o_summed, 1)
                dve.wait_ge(o_summed, groups(t, g))
                nc.vector.reciprocal(rden[:, g % 2, :], osum[:, g % 2, :, DH]).then_inc(inverted, 1)
                dve.wait_ge(inverted, groups(t, g))
                if gi == 0:
                    dve.wait_ge(head_stored[k], 16 * head_turns(t, g))
                nc.vector.tensor_tensor(oh[:, k, 4 * gi:4 * gi + 4, :], osum[:, g % 2, :, 0:DH],
                                        rden[:, g % 2, :, None].to_broadcast([P, 4, DH]), ALU.mult).then_inc(o_done[k], 1)

            def steps(t, n, valid):
                mw = n - LAGS["turn_w"]
                if valid(mw) and n % UNITS_HEAD in VECTOR_W:
                    related = n - LAGS["relate"]
                    if valid(related):
                        dve.wait_ge(r_out[related % SLOTS], use(t, related))
                    dve.wait_ge(w_turned[mw % SLOTS], use(t, mw))
                    copy_w(dve, nc.vector.tensor_copy, t, mw, valid)
                g = group_at(n, "copy_o", valid)
                if g is not None and n % UNITS_HEAD in VECTOR_O:
                    copy_o(dve, nc.vector.tensor_copy, t, g)
                m = n - LAGS["turn"]
                chunks = len(far_chunks(n % UNITS_HEAD)) + 1 if n >= 0 and valid(n) else 0
                split, back = group_at(n, "split", valid), group_at(n, "combine", valid)
                for c in range(max(4, chunks)):
                    if c < chunks:
                        score_chunk(t, n, c, valid)
                    if c < 4 and split is not None:
                        split_max(t, split, c, valid)
                    if c == 0 and back is not None:
                        combine(t, back)
                    g = group_at(n, "spread", valid)
                    if c == 0 and g is not None and n % UNITS_HEAD in VECTOR_SPREAD:
                        copy_spread(dve, nc.vector.tensor_copy, t, g)
                if valid(m) and n % UNITS_HEAD in VECTOR_TURNED:
                    copy_turned(dve, nc.vector.tensor_copy, t, m, valid)

            emit(dve, steps)

        @block.scalar
        def _(act):
            def copy(out, in_):
                return nc.scalar.activation(out, in_, ACT.Copy)

            def steps(t, n, valid):
                m, mw = n - LAGS["relate"], n - LAGS["turn_w"]
                if valid(m):
                    act.wait_ge(r_done, units(t, m))
                if valid(mw):
                    act.wait_ge(w_turned[mw % SLOTS], use(t, mw))
                if valid(m):
                    sl = m % SLOTS
                    if valid(m - SLOTS):
                        act.wait_ge(r_stored[sl], 16 * use(t, m - SLOTS))
                    copy(r_sb[:, sl, :], ps_rw[:, 0, :]).then_inc(r_out[sl], 1)
                if valid(mw) and n % UNITS_HEAD not in VECTOR_W:
                    copy_w(act, copy, t, mw, valid)
                g = group_at(n, "copy_o", valid)
                if g is not None and n % UNITS_HEAD not in VECTOR_O:
                    copy_o(act, copy, t, g)
                for part in range(4):
                    g = group_at(n, "far", valid, part)
                    if g is None:
                        continue
                    if part == 0:
                        group_read(act, t, g, valid)
                    for b, q0 in quarter(far_blocks(g % GPH), part):
                        bank, count = far_bank(t, g, b)
                        act.wait_ge(far_done[bank], count)
                        nc.scalar.activation(pt[:, PT_AT[g % GPH] + b, q0:GROUP], ps_f[:, bank, q0:GROUP], ACT.Exp)\
                            .then_inc(far_out[bank], 1)
                g = group_at(n, "spread", valid)
                if g is not None and n % UNITS_HEAD not in VECTOR_SPREAD:
                    copy_spread(act, copy, t, g)
                m = n - LAGS["turn"]
                if valid(m) and n % UNITS_HEAD not in VECTOR_TURNED:
                    copy_turned(act, copy, t, m, valid)
                m = n - LAGS["exp"]
                if valid(m):
                    sl, keys = m % SLOTS, min(m % UNITS_HEAD + 1, 3) * P
                    act.wait_ge(neg_done, units(t, m))
                    row = p[:, sl, NEAR - keys:NEAR]
                    nc.scalar.activation(row, row, ACT.Exp, bias=negtop[:, sl:sl + 1]).then_inc(expd[sl], 1)

            emit(act, steps)

        @block.tensor
        def _(pe):
            pe.wait_ge(ident_ready, 2)
            pe.wait_ge(setup, 2)
            for c in range(2):
                last = nc.tensor.transpose(ps_rw[0:DH, 0, c * P:(c + 1) * P], pek_d[:, c, :], ident[:, :])
            last.then_inc(pek_turned, 1)
            pe.wait_ge(stacked, 16 * len(LEFT))
            pe.wait_ge(pek_turned, 2)

            def relate_and_turn_w(t, m, mw, valid):
                k, i = (m // UNITS_HEAD) % HEADS, m % UNITS_HEAD
                if valid(m) and i == 0:
                    pe.wait_ge(q_loaded[k], (16 * SIDE_DMAS) * (t + m // UNITS) + 16 * SIDE_DMAS)
                if valid(m - 1):
                    pe.wait_ge(r_out[(m - 1) % SLOTS], use(t, m - 1))
                if valid(mw - 1):
                    pe.wait_ge(w_out, units(t, mw - 1))
                if valid(m):
                    nc.tensor.matmul(ps_rw[:, 0, :], qs[0:STACK, k, i * P:(i + 1) * P], pek_s[:, :], start=True, stop=True)\
                        .then_inc(r_done, 1)
                if valid(mw):
                    pe.wait_ge(w_loaded[mw % SLOTS], 16 * use(t, mw))
                    for c in range(2):
                        last = nc.tensor.transpose(ps_rw[:, 1, c * P:(c + 1) * P], w[:, mw % SLOTS, c * P:(c + 1) * P],
                                                   ident[:, :])
                    last.then_inc(w_turned[mw % SLOTS], 1)

            def score_chunk(t, m, c):
                k, i = (m // UNITS_HEAD) % HEADS, m % UNITS_HEAD
                far = far_chunks(i)
                bank, count = score_bank(t, m, c)
                near = min(i + 1, 3) * P
                if i == 0:
                    pe.wait_ge(k_loaded[k], (16 * SIDE_DMAS) * t + 16 * SIDE_DMAS)
                k0, keys = far[c] if c < len(far) else ((i + 1) * P - near, near)
                pe.wait_ge(score_out[bank], count - 1)
                nc.tensor.matmul(ps_s[:, bank, 0:keys], qs[0:STACK, k, i * P:(i + 1) * P], ks[0:STACK, k, k0:k0 + keys],
                                 start=True, stop=True).then_inc(scored[bank], 1)

            def turn_near(t, m, n, valid):
                blocks = min(m % UNITS_HEAD + 1, 3)
                pe.wait_ge(expd[m % SLOTS], use(t, m))
                spread, turned_back = group_at(n, "spread", valid), group_at(n, "turn_o", valid)
                if spread is not None:
                    pe.wait_ge(spread_out, groups(t, spread))
                elif turned_back is not None:
                    pe.wait_ge(o_summed, groups(t, turned_back))
                elif valid(m - 1):
                    pe.wait_ge(turned_out, units(t, m - 1))
                for b in range(blocks):
                    last = nc.tensor.transpose(ps_p[:, b * P:(b + 1) * P], p[:, m % SLOTS, (3 - blocks + b) * P:(4 - blocks + b) * P],
                                               ident[:, :])
                last.then_inc(turned, 1)

            def spread_max(t, g):
                pe.wait_ge(neg_split, head_turns(t, g) * (4 * GROUPS) + (4 * (g % GROUPS) + 4))
                pe.wait_ge(turned_out, units(t, 4 * g + 2 + LAGS["spread"] - LAGS["turn"]))
                for u in range(4):
                    last = nc.tensor.matmul(ps_p[MAX_ROW:ROWS, u * P:(u + 1) * P], neg_parts[:, g % 2, u, :], ident_b[:, :],
                                            start=True, stop=True)
                last.then_inc(spread_done, 1)

            def far_block(t, g, b, q0):
                k, gi = head_of(g), g % GPH
                bank, count = far_bank(t, g, b)
                if b == 0:
                    pe.wait_ge(spread_out, groups(t, g))
                pe.wait_ge(far_out[bank], count - 1)
                nc.tensor.matmul(ps_f[:, bank, q0:GROUP], ks[:, k, b * P:(b + 1) * P], qs[:, k, gi * GROUP + q0:(gi + 1) * GROUP],
                                 start=True, stop=True).then_inc(far_done[bank], 1)

            def weigh_parts(g):
                k, gi = head_of(g), g % GPH
                v_of = lambda b: (vh[:, k, b, :], pt[:, PT_AT[gi] + b, :], max(0, b - 4 * gi) * P, b)
                near = [(pev_d[:, c, :], wt[:, gi, c, :], 0, None) for c in range(2)]
                if gi == 0:
                    return [v_of(0), near[0], near[1], v_of(3), v_of(1), v_of(2)]
                return [v_of(b) for b in range(4 * gi + 4)] + near

            def weigh(t, g, part, n, valid):
                k, gi = head_of(g), g % GPH
                parts = weigh_parts(g)
                tiles = 3 if gi == 0 else 4
                if n == 0:
                    pe.wait_ge(turned_out, units(t, 4 * g + 3))
                    if valid(4 * (g - 1)):
                        pe.wait_ge(o_out, groups(t, g - 1))
                    if gi == 0:
                        pe.wait_ge(v_loaded[k], 16 * head_turns(t, g) + 16)
                left, right, q0, b = parts[n]
                if b is None:
                    pe.wait_ge(w_out, units(t, 4 * g + 3))
                elif b <= 4 * gi:
                    bank, count = far_bank(t, g, b)
                    pe.wait_ge(far_out[bank], count)
                ct = n % tiles
                done = nc.tensor.matmul(ps_o[ct * CT:ct * CT + DV, q0:GROUP], left, right[:, q0:GROUP],
                                        start=n < tiles, stop=n >= len(parts) - tiles, skip_group_check=True)
                if n == len(parts) - 1:
                    done.then_inc(pv_done[k], 1)

            def turn_o(t, g, valid):
                pe.wait_ge(o_out, groups(t, g))
                m = 4 * g + 2 + LAGS["turn_o"] - LAGS["turn"]
                if valid(m):
                    pe.wait_ge(turned_out, units(t, m))
                else:
                    pe.wait_ge(turned_out, units(t, UNITS - 1))
                    pe.wait_ge(o_summed, groups(t, g - 1))
                for q in range(4):
                    last = nc.tensor.transpose(ps_p[:, q * P:(q + 1) * P], ot[:, q * P:(q + 1) * P], ident[:, :])
                last.then_inc(o_back, 1)

            def steps(t, n, valid):
                relate_and_turn_w(t, n - LAGS["relate"], n - LAGS["turn_w"], valid)
                scores, fars, weighs = [], [], []
                if n >= 0 and valid(n):
                    scores = list(range(len(far_chunks(n % UNITS_HEAD)) + 1))
                for part in range(4):
                    g = group_at(n, "far", valid, part)
                    if g is not None:
                        fars = [(g, b, q0) for b, q0 in quarter(far_blocks(g % GPH), part)]
                    g = group_at(n, "weigh", valid, part)
                    if g is not None:
                        places = list(range(len(weigh_parts(g))))
                        if g % GPH:
                            weighs += [(g, part, x) for x in quarter(places, part)]
                        elif part == 3:
                            weighs += [(g, part, x) for x in places]
                m = n - LAGS["turn"]
                first_weighs = [what for what in weighs if what[1] == 0]
                weighs = [what for what in weighs if what[1] > 0]
                steps_here = max(1, len(scores), len(fars), len(weighs))
                for c in range(steps_here):
                    if c < len(scores):
                        score_chunk(t, n, c)
                    if c < len(fars):
                        far_block(t, *fars[c])
                    if c < len(weighs):
                        weigh(t, *weighs[c], valid)
                    if c == (steps_here - 1) // 4:
                        g = group_at(n, "spread", valid)
                        if g is not None:
                            spread_max(t, g)
                        g = group_at(n, "turn_o", valid)
                        if g is not None:
                            turn_o(t, g, valid)
                if valid(m):
                    turn_near(t, m, n, valid)
                for what in first_weighs:
                    weigh(t, *what, valid)

            emit(pe, steps)


def hybrid_layer_kernel(nc, a, out):
    def scratch(name, shape, dt=F32):
        return nc.dram_tensor(name, shape, dt, kind="Internal").ap()

    x0 = a["x"].rearrange("b l c -> (b l) c")
    x1, x2 = (scratch(f"x{n}", (NTOK, D)) for n in (1, 2))
    qk_a = scratch("qk_a", (2, 3, D, B, L + 2 * PAD), BF16)
    v_a = scratch("v_a", (B, L + 2 * PAD, H * (DH + 1)))
    qk_b = scratch("qk_b", (2, 3, D, B, L), BF16)
    v_b = scratch("v_b", (B, H, P, L // P, DH + 1))
    att = scratch("att", (NTOK, D))
    bias_rows = scratch("bias_rows", (SHIFT_SLOTS, P, 4 * P))
    prob_rows = scratch("prob_rows", (SHIFT_SLOTS, P, 3 * P))
    ffn = [a[n] for n in ("sw1", "sb1", "sw3", "sb3", "sw2", "sb2", "w1", "b1", "w2", "b2")]

    project_stage(nc, "pa", x0, a["a_wq_t"], a["a_wk_t"], a["a_wv_t"], qk_a, v_a)
    window_stage(nc, "wa", x0, x1, qk_a, v_a, a["a_wo_t"], a["bo"])
    ffn_stage(nc, "fa", x1, x2, *ffn)
    project_stage(nc, "pb", x2, a["b_wq_t"], a["b_wk_t"], a["b_wv_t"], qk_b, v_b, a["pek"][0:1, :], a["pev"][0:1, :])
    causal_stage(nc, "ca", att, qk_b, v_b, a["pek"], a["pev"], bias_rows, prob_rows)
    ffn_stage(nc, "fb", x2, out.rearrange("b l c -> (b l) c"), *ffn, att=att, wo_t=a["b_wo_t"])


def kernel(**inputs):
    import numpy as _np
    import concourse.bacc as _bacc
    from concourse import mybir as _mybir
    from concourse.bass_utils import run_bass_kernel_spmd as _run

    i = {n.removeprefix("L0_"): _np.asarray(v) for n, v in inputs.items()}
    laid = {"x": i["attn_a_x"], "bo": i["attn_a_bo"], "pek": i["attn_b_pek"], "pev": i["attn_b_pev"]}
    for part in "ab":
        for m in ("Wq", "Wk", "Wv", "Wo"):
            laid[f"{part}_{m.lower()}_t"] = i[f"attn_{part}_{m}"].T
    for n in ("sw1", "sb1", "sw3", "sb3", "sw2", "sb2", "w1", "b1", "w2", "b2"):
        laid[n] = i[f"ffn_{n}"]

    nc = _bacc.Bacc("TRN2", target_bir_lowering=False, num_devices=1)
    arrays, aps = {}, {}
    for n, v in laid.items():
        arrays[f"in_{n}"] = _np.ascontiguousarray(v)
        aps[n] = nc.dram_tensor(f"in_{n}", v.shape, _mybir.dt.from_np(v.dtype), kind="ExternalInput").ap()
    out = nc.dram_tensor("out", (B, L, D), _mybir.dt.float32, kind="ExternalOutput").ap()
    hybrid_layer_kernel(nc, aps, out)
    return _run(nc, [arrays], core_ids=[0]).results[0]["out"]
```
